# Optimizing a Trainium2 kernel written in Bass

```python
import numpy as np
import jax
import jax.numpy as jnp

def _softmax(x, axis=-1):
    return jax.nn.softmax(x, axis=axis)

def _gelu(x):
    return jax.nn.gelu(x, approximate=True)

def _silu(x):
    return jax.nn.silu(x)

def _sigmoid(x):
    return jax.nn.sigmoid(x)

def _layernorm(x, axis=-1, eps=1e-05):
    m = jnp.mean(x, axis=axis, keepdims=True)
    v = jnp.var(x, axis=axis, keepdims=True)
    return (x - m) / jnp.sqrt(v + eps)

def _scatter_add(tgt, idx, src, axis=0):
    return tgt.at[idx].add(src)

def _segment_sum(src, seg, n):
    return jax.ops.segment_sum(src, seg, n)
kernel_name = 'mk_gnn_preln_d2_gnn_r64_b02f9e'

def setup_inputs(seed: int=0):
    np.random.seed(seed)
    _w = jnp.asarray

    def _rec_inputs():
        import jax
        import jax.numpy as jnp
        _gk = jax.random.key(seed)
        x = -0.0008691 + 1 * jax.random.normal(jax.random.fold_in(_gk, 1), (100000, 64), jnp.float32)
        src = jax.random.randint(jax.random.fold_in(_gk, 2), (50000,), 0, 100000, jnp.int32)
        dst = jax.random.randint(jax.random.fold_in(_gk, 3), (50000,), 0, 100000, jnp.int32)
        _o = jnp.argsort(dst, stable=True)
        src = src[_o]
        dst = dst[_o]
        edge_attr_64 = 0.000135552 + 1.00015 * jax.random.normal(jax.random.fold_in(_gk, 12), (50000, 64), jnp.float32)
        return (x, src, dst, edge_attr_64)
    x, src, dst, edge_attr_64 = _rec_inputs()

    def _L0_gnn_setup():
        import jax, jax.numpy as jnp
        import numpy as np
        N_NODES = 20000
        N_EDGES = 5000
        HIDDEN = 64
        HEADS = 4
        D_INNER = 256
        NEG_SLOPE = 0.2
        BN_EPS = 1e-05

        def _batch_norm(x, gamma, beta):
            mu = x.mean(0)
            var = jnp.mean((x - mu) ** 2, axis=0)
            return (x - mu) * jax.lax.rsqrt(var + BN_EPS) * gamma + beta

        def _gatv2(x, edge_index, W_l, b_l, W_r, b_r, att, bias_gat):
            N = x.shape[0]
            H, C = att.shape
            src, dst = (edge_index[0], edge_index[1])
            xl = (x @ W_l + b_l).reshape(N, H, C)
            xr = (x @ W_r + b_r).reshape(N, H, C)
            e = jax.nn.leaky_relu(xl[src] + xr[dst], NEG_SLOPE)
            score = jnp.einsum('ehc,hc->eh', e, att)
            m = jax.ops.segment_max(score, dst, num_segments=N)
            ex = jnp.exp(score - m[dst])
            denom = jax.ops.segment_sum(ex, dst, num_segments=N)
            alpha = ex / jnp.maximum(denom[dst], 1e-16)
            out = jax.ops.segment_sum(alpha[:, :, None] * xl[src], dst, num_segments=N)
            return out.mean(axis=1) + bias_gat
        key = jax.random.key(seed)
        ks = jax.random.split(key, 8)
        s = 1.0 / np.sqrt(HIDDEN)
        return {'x': jax.random.normal(ks[0], (N_NODES, HIDDEN), jnp.float32), 'edge_index': jax.random.randint(ks[1], (2, N_EDGES), 0, N_NODES, jnp.int64), 'W_l': jax.random.normal(ks[2], (HIDDEN, HEADS * HIDDEN), jnp.float32) * s, 'b_l': jnp.zeros((HEADS * HIDDEN,), jnp.float32), 'W_r': jax.random.normal(ks[3], (HIDDEN, HEADS * HIDDEN), jnp.float32) * s, 'b_r': jnp.zeros((HEADS * HIDDEN,), jnp.float32), 'att': jax.random.normal(ks[4], (HEADS, HIDDEN), jnp.float32) * s, 'bias_gat': jnp.zeros((HIDDEN,), jnp.float32), 'gamma1': jnp.ones((HIDDEN,), jnp.float32), 'beta1': jnp.zeros((HIDDEN,), jnp.float32), 'W1': jax.random.normal(ks[5], (HIDDEN, D_INNER), jnp.float32) * s, 'b1': jnp.zeros((D_INNER,), jnp.float32), 'W2': jax.random.normal(ks[6], (D_INNER, HIDDEN), jnp.float32) / np.sqrt(D_INNER), 'b2': jnp.zeros((HIDDEN,), jnp.float32), 'gamma2': jnp.ones((HIDDEN,), jnp.float32), 'beta2': jnp.zeros((HIDDEN,), jnp.float32)}
    _L0_gnn_all = _L0_gnn_setup()
    _L0_gnn_in = {k: v for k, v in _L0_gnn_all.items() if k in ('W_l', 'b_l', 'W_r', 'b_r', 'att', 'bias_gat', 'gamma1', 'beta1', 'W1', 'b1', 'W2', 'b2', 'gamma2', 'beta2')}
    del _L0_gnn_all

    def _L1_gnn_setup():
        import jax, jax.numpy as jnp
        import numpy as np
        N_NODES, N_EDGES, D = (50000, 12500, 64)
        key = jax.random.key(seed)
        ks = jax.random.split(key, 6)
        node_features = jax.random.normal(ks[0], (N_NODES, D), dtype=jnp.float32)
        senders = jax.random.randint(ks[1], (N_EDGES,), 0, N_NODES, dtype=jnp.int32)
        receivers = jax.random.randint(ks[2], (N_EDGES,), 0, N_NODES, dtype=jnp.int32)
        edge_features = jax.random.normal(ks[3], (N_EDGES, D), dtype=jnp.float32)
        s_w = (2.0 / (D + 4 * D)) ** 0.5
        W_kernel = jax.random.normal(ks[4], (D, 4 * D), dtype=jnp.float32) * s_w
        W_bias = jnp.zeros((4 * D,), jnp.float32)
        s_we = (2.0 / (D + D)) ** 0.5
        We_kernel = jax.random.normal(ks[5], (D, D), dtype=jnp.float32) * s_we
        We_bias = jnp.zeros((D,), jnp.float32)
        return dict(node_features=node_features, edge_features=edge_features, W_kernel=W_kernel, W_bias=W_bias, We_kernel=We_kernel, We_bias=We_bias, senders=senders, receivers=receivers)
    _L1_gnn_all = _L1_gnn_setup()
    _L1_gnn_in = {k: v for k, v in _L1_gnn_all.items() if k in ('W_kernel', 'W_bias', 'We_kernel', 'We_bias')}
    del _L1_gnn_all
    return {'x': x, 'src': src, 'dst': dst, 'edge_attr_64': edge_attr_64, 'L0_gnn_W_l': _L0_gnn_in['W_l'], 'L0_gnn_b_l': _L0_gnn_in['b_l'], 'L0_gnn_W_r': _L0_gnn_in['W_r'], 'L0_gnn_b_r': _L0_gnn_in['b_r'], 'L0_gnn_att': _L0_gnn_in['att'], 'L0_gnn_bias_gat': _L0_gnn_in['bias_gat'], 'L0_gnn_gamma1': _L0_gnn_in['gamma1'], 'L0_gnn_beta1': _L0_gnn_in['beta1'], 'L0_gnn_W1': _L0_gnn_in['W1'], 'L0_gnn_b1': _L0_gnn_in['b1'], 'L0_gnn_W2': _L0_gnn_in['W2'], 'L0_gnn_b2': _L0_gnn_in['b2'], 'L0_gnn_gamma2': _L0_gnn_in['gamma2'], 'L0_gnn_beta2': _L0_gnn_in['beta2'], 'L1_gnn_W_kernel': _L1_gnn_in['W_kernel'], 'L1_gnn_W_bias': _L1_gnn_in['W_bias'], 'L1_gnn_We_kernel': _L1_gnn_in['We_kernel'], 'L1_gnn_We_bias': _L1_gnn_in['We_bias']}

def reference(x, src, dst, edge_attr_64, L0_gnn_W_l, L0_gnn_b_l, L0_gnn_W_r, L0_gnn_b_r, L0_gnn_att, L0_gnn_bias_gat, L0_gnn_gamma1, L0_gnn_beta1, L0_gnn_W1, L0_gnn_b1, L0_gnn_W2, L0_gnn_b2, L0_gnn_gamma2, L0_gnn_beta2, L1_gnn_W_kernel, L1_gnn_W_bias, L1_gnn_We_kernel, L1_gnn_We_bias):
    import jax
    import jax.numpy as jnp

    def _L0_gnn_ref(x, edge_index, W_l, b_l, W_r, b_r, att, bias_gat, gamma1, beta1, W1, b1, W2, b2, gamma2, beta2):
        import jax, jax.numpy as jnp
        import numpy as np
        N_NODES = 20000
        N_EDGES = 5000
        HIDDEN = 64
        HEADS = 4
        D_INNER = 256
        NEG_SLOPE = 0.2
        BN_EPS = 1e-05

        def _batch_norm(x, gamma, beta):
            mu = x.mean(0)
            var = jnp.mean((x - mu) ** 2, axis=0)
            return (x - mu) * jax.lax.rsqrt(var + BN_EPS) * gamma + beta

        def _gatv2(x, edge_index, W_l, b_l, W_r, b_r, att, bias_gat):
            N = x.shape[0]
            H, C = att.shape
            src, dst = (edge_index[0], edge_index[1])
            xl = (x @ W_l + b_l).reshape(N, H, C)
            xr = (x @ W_r + b_r).reshape(N, H, C)
            e = jax.nn.leaky_relu(xl[src] + xr[dst], NEG_SLOPE)
            score = jnp.einsum('ehc,hc->eh', e, att)
            m = jax.ops.segment_max(score, dst, num_segments=N)
            ex = jnp.exp(score - m[dst])
            denom = jax.ops.segment_sum(ex, dst, num_segments=N)
            alpha = ex / jnp.maximum(denom[dst], 1e-16)
            out = jax.ops.segment_sum(alpha[:, :, None] * xl[src], dst, num_segments=N)
            return out.mean(axis=1) + bias_gat
        x2 = _gatv2(x, edge_index, W_l, b_l, W_r, b_r, att, bias_gat)
        x = x + x2
        x = _batch_norm(x, gamma1, beta1)
        ff = jax.nn.relu(x @ W1 + b1) @ W2 + b2
        x = x + ff
        x = _batch_norm(x, gamma2, beta2)
        return x

    def _L1_gnn_ref(node_features, edge_features, W_kernel, W_bias, We_kernel, We_bias, senders, receivers):
        import jax, jax.numpy as jnp
        import numpy as np
        N_NODES, N_EDGES, D = (50000, 12500, 64)
        num_nodes = node_features.shape[0]
        proj = node_features @ W_kernel + W_bias
        h, Q, K, V = jnp.split(proj, 4, axis=-1)
        key_edges = K[senders]
        value_edges = V[senders]
        query_edges = Q[receivers]
        edges = query_edges + key_edges + (edge_features @ We_kernel + We_bias)
        eta = jax.nn.sigmoid(edges)
        nodes = h + jax.ops.segment_sum(eta * value_edges, receivers, num_segments=num_nodes)
        return nodes
    edge_index = jnp.stack([src, dst])
    h = jnp.maximum(_layernorm(x, axis=-1), 0.0)
    x = x + _L0_gnn_ref(h, edge_index, L0_gnn_W_l, L0_gnn_b_l, L0_gnn_W_r, L0_gnn_b_r, L0_gnn_att, L0_gnn_bias_gat, L0_gnn_gamma1, L0_gnn_beta1, L0_gnn_W1, L0_gnn_b1, L0_gnn_W2, L0_gnn_b2, L0_gnn_gamma2, L0_gnn_beta2)
    h = jnp.maximum(_layernorm(x, axis=-1), 0.0)
    x = x + _L1_gnn_ref(h, edge_attr_64, L1_gnn_W_kernel, L1_gnn_W_bias, L1_gnn_We_kernel, L1_gnn_We_bias, src, dst)
    return x

_drawn_inputs = setup_inputs


def setup_inputs(seed=0):
    import zlib

    import numpy as np

    out = dict(_drawn_inputs(seed))
    spreads = {'L0_gnn_b_l': (0.0, 0.35),
     'L0_gnn_b_r': (0.0, 2.0),
     'L0_gnn_bias_gat': (0.0, 2.0),
     'L0_gnn_gamma1': (1.0, 0.2),
     'L0_gnn_beta1': (0.0, 0.392),
     'L0_gnn_b1': (0.0, 0.359),
     'L0_gnn_b2': (0.0, 2.0),
     'L0_gnn_gamma2': (1.0, 0.2),
     'L0_gnn_beta2': (0.0, 0.1),
     'L1_gnn_W_bias': (0.0, 0.1),
     'L1_gnn_We_bias': (0.0, 2.0)}
    factors = {'L0_gnn_W_r': 8.0, 'L0_gnn_att': 3.701}
    for name, (base, spread) in spreads.items():
        noise = np.random.default_rng([zlib.crc32(name.encode()), seed]).standard_normal(out[name].shape)
        drawn = base * np.exp(spread * noise) if base else spread * noise
        out[name] = jnp.asarray(drawn.astype(out[name].dtype))
    for name, factor in factors.items():
        out[name] = (out[name] * factor).astype(out[name].dtype)
    return out
```

```python
from contextlib import ExitStack

import numpy as np

import concourse.bass as bass
from concourse import mybir

F32 = mybir.dt.float32
I32 = mybir.dt.int32
ALU = mybir.AluOpType
ACT = mybir.ActivationFunctionType
AXX = mybir.AxisListType.X

P = 128
D = 64
HEADS = 4
ROWS = 8
TILE = P * ROWS
GROUPS = 4
UNIT = P * GROUPS
RING = 4
FAR = float(1 << 22)
EPS = 1e-5
NEG_SLOPE = 0.2
RESET = 1e30


class Turn:

    def __init__(self, base, r=None):
        self.base, self.r = base, r

    def unit(self, lag=0):
        return self.base - lag if self.r is None else self.r * RING + (self.base - lag)

    def slot(self, lag=0, ring=RING):
        return (self.base - lag) % ring

    def lap(self, lag=0):
        n = (self.base - lag) // RING
        return n if self.r is None else self.r + n

    def first(self, lag=0):
        return self.r is None and self.base - lag == 0

    def has(self, lag, count):
        return self.r is not None or 0 <= self.base - lag < count


def pipeline(eng, count, depth, step):
    warm = depth + RING
    laps = (count - warm) // RING
    for i in range(warm):
        step(Turn(i))
    if laps > 0:
        with eng.Fori(0, laps) as r:
            for u in range(RING):
                step(Turn(warm + u, r))
    for i in range(warm + RING * max(laps, 0), count + depth):
        step(Turn(i))


def await_unit(eng, sem, turn, lag, per=1):
    eng.wait_ge(sem, (turn.unit(lag) + 1) * per)


def await_free(eng, sem, turn, lag, ring=RING, per=1):
    if turn.r is None and turn.base - lag < ring:
        return
    eng.wait_ge(sem, (turn.unit(lag) + (1 - ring)) * per)


def await_slot(eng, sems, turn, lag, per=16):
    eng.wait_ge(sems[turn.slot(lag)], (turn.lap(lag) + 1) * per)


def await_slot_free(eng, sems, turn, lag, per=16):
    if turn.r is None and turn.base - lag < RING:
        return
    eng.wait_ge(sems[turn.slot(lag)], turn.lap(lag) * per)


def part_wait(eng, passed):
    eng.sem_inc(passed, 1)


def build(nc, a, out):
    NP = a["x"].shape[0]
    N = a["nodes"]
    NT = NP // TILE
    EP = a["dst_flat"].shape[0]
    EU = EP // UNIT
    EC = EP // P
    PADROWS = NP - N

    def dram(name, shape, dt=F32):
        return nc.dram_tensor(name, shape, dt, kind="Internal").ap()

    h_rows = dram("h_rows", (NP, D))
    z_rows = dram("z_rows", (NP, D))
    xy_rows = dram("xy_rows", (NP, 2 * D))
    hx_rows = dram("hx_rows", (NP, 2 * D))
    reset_d = dram("reset_d", (EP,))
    same_d = dram("same_d", (EP,))
    ends_d = dram("ends_d", (P, EU, GROUPS))
    sidx_d = dram("sidx_d", (P, EU, GROUPS), I32)

    def tiles(t):
        return t.rearrange("(t p j) d -> t p (j d)", p=P, j=ROWS)

    stage_sems = []
    with ExitStack() as top:
        def sb(ctx, name, shape, dt=F32):
            return ctx.enter_context(nc.sbuf_tensor(name, shape, dt))

        def sem(ctx, name):
            handle = nc.alloc_semaphore(name=name)
            if ctx is not top:
                stage_sems.append(handle)
            return handle

        def sems(ctx, name, n=RING):
            return [sem(ctx, f"{name}{i}") for i in range(n)]

        def end_stage():
            nc.clear_and_free_semaphores(stage_sems)
            stage_sems.clear()
            nc.all_engine_barrier()

        ps = [top.enter_context(nc.psum_tensor(f"ps{i}", [P, 512], F32)) for i in range(8)]
        sum_z, sum_zz = ps[6], ps[7]

        ident = sb(top, "ident", [P, P])
        ones = sb(top, "ones", [P, P])
        sel = sb(top, "sel", [P, 2, P])
        pads = sb(top, "pads", [P, 1])
        epsc = sb(top, "epsc", [P, 1])
        consts_loaded = sem(top, "consts_loaded")
        eps_set = sem(top, "eps_set")
        passed_pe = sem(top, "passed_pe")
        passed_pool = sem(top, "passed_pool")
        passed_sp = sem(top, "passed_sp")

        with ExitStack() as c:
            dst_f = sb(c, "dst_f", [P, EC], I32)
            prev_f = sb(c, "prev_f", [P, EC], I32)
            dst_g = sb(c, "dst_g", [P, EC], I32)
            next_g = sb(c, "next_g", [P, EC], I32)
            same = sb(c, "same", [P, EC])
            reset = sb(c, "reset", [P, EC])
            ends = sb(c, "ends", [P, EC])
            shifted = sb(c, "shifted", [P, EC])
            sidx = sb(c, "sidx", [P, EC], I32)
            X = sb(c, "X", [P, RING, ROWS, D])
            xc = sb(c, "xc", [P, RING, ROWS, D])
            sq = sb(c, "sq", [P, RING, ROWS, D])
            hn = sb(c, "hn", [P, RING, ROWS, D])
            hh = sb(c, "hh", [P, RING, ROWS, D])
            s1 = sb(c, "s1", [P, RING, ROWS])
            vs = sb(c, "vs", [P, RING, ROWS])
            lnv = sb(c, "lnv", [P, RING, ROWS])
            rstd = sb(c, "rstd", [P, RING, ROWS])

            lists_loaded = sem(c, "lists_loaded")
            lists_made = sem(c, "lists_made")
            lists_stored = sem(c, "lists_stored")
            x_loaded = sems(c, "x_loaded")
            h_stored = sems(c, "h_stored")
            s1_ready = sem(c, "s1_ready")
            xc_ready = sem(c, "xc_ready")
            sq_ready = sem(c, "sq_ready")
            vs_ready = sem(c, "vs_ready")
            ln_ready = sem(c, "ln_ready")
            rstd_ready = sem(c, "rstd_ready")
            hn_ready = sem(c, "hn_ready")
            hh_ready = sem(c, "hh_ready")
            h_summed = sem(c, "h_summed")
            block = c.enter_context(nc.Block())
            DEPTH = 3

            @block.sync
            def _(eng):
                for dst, src in ((dst_f, a["dst_flat"]), (prev_f, a["prev_flat"])):
                    eng.dma_start(dst[:, :], src.rearrange("(p c) -> p c", p=P)).then_inc(lists_loaded, 16)
                for dst, src in ((dst_g, a["dst_groups"]), (next_g, a["next_groups"])):
                    eng.dma_start(dst[:, :], src).then_inc(lists_loaded, 16)
                for dst, src in ((ident, a["ident"]), (ones, a["ones"]), (sel, a["sel"]), (pads, a["pads"])):
                    eng.dma_start(dst[:], src).then_inc(consts_loaded, 16)

                def step(t):
                    if t.has(0, NT):
                        await_free(eng, xc_ready, t, 0)
                        eng.dma_start(X[:, t.slot()].rearrange("p j d -> p (j d)"),
                                      tiles(a["x"])[t.unit()]).then_inc(x_loaded[t.slot()], 16)
                    if t.has(3, NT):
                        await_unit(eng, hn_ready, t, 3)
                        rows = hn[:, t.slot(3)].rearrange("p j d -> p (j d)")
                        for dst in (h_rows, z_rows):
                            eng.dma_start(tiles(dst)[t.unit(3)], rows).then_inc(h_stored[t.slot(3)], 16)

                pipeline(eng, NT, DEPTH, step)
                eng.wait_ge(lists_made, 4)
                eng.dma_start(reset_d.rearrange("(p c) -> p c", p=P), reset[:, :]).then_inc(lists_stored, 16)
                eng.dma_start(same_d.rearrange("(p c) -> p c", p=P), same[:, :]).then_inc(lists_stored, 16)
                eng.dma_start(ends_d.rearrange("p u g -> p (u g)"), ends[:, :]).then_inc(lists_stored, 16)
                eng.dma_start(sidx_d.rearrange("p u g -> p (u g)"), sidx[:, :]).then_inc(lists_stored, 16)
                eng.wait_ge(lists_stored, 64)
                for s in range(RING):
                    eng.wait_ge(h_stored[s], 32 * len(range(s, NT, RING)))

            @block.scalar
            def _(eng):
                eng.preload_act_table_set("natural_log_exp_and_others")

                def step(t):
                    if t.has(0, NT):
                        await_unit(eng, xc_ready, t, 0)
                        await_free(eng, vs_ready, t, 0)
                        eng.activation(sq[:, t.slot()], xc[:, t.slot()], ACT.Square).then_inc(sq_ready, 1)
                    if t.has(1, NT):
                        await_unit(eng, vs_ready, t, 1)
                        await_free(eng, rstd_ready, t, 1)
                        eng.activation(lnv[:, t.slot(1)], vs[:, t.slot(1)], ACT.Ln,
                                       bias=epsc[:, :], scale=1.0 / D).then_inc(ln_ready, 1)
                        await_unit(eng, ln_ready, t, 1)
                        await_free(eng, hn_ready, t, 1)
                        eng.activation(rstd[:, t.slot(1)], lnv[:, t.slot(1)], ACT.Exp,
                                       scale=-0.5).then_inc(rstd_ready, 1)
                    if t.has(2, NT):
                        await_unit(eng, hn_ready, t, 2)
                        await_free(eng, h_summed, t, 2)
                        eng.activation(hh[:, t.slot(2)], hn[:, t.slot(2)], ACT.Square).then_inc(hh_ready, 1)

                eng.wait_ge(eps_set, 1)
                pipeline(eng, NT, DEPTH, step)

            @block.vector
            def _(eng):
                eng.memset(epsc[:, :], EPS).then_inc(eps_set, 1)
                eng.wait_ge(lists_loaded, 64)
                eng.tensor_tensor(same[:, :], dst_f[:, :], prev_f[:, :], ALU.is_equal).then_inc(lists_made, 1)
                eng.tensor_tensor(ends[:, :], dst_g[:, :], next_g[:, :], ALU.not_equal).then_inc(lists_made, 1)
                eng.tensor_scalar(shifted[:, :], dst_g[:, :], -FAR, None, ALU.add).then_inc(lists_made, 1)
                eng.wait_ge(lists_made, 3)
                eng.tensor_scalar(reset[:, :], same[:, :], -1.0, RESET, ALU.add, ALU.mult)
                eng.tensor_tensor(shifted[:, :], shifted[:, :], ends[:, :], ALU.mult).then_inc(s1_ready, 1)
                eng.wait_ge(s1_ready, 1)
                eng.tensor_scalar(sidx[:, :], shifted[:, :], FAR, None, ALU.add).then_inc(lists_made, 1)

                def step(t):
                    if t.has(0, NT):
                        await_slot(eng, x_loaded, t, 0)
                        eng.tensor_reduce(s1[:, t.slot()], X[:, t.slot()], AXX, ALU.add).then_inc(s1_ready, 1)
                        eng.wait_ge(s1_ready, t.unit() + 2)
                        await_free(eng, hn_ready, t, 0)
                        await_free(eng, sq_ready, t, 0)
                        eng.scalar_tensor_tensor(
                            out=xc[:, t.slot()], in0=s1[:, t.slot()].unsqueeze(2).to_broadcast([P, ROWS, D]),
                            scalar=-1.0 / D, in1=X[:, t.slot()], op0=ALU.mult, op1=ALU.add).then_inc(xc_ready, 1)
                    if t.has(1, NT):
                        await_unit(eng, sq_ready, t, 1)
                        await_free(eng, ln_ready, t, 1)
                        eng.tensor_reduce(vs[:, t.slot(1)], sq[:, t.slot(1)], AXX, ALU.add).then_inc(vs_ready, 1)
                    if t.has(2, NT):
                        await_unit(eng, rstd_ready, t, 2)
                        await_unit(eng, xc_ready, t, 2)
                        await_free(eng, hh_ready, t, 2)
                        await_free(eng, h_summed, t, 2)
                        await_slot_free(eng, h_stored, t, 2, 32)
                        eng.scalar_tensor_tensor(
                            out=hn[:, t.slot(2)], in0=xc[:, t.slot(2)], scalar=0.0,
                            in1=rstd[:, t.slot(2)].unsqueeze(2).to_broadcast([P, ROWS, D]),
                            op0=ALU.max, op1=ALU.mult).then_inc(hn_ready, 1)

                pipeline(eng, NT, DEPTH, step)

            @block.tensor
            def _(eng):
                eng.wait_ge(consts_loaded, 64)

                def step(t):
                    if t.has(3, NT):
                        await_unit(eng, hn_ready, t, 3)
                        await_unit(eng, hh_ready, t, 3)
                        eng.matmul(sum_z[0:1, :], ones[:, 0:1], hn[:, t.slot(3)].rearrange("p j d -> p (j d)"),
                                   start=t.first(3), stop=False, skip_group_check=True)
                        eng.matmul(sum_zz[0:1, :], ones[:, 0:1], hh[:, t.slot(3)].rearrange("p j d -> p (j d)"),
                                   start=t.first(3), stop=False, skip_group_check=True).then_inc(h_summed, 1)

                pipeline(eng, NT, DEPTH, step)

        end_stage()

        with ExitStack() as c:
            wlr = sb(c, "wlr", [P, 2 * P])
            attc = sb(c, "attc", [P, 2, HEADS])
            bpre = sb(c, "bpre", [P, 2, 2])
            bsum = sb(c, "bsum", [P, 2])
            wfin = sb(c, "wfin", [P, 2, D])
            wfq = sb(c, "wfq", [P, 2, D])
            blh = sb(c, "blh", [HEADS, D])
            quarter = sb(c, "quarter", [HEADS, P])
            cb = sb(c, "cb", [P, D])
            gidx = sb(c, "gidx", [P, RING, 2 * GROUPS], I32)
            G = sb(c, "G", [P, RING, 1 + 2 * GROUPS, D])
            rs = sb(c, "rs", [HEADS, RING, UNIT])
            endf = sb(c, "endf", [P, RING, GROUPS])
            sidx = sb(c, "sidx2", [P, RING, GROUPS], I32)
            HT = sb(c, "HT", [P, RING, UNIT])
            HH = sb(c, "HH", [P, RING, UNIT])
            LK = sb(c, "LK", [P, RING, 2, UNIT])
            att_lin = sb(c, "att_lin", [P, 2, HEADS])
            att_relu = sb(c, "att_relu", [P, 2, HEADS])
            wlrT = sb(c, "wlrT", [P, 2, P])
            wlin = sb(c, "wlin", [P, HEADS])
            blin = sb(c, "blin", [P, HEADS])
            ones_rows = sb(c, "ones_rows", [P, UNIT])
            M = sb(c, "M", [HEADS, 1 + RING * UNIT])
            TT = sb(c, "TT", [HEADS, 2, 2, UNIT])
            TA = sb(c, "TA", [HEADS, 2, UNIT])
            RW = sb(c, "RW", [HEADS, 2, 2, UNIT])
            DEN = sb(c, "DEN", [HEADS, RING, UNIT])
            DG = sb(c, "DG", [HEADS, 2, UNIT])
            RC = sb(c, "RC", [HEADS, 2, UNIT])
            B = sb(c, "B", [P, RING, UNIT])
            KEEP = sb(c, "KEEP", [P, 2, 2, UNIT])
            PR = sb(c, "PR", [P, 2, 2, UNIT])
            GM = sb(c, "GM", [P, RING, 2, UNIT])
            AB = sb(c, "AB", [P, RING, GROUPS, D])
            Z = sb(c, "Z", [P, RING, GROUPS, D])
            ZH = sb(c, "ZH", [P, 2, GROUPS, D])
            QD = sb(c, "QD", [P, RING, GROUPS, D])
            pT, pS, pB, pA = ps[0:2], ps[2], ps[3:5], ps[5]

            w_loaded = sem(c, "w_loaded")
            att_zeroed = sem(c, "att_zeroed")
            w_ready = sem(c, "w_ready")
            cb_ready = sem(c, "cb_ready")
            lin_ready = sem(c, "lin_ready")
            lin_out = sem(c, "lin_out")
            gidx_loaded = sems(c, "gidx_loaded")
            reset_loaded = sems(c, "reset_loaded")
            ends_loaded = sems(c, "ends_loaded")
            gathered = sems(c, "gathered")
            scattered = sems(c, "scattered")
            turned = sem(c, "turned")
            turned_taken = sem(c, "turned_taken")
            pre_ready = sem(c, "pre_ready")
            relu_ready = sem(c, "relu_ready")
            score_ready = sem(c, "score_ready")
            m_carried = sem(c, "m_carried")
            m_ready = sem(c, "m_ready")
            ta_ready = sem(c, "ta_ready")
            tt_ready = sem(c, "tt_ready")
            rw_ready = sem(c, "rw_ready")
            den_ready = sem(c, "den_ready")
            dg_ready = sem(c, "dg_ready")
            rc_ready = sem(c, "rc_ready")
            b_ready = sem(c, "b_ready")
            share_spread = sem(c, "share_spread")
            keep_ready = sem(c, "keep_ready")
            pr_ready = sem(c, "pr_ready")
            gm_ready = sem(c, "gm_ready")
            att_out = sem(c, "att_out")
            ab_ready = sem(c, "ab_ready")
            z_ready = sem(c, "z_ready")
            zh_ready = sem(c, "zh_ready")
            qd_ready = sem(c, "qd_ready")
            z_summed = sem(c, "z_summed")
            block = c.enter_context(nc.Block())
            DEPTH = 5
            NW = 2 + HEADS + 2 + 2 + 1

            @block.sync
            def _(eng):
                eng.wait_ge(att_zeroed, 1)
                eng.dma_start(wlr[0:D, :], a["L0_gnn_W_l"]).then_inc(w_loaded, 16)
                eng.dma_start(wlr[D:P, :], a["L0_gnn_W_r"]).then_inc(w_loaded, 16)
                for h in range(HEADS):
                    eng.dma_start(attc[(h % 2) * D:(h % 2) * D + D, h // 2, h:h + 1],
                                  a["L0_gnn_att"].rearrange("h (c o) -> h c o", o=1)[h]).then_inc(w_loaded, 16)
                for i, b in enumerate(("L0_gnn_b_l", "L0_gnn_b_r")):
                    eng.dma_start(bpre[:, i, :], a[b].rearrange("(k p) -> p k", p=P),
                                  allow_slow_non_contiguous=True).then_inc(w_loaded, 16)
                for h in range(2):
                    eng.dma_start(wfin[h * D:h * D + D, :, :],
                                  a["L0_gnn_W_l"].rearrange("f (k h c) -> h f k c", k=2, h=2)[h]
                                  ).then_inc(w_loaded, 16)
                eng.dma_start(blh[:, :], a["L0_gnn_b_l"].rearrange("(h c) -> h c", h=HEADS)).then_inc(w_loaded, 16)

                def step(t):
                    if t.has(0, EU):
                        await_slot_free(eng, gathered, t, 0, 16 * 2 * GROUPS)
                        eng.dma_start(gidx[:, t.slot()], a["gather_rows"][t.unit()]
                                      ).then_inc(gidx_loaded[t.slot()], 16)
                        await_free(eng, ta_ready, t, 0)
                        await_free(eng, m_ready, t, 0)
                        eng.dma_start(rs[:, t.slot()],
                                      reset_d.rearrange("(u o e) -> u o e", o=1, e=UNIT)[t.unit()]
                                      .to_broadcast([HEADS, UNIT])).then_inc(reset_loaded[t.slot()], 16)
                    if t.has(3, EU):
                        await_slot_free(eng, scattered, t, 3, 16 * GROUPS)
                        part_wait(eng, passed_sp)
                        await_free(eng, z_summed, t, 3)
                        part_wait(eng, passed_sp)
                        eng.dma_start(endf[:, t.slot(3)], ends_d[:, t.unit(3)]).then_inc(ends_loaded[t.slot(3)], 16)
                        eng.dma_start(sidx[:, t.slot(3)], sidx_d[:, t.unit(3)]).then_inc(ends_loaded[t.slot(3)], 16)

                pipeline(eng, EU, DEPTH, step)

            @block.gpsimd
            def _(eng):
                last_row = eng.to_reg(N - 1)

                def step(t):
                    if t.has(5, EU):
                        await_unit(eng, z_ready, t, 5)
                        await_slot(eng, ends_loaded, t, 5, 32)
                        part_wait(eng, passed_pool)
                        for g in range(GROUPS):
                            eng.indirect_dma_start(
                                out=z_rows, out_offset=bass.IndirectOffsetOnAxis(
                                    ap=sidx[:, t.slot(5), g:g + 1], axis=0),
                                in_=Z[:, t.slot(5), g, :], in_offset=None, bounds_check=last_row,
                                oob_is_err=False).then_inc(scattered[t.slot(5)], 16)
                    if t.has(0, EU):
                        await_slot(eng, gidx_loaded, t, 0)
                        await_free(eng, turned, t, 0)
                        await_free(eng, zh_ready, t, 0)
                        part_wait(eng, passed_pool)
                        for g in range(GROUPS):
                            for side in range(2):
                                k = side * GROUPS + g
                                eng.indirect_dma_start(
                                    out=G[:, t.slot(), 1 + 2 * g + side, :], out_offset=None, in_=h_rows,
                                    in_offset=bass.IndirectOffsetOnAxis(ap=gidx[:, t.slot(), k:k + 1], axis=0),
                                    bounds_check=NP - 1).then_inc(gathered[t.slot()], 16)

                pipeline(eng, EU, DEPTH, step)
                for s in range(RING):
                    eng.wait_ge(scattered[s], 16 * GROUPS * len(range(s, EU, RING)))

            @block.tensor
            def _(eng):
                eng.wait_ge(w_ready, 10)
                eng.matmul(pA[:, 0:D], quarter[:, :], blh[:, :], start=True, stop=True)
                for k in range(2):
                    mm = eng.transpose(pT[0][:, k * P:k * P + P], wlr[:, k * P:k * P + P], ident[:, :])
                mm.then_inc(cb_ready, 1)
                eng.wait_ge(lin_ready, 1)
                for k in range(2):
                    eng.matmul(pT[1][:, 0:HEADS], wlrT[:, k], att_lin[:, k], start=(k == 0), stop=(k == 1))
                for k in range(2):
                    mm = eng.matmul(pT[1][0:1, HEADS:2 * HEADS], bsum[:, k:k + 1], att_lin[:, k],
                                    start=(k == 0), stop=(k == 1))
                mm.then_inc(lin_out, 1)

                def step(t):
                    if t.has(4, EU):
                        await_unit(eng, gm_ready, t, 4, 2)
                        await_free(eng, ab_ready, t, 4, 1)
                        for g in range(GROUPS):
                            for k in range(2):
                                mm = eng.matmul(pA[:, g * D:g * D + D], GM[:, t.slot(4), k, g * P:g * P + P],
                                                wfq[:, k, :], start=(k == 0), stop=(k == 1))
                        mm.then_inc(att_out, 1)
                    if t.has(3, EU):
                        await_unit(eng, b_ready, t, 3)
                        await_free(eng, pr_ready, t, 3, 1, 2)
                        await_free(eng, keep_ready, t, 3, 1, 2)
                        for k in range(2):
                            eng.matmul(pB[k][:, :], sel[:, k, :], B[:, t.slot(3)],
                                       start=True, stop=True).then_inc(share_spread, 1)
                    if t.has(1, EU):
                        await_slot(eng, gathered, t, 1, 16 * 2 * GROUPS)
                        await_free(eng, relu_ready, t, 1, 1, 2)
                        for g in range(GROUPS):
                            mm = eng.transpose(pT[0][:, g * P:g * P + P],
                                               G[:, t.slot(1), 1 + 2 * g:3 + 2 * g].rearrange("p s d -> p (s d)"),
                                               ident[:, :])
                        for g in range(GROUPS):
                            mm = eng.transpose(pT[1][:, g * P:g * P + P],
                                               G[:, t.slot(1), 2 * g:2 + 2 * g].rearrange("p s d -> p (s d)"),
                                               ident[:, :])
                        mm.then_inc(turned, 1)
                    if t.has(5, EU):
                        await_unit(eng, qd_ready, t, 5)
                        await_slot(eng, ends_loaded, t, 5, 32)
                        for g in range(GROUPS):
                            for acc, rows in ((sum_z, AB), (sum_zz, QD)):
                                mm = eng.matmul(acc[0:1, 0:D], endf[:, t.slot(5), g:g + 1], rows[:, t.slot(5), g],
                                                start=False, stop=False, skip_group_check=True)
                        mm.then_inc(z_summed, 1)
                    if t.has(1, EU):
                        await_unit(eng, turned_taken, t, 1, 3)
                        for k in range(2):
                            eng.matmul(pT[k][:, :], wlr[:, k * P:k * P + P], HT[:, t.slot(1)],
                                       start=True, stop=True).then_inc(pre_ready, 1)
                        await_free(eng, tt_ready, t, 1, 1)
                        eng.matmul(pS[0:HEADS, :], wlin[:, :], HT[:, t.slot(1)], start=True, stop=False)
                        eng.matmul(pS[0:HEADS, :], blin[:, :], ones_rows[:, :], start=False, stop=False)
                        await_unit(eng, relu_ready, t, 1, 2)
                        for k in range(2):
                            mm = eng.matmul(pS[0:HEADS, :], att_relu[:, k, :], LK[:, t.slot(1), k],
                                            start=False, stop=(k == 1))
                        mm.then_inc(score_ready, 1)

                eng.wait_ge(lin_ready, 2)
                pipeline(eng, EU, DEPTH, step)

            @block.scalar
            def _(eng):
                def step(t):
                    if t.has(1, EU):
                        await_unit(eng, turned, t, 1)
                        await_free(eng, score_ready, t, 1)
                        await_free(eng, pr_ready, t, 1, RING, 2)
                        eng.activation(HT[:, t.slot(1)], pT[0][:, :], ACT.Copy).then_inc(turned_taken, 1)
                        eng.activation(HH[0:D, t.slot(1)], pT[0][0:D, :], ACT.Copy).then_inc(turned_taken, 1)
                        eng.activation(HH[D:P, t.slot(1)], pT[1][D:P, :], ACT.Copy).then_inc(turned_taken, 1)
                    if t.has(3, EU):
                        await_free(eng, gm_ready, t, 3, 2, 2)
                        for k in range(2):
                            eng.wait_ge(pr_ready, t.unit(3) * 2 + (k + 1))
                            eng.activation(KEEP[:, t.slot(3, 2), k], pB[k][:, :], ACT.Copy, bias=1.0,
                                           scale=-1.0).then_inc(keep_ready, 1)
                    if t.has(2, EU):
                        await_unit(eng, tt_ready, t, 2)
                        await_free(eng, b_ready, t, 2, 2)
                        eng.activation(RW[:, t.slot(2, 2)], TT[:, t.slot(2, 2)], ACT.Exp).then_inc(rw_ready, 1)
                    if t.has(1, EU):
                        await_unit(eng, pre_ready, t, 1, 2)
                        for k in range(2):
                            eng.activation(LK[:, t.slot(1), k], pT[k][:, :], ACT.Relu, bias=bsum[:, k:k + 1],
                                           scale=1.0).then_inc(relu_ready, 1)

                pipeline(eng, EU, DEPTH, step)

            @block.vector
            def _(eng):
                eng.memset(attc[:, :, :], 0.0).then_inc(att_zeroed, 1)
                eng.memset(quarter[:, :], 1.0 / HEADS).then_inc(w_ready, 1)
                eng.memset(M[:, 0:1], 0.0).then_inc(w_ready, 1)
                eng.memset(G[:, :, 0], 0.0).then_inc(w_ready, 1)
                eng.memset(ones_rows[:, :], 1.0).then_inc(w_ready, 1)
                eng.memset(blin[:, :], 0.0).then_inc(w_ready, 1)
                eng.memset(B[:, :, :], 0.0).then_inc(w_ready, 1)
                eng.wait_ge(w_loaded, 16 * NW)
                eng.tensor_tensor(bsum[:, :], bpre[:, 0], bpre[:, 1], ALU.add).then_inc(w_ready, 1)
                eng.tensor_scalar(wfq[:, :, :], wfin[:, :, :], 1.0 / HEADS, None, ALU.mult).then_inc(w_ready, 1)
                eng.tensor_scalar(att_lin[:, :, :], attc[:, :, :], NEG_SLOPE, None, ALU.mult).then_inc(w_ready, 1)
                eng.tensor_scalar(att_relu[:, :, :], attc[:, :, :], 1.0 - NEG_SLOPE, None, ALU.mult).then_inc(w_ready, 1)
                eng.wait_ge(cb_ready, 1)
                eng.tensor_copy(cb[:, :], pA[:, 0:D])
                eng.tensor_copy(wlrT[:, :, :], pT[0][:, 0:2 * P].rearrange("p (k f) -> p k f", k=2)
                                ).then_inc(lin_ready, 1)
                eng.wait_ge(lin_out, 1)
                eng.wait_ge(w_ready, 10)
                eng.tensor_copy(wlin[:, :], pT[1][:, 0:HEADS])
                eng.tensor_copy(blin[0:1, :], pT[1][0:1, HEADS:2 * HEADS]).then_inc(lin_ready, 1)

                def step(t):
                    if t.has(2, EU):
                        s, s2 = t.slot(2), t.slot(2, 2)
                        lo, hi = 1 + s * UNIT, 1 + (s + 1) * UNIT
                        if s == 0 and not t.first(2):
                            await_unit(eng, m_ready, t, 3)
                            await_unit(eng, tt_ready, t, 3)
                            eng.tensor_copy(M[:, 0:1], M[:, RING * UNIT:RING * UNIT + 1]).then_inc(m_carried, 1)
                            eng.wait_ge(m_carried, t.lap(2))
                        elif not t.first(2):
                            await_unit(eng, m_ready, t, 3)
                        await_unit(eng, score_ready, t, 2)
                        await_slot(eng, reset_loaded, t, 2)
                        eng.tensor_tensor_scan(M[:, lo:hi], rs[:, s], pS[0:HEADS, :], M[:, lo - 1:lo],
                                               ALU.add, ALU.max).then_inc(m_ready, 1)
                        await_unit(eng, m_ready, t, 2)
                        await_free(eng, tt_ready, t, 2, 2)
                        eng.tensor_tensor(TA[:, s2], M[:, lo - 1:hi - 1], rs[:, s], ALU.add).then_inc(ta_ready, 1)
                        await_free(eng, rw_ready, t, 2, 2)
                        eng.tensor_tensor(TT[:, s2, 1], pS[0:HEADS, :], M[:, lo:hi], ALU.subtract)
                        await_unit(eng, ta_ready, t, 2)
                        eng.tensor_tensor(TT[:, s2, 0], TA[:, s2], M[:, lo:hi], ALU.subtract).then_inc(tt_ready, 1)
                    if t.has(3, EU):
                        await_unit(eng, turned_taken, t, 3, 3)
                        await_unit(eng, share_spread, t, 3, 2)
                        await_free(eng, gm_ready, t, 3, 2, 2)
                        for k in range(2):
                            eng.tensor_tensor(PR[:, t.slot(3, 2), k], pB[k][:, :], HH[:, t.slot(3)],
                                              ALU.mult).then_inc(pr_ready, 1)
                    if t.has(4, EU):
                        s = t.slot(4)
                        await_unit(eng, att_out, t, 4)
                        await_free(eng, z_summed, t, 4)
                        eng.tensor_tensor(AB[:, s], pA[:, 0:GROUPS * D].rearrange("p (g d) -> p g d", g=GROUPS),
                                          cb[:, :].unsqueeze(1).to_broadcast([P, GROUPS, D]),
                                          ALU.add).then_inc(ab_ready, 1)
                        await_unit(eng, ab_ready, t, 4)
                        await_slot(eng, gathered, t, 4, 16 * 2 * GROUPS)
                        await_slot_free(eng, scattered, t, 4, 16 * GROUPS)
                        eng.tensor_tensor(Z[:, s], AB[:, s], G[:, s, 2::2, :], ALU.add).then_inc(z_ready, 1)
                        await_unit(eng, z_ready, t, 4)
                        await_free(eng, qd_ready, t, 4, 2)
                        eng.tensor_tensor(ZH[:, t.slot(4, 2)], Z[:, s], G[:, s, 2:2 * GROUPS + 1:2, :],
                                          ALU.add).then_inc(zh_ready, 1)
                        await_unit(eng, zh_ready, t, 4)
                        eng.tensor_tensor(QD[:, s], ZH[:, t.slot(4, 2)], AB[:, s], ALU.mult).then_inc(qd_ready, 1)
                    if t.has(2, EU):
                        s, s2 = t.slot(2), t.slot(2, 2)
                        await_unit(eng, rw_ready, t, 2)
                        if not t.first(2):
                            await_unit(eng, den_ready, t, 3)
                        await_free(eng, dg_ready, t, 2)
                        eng.tensor_tensor_scan(DEN[:, s], RW[:, s2, 0], RW[:, s2, 1],
                                               0.0 if t.first(2) else DEN[:, (s - 1) % RING, UNIT - 1:UNIT],
                                               ALU.mult, ALU.add).then_inc(den_ready, 1)
                        await_unit(eng, den_ready, t, 2)
                        await_free(eng, rc_ready, t, 2, 2)
                        eng.tensor_scalar(DG[:, s2], DEN[:, s], 1e-16, None, ALU.max).then_inc(dg_ready, 1)
                    if t.has(3, EU):
                        await_unit(eng, pr_ready, t, 3, 2)
                        await_unit(eng, keep_ready, t, 3, 2)
                        await_free(eng, att_out, t, 3)
                        if not t.first(3):
                            await_unit(eng, gm_ready, t, 4, 2)
                        for k in range(2):
                            s = t.slot(3)
                            eng.tensor_tensor_scan(
                                GM[:, s, k], KEEP[:, t.slot(3, 2), k], PR[:, t.slot(3, 2), k],
                                0.0 if t.first(3) else GM[:, (s - 1) % RING, k, UNIT - 1:UNIT],
                                ALU.mult, ALU.add).then_inc(gm_ready, 1)
                    if t.has(2, EU):
                        s, s2 = t.slot(2), t.slot(2, 2)
                        await_unit(eng, dg_ready, t, 2)
                        await_free(eng, b_ready, t, 2, 2)
                        eng.reciprocal(RC[:, s2], DG[:, s2]).then_inc(rc_ready, 1)
                        await_unit(eng, rc_ready, t, 2)
                        await_free(eng, share_spread, t, 2, RING, 2)
                        eng.tensor_tensor(B[0:HEADS, s], RC[:, s2], RW[:, s2, 1], ALU.mult).then_inc(b_ready, 1)

                pipeline(eng, EU, DEPTH, step)

        end_stage()

        sc2b = sb(top, "sc2b", [P, D])
        sh2b = sb(top, "sh2b", [P, D])

        def fold(link, eng, s, sums, squares):
            mean, ms, m2, var = s[:, 0], s[:, 1], s[:, 2], s[:, 3]
            link(eng.tensor_reduce(mean, sums[0:1, :].rearrange("o (j d) -> o d j", j=ROWS), AXX, ALU.add))
            link(eng.tensor_reduce(ms, squares[0:1, :].rearrange("o (j d) -> o d j", j=ROWS), AXX, ALU.add))
            link(eng.tensor_scalar(mean, mean, 1.0 / N, None, ALU.mult))
            link(eng.tensor_scalar(ms, ms, 1.0 / N, None, ALU.mult))
            link(eng.tensor_tensor(m2, mean, mean, ALU.mult))
            link(eng.tensor_tensor(var, ms, m2, ALU.subtract))

        def fold_shift(link, eng, s, rstd, gamma, beta, bias, scale, shift):
            mean, mu, off, prod = s[:, 0], s[:, 4], s[:, 5], s[:, 6]
            link(eng.tensor_tensor(scale, rstd, gamma, ALU.mult))
            link(eng.tensor_tensor(mu, mean, bias, ALU.add))
            link(eng.tensor_tensor(off, bias, mu, ALU.subtract))
            link(eng.tensor_tensor(prod, off, scale, ALU.mult))
            link(eng.tensor_tensor(shift, prod, beta, ALU.add))

        with ExitStack() as c:
            vec1 = sb(c, "vec1", [1, 3, D])
            vec2 = sb(c, "vec2", [1, 3, D])
            st = sb(c, "st", [1, 10, D])
            fold1 = sb(c, "fold1", [1, 2, 2, D])
            fold2 = sb(c, "fold2", [1, 2, D])
            off2 = sb(c, "off2", [1, D])
            col1 = sb(c, "col1", [P, 2])
            sc1b = sb(c, "sc1b", [P, D])
            w1 = sb(c, "w1", [P, 2, 2 * P])
            b1c = sb(c, "b1c", [P, 2])
            w2 = sb(c, "w2", [P, 2, D])
            Zt = sb(c, "Zt", [P, RING, ROWS, D])
            XT = sb(c, "XT", [P, RING, 512])
            R = sb(c, "R", [P, 2, 2, 2, 512])
            ZS = sb(c, "ZS", [P, RING, ROWS, D])
            XY = sb(c, "XY", [P, RING, ROWS, 2, D])
            YY = sb(c, "YY", [P, 2, ROWS, D])
            accy = sb(c, "accy", [P, ROWS, D])
            accyy = sb(c, "accyy", [P, ROWS, D])
            pT, pH, pY = ps[0:2], ps[2:6], ps[6:8]

            w_zeroed = sem(c, "w_zeroed3")
            w_loaded = sem(c, "w_loaded3")
            chain = sem(c, "chain")
            var_ready = sem(c, "var_ready")
            rstd_ready = sem(c, "rstd_ready3")
            folded = sem(c, "folded")
            turned_col = sem(c, "turned_col")
            col_ready = sem(c, "col_ready")
            z_loaded = sems(c, "z_loaded")
            x_loaded = sems(c, "x_loaded3")
            y_stored = sems(c, "y_stored")
            turned = sem(c, "turned3")
            xt_ready = sem(c, "xt_ready")
            hid_ready = sem(c, "hid_ready")
            relu_a = sem(c, "relu_a")
            relu_v = sem(c, "relu_v")
            zs_ready = sem(c, "zs_ready")
            y_out = sem(c, "y_out")
            y_ready = sem(c, "y_ready")
            yy_ready = sem(c, "yy_ready")
            acc_zeroed = sem(c, "acc_zeroed")
            accy_ready = sem(c, "accy_ready")
            accyy_ready = sem(c, "accyy_ready")
            sums_ready = sem(c, "sums_ready")
            block = c.enter_context(nc.Block())
            DEPTH = 4
            links = [0]

            @block.sync
            def _(eng):
                for i, n in enumerate(("gamma1", "beta1", "bias_gat")):
                    eng.dma_start(vec1[:, i, :], a["L0_gnn_" + n].rearrange("(o d) -> o d", o=1)).then_inc(w_loaded, 16)
                for i, n in enumerate(("gamma2", "beta2", "b2")):
                    eng.dma_start(vec2[:, i, :], a["L0_gnn_" + n].rearrange("(o d) -> o d", o=1)).then_inc(w_loaded, 16)
                eng.wait_ge(w_zeroed, 1)
                for q in range(2):
                    eng.dma_start(w1[q * D:q * D + D, q, :], a["L0_gnn_W1"]).then_inc(w_loaded, 16)
                eng.dma_start(b1c[:, :], a["L0_gnn_b1"].rearrange("(k p) -> p k", p=P),
                              allow_slow_non_contiguous=True).then_inc(w_loaded, 16)
                eng.dma_start(w2[:, :, :], a["L0_gnn_W2"].rearrange("(k p) d -> p k d", p=P)).then_inc(w_loaded, 16)

                def step(t):
                    if t.has(0, NT):
                        await_free(eng, turned, t, 0)
                        await_free(eng, zs_ready, t, 0)
                        eng.dma_start(Zt[:, t.slot()].rearrange("p j d -> p (j d)"),
                                      tiles(z_rows)[t.unit()]).then_inc(z_loaded[t.slot()], 16)
                        await_slot_free(eng, y_stored, t, 0)
                        eng.dma_start(XY[:, t.slot(), :, 0, :],
                                      a["x"].rearrange("(t p j) d -> t p j d", p=P, j=ROWS)[t.unit()]
                                      ).then_inc(x_loaded[t.slot()], 16)
                    if t.has(3, NT):
                        await_unit(eng, y_ready, t, 3)
                        await_slot(eng, x_loaded, t, 3)
                        eng.dma_start(tiles(xy_rows)[t.unit(3)], XY[:, t.slot(3)].rearrange("p j s d -> p (j s d)")
                                      ).then_inc(y_stored[t.slot(3)], 16)

                pipeline(eng, NT, DEPTH, step)
                for s in range(RING):
                    eng.wait_ge(y_stored[s], 16 * len(range(s, NT, RING)))

            @block.scalar
            def _(eng):
                def rstd_of(n, k):
                    eng.wait_ge(var_ready, n)
                    eng.activation(st[:, 7], st[:, 3], ACT.Ln, bias=epsc[0:1, :]).then_inc(rstd_ready, 1)
                    eng.wait_ge(rstd_ready, k)
                    eng.activation(st[:, 8], st[:, 7], ACT.Exp, scale=-0.5).then_inc(rstd_ready, 1)

                rstd_of(1, 1)
                eng.wait_ge(col_ready, 1)

                def step(t):
                    if t.has(0, NT):
                        await_unit(eng, turned, t, 0)
                        await_free(eng, hid_ready, t, 0, RING, 4)
                        eng.activation(XT[:, t.slot()], pT[t.slot(0, 2)][:, :], ACT.Identity, bias=col1[:, 1:2],
                                       scale=col1[:, 0:1]).then_inc(xt_ready, 1)
                    if t.has(3, NT):
                        await_unit(eng, y_ready, t, 3)
                        await_free(eng, accyy_ready, t, 3, 2)
                        eng.activation(YY[:, t.slot(3, 2)], XY[:, t.slot(3), :, 1, :],
                                       ACT.Square).then_inc(yy_ready, 1)
                    if t.has(1, NT):
                        await_free(eng, y_out, t, 1, 2)
                        for k in range(2):
                            eng.wait_ge(hid_ready, t.unit(1) * 4 + (k + 1))
                            eng.activation(R[:, t.slot(1, 2), 0, k], pH[k][:, :], ACT.Relu,
                                           bias=b1c[:, k:k + 1]).then_inc(relu_a, 1)

                pipeline(eng, NT, DEPTH, step)
                rstd_of(2, 3)

            @block.vector
            def _(eng):
                def link(ins):
                    links[0] += 1
                    ins.then_inc(chain, 1)
                    eng.wait_ge(chain, links[0])

                eng.memset(w1[:, :, :], 0.0).then_inc(w_zeroed, 1)
                eng.memset(accy[:, :, :], 0.0).then_inc(acc_zeroed, 1)
                eng.memset(accyy[:, :, :], 0.0).then_inc(acc_zeroed, 1)
                eng.wait_ge(w_loaded, 16 * 10)
                fold(link, eng, st, sum_z, sum_zz)
                eng.sem_inc(var_ready, 1)
                eng.wait_ge(rstd_ready, 2)
                fold_shift(link, eng, st, st[:, 8], vec1[:, 0], vec1[:, 1], vec1[:, 2], fold1[:, 0, 0], fold1[:, 1, 0])
                link(eng.tensor_copy(fold1[:, :, 1], fold1[:, :, 0]))
                link(eng.tensor_tensor(off2[:, :], vec2[:, 2], fold1[:, 1, 0], ALU.add))
                eng.sem_inc(folded, 1)
                eng.wait_ge(turned_col, 1)
                eng.tensor_copy(col1[:, :], pH[0][:, 0:2])
                eng.tensor_copy(sc1b[:, :], pH[1][:, 0:D]).then_inc(col_ready, 1)

                def step(t):
                    if t.has(2, NT):
                        await_unit(eng, y_out, t, 2)
                        await_unit(eng, zs_ready, t, 2)
                        await_free(eng, yy_ready, t, 2)
                        await_free(eng, accy_ready, t, 2)
                        await_slot_free(eng, y_stored, t, 2)
                        eng.tensor_tensor(XY[:, t.slot(2), :, 1, :], ZS[:, t.slot(2)],
                                          pY[t.slot(2, 2)][:, :].rearrange("p (j d) -> p j d", j=ROWS),
                                          ALU.add).then_inc(y_ready, 1)
                    if t.has(1, NT):
                        await_free(eng, y_out, t, 1, 2)
                        for k in range(2):
                            eng.wait_ge(hid_ready, t.unit(1) * 4 + (3 + k))
                            eng.tensor_scalar(R[:, t.slot(1, 2), 1, k], pH[2 + k][:, :], b1c[:, k:k + 1], 0.0,
                                              ALU.add, ALU.max).then_inc(relu_v, 1)

                pipeline(eng, NT, DEPTH, step)
                eng.wait_ge(sums_ready, 1)
                fold(link, eng, st, pT[0], pT[1])
                eng.sem_inc(var_ready, 1)
                eng.wait_ge(rstd_ready, 4)
                fold_shift(link, eng, st, st[:, 8], vec2[:, 0], vec2[:, 1], off2[:, :], fold2[:, 0], fold2[:, 1])
                eng.sem_inc(folded, 1)
                eng.wait_ge(turned_col, 2)
                eng.tensor_copy(sc2b[:, :], pH[0][:, 0:D])
                eng.tensor_copy(sh2b[:, :], pH[0][:, D:2 * D])

            @block.gpsimd
            def _(eng):
                eng.wait_ge(col_ready, 1)

                def step(t):
                    if t.has(0, NT):
                        await_slot(eng, z_loaded, t, 0)
                        await_free(eng, y_ready, t, 0)
                        eng.tensor_tensor(ZS[:, t.slot()], Zt[:, t.slot()],
                                          sc1b[:, :].unsqueeze(1).to_broadcast([P, ROWS, D]),
                                          ALU.mult).then_inc(zs_ready, 1)
                    if t.has(4, NT):
                        await_unit(eng, y_ready, t, 4)
                        if t.first(4):
                            eng.wait_ge(acc_zeroed, 2)
                        else:
                            await_unit(eng, accy_ready, t, 5)
                        eng.tensor_tensor(accy[:, :, :], accy[:, :, :], XY[:, t.slot(4), :, 1, :],
                                          ALU.add).then_inc(accy_ready, 1)
                        await_unit(eng, yy_ready, t, 4)
                        if not t.first(4):
                            await_unit(eng, accyy_ready, t, 5)
                        eng.tensor_tensor(accyy[:, :, :], accyy[:, :, :], YY[:, t.slot(4, 2)],
                                          ALU.add).then_inc(accyy_ready, 1)

                pipeline(eng, NT, DEPTH, step)

            @block.tensor
            def _(eng):
                eng.wait_ge(folded, 1)
                for k in range(2):
                    eng.matmul(pH[0][:, k:k + 1], fold1[:, k].rearrange("o t d -> o (t d)"), ones[0:1, 0:1],
                               start=True, stop=True)
                eng.matmul(pH[1][:, 0:D], ones[0:1, :], fold1[:, 0, 0], start=True, stop=True
                           ).then_inc(turned_col, 1)
                eng.wait_ge(col_ready, 1)

                def step(t):
                    if t.has(0, NT):
                        await_slot(eng, z_loaded, t, 0)
                        await_free(eng, xt_ready, t, 0, 2)
                        for g in range(4):
                            mm = eng.transpose(pT[t.slot(0, 2)][:, g * P:g * P + P],
                                               Zt[:, t.slot(), 2 * g:2 * g + 2].rearrange("p j d -> p (j d)"),
                                               ident[:, :])
                        mm.then_inc(turned, 1)
                    if t.has(2, NT):
                        await_unit(eng, relu_a, t, 2, 2)
                        await_unit(eng, relu_v, t, 2, 2)
                        await_free(eng, y_ready, t, 2, 2)
                        o = pY[t.slot(2, 2)]
                        for g in range(4):
                            for q in range(2):
                                for k in range(2):
                                    mm = eng.matmul(o[:, (2 * g + q) * D:(2 * g + q + 1) * D],
                                                    R[:, t.slot(2, 2), q, k, g * P:g * P + P], w2[:, k, :],
                                                    start=(k == 0), stop=(k == 1))
                        mm.then_inc(y_out, 1)
                    if t.has(1, NT):
                        await_unit(eng, xt_ready, t, 1)
                        for q in range(2):
                            if q == 0:
                                await_free(eng, relu_a, t, 1, 1, 2)
                            else:
                                await_free(eng, relu_v, t, 1, 1, 2)
                            for k in range(2):
                                eng.matmul(pH[2 * q + k][:, :], w1[:, q, k * P:k * P + P],
                                           XT[:, t.slot(1)], start=True, stop=True).then_inc(hid_ready, 1)

                pipeline(eng, NT, DEPTH, step)
                eng.wait_ge(accy_ready, NT)
                eng.wait_ge(accyy_ready, NT)
                last = NT - 1
                eng.matmul(pT[0][0:1, :], ones[:, 0:1], accy[:, :, :].rearrange("p j d -> p (j d)"),
                           start=True, stop=False)
                eng.matmul(pT[0][0:1, :].rearrange("o (j d) -> o j d", j=ROWS), pads[:, :],
                           XY[:, last % RING, :, 1, :], start=False, stop=True)
                eng.matmul(pT[1][0:1, :], ones[:, 0:1], accyy[:, :, :].rearrange("p j d -> p (j d)"),
                           start=True, stop=False)
                eng.matmul(pT[1][0:1, :], pads[:, :], YY[:, last % 2].rearrange("p j d -> p (j d)"),
                           start=False, stop=True).then_inc(sums_ready, 1)
                eng.wait_ge(folded, 2)
                eng.matmul(pH[0][:, 0:2 * D], ones[0:1, :], fold2[:, :, :].rearrange("o k d -> o (k d)"),
                           start=True, stop=True).then_inc(turned_col, 1)


        end_stage()

        with ExitStack() as c:
            wh = sb(c, "wh", [D, D])
            bh = sb(c, "bh", [1, ROWS, D])
            XY = sb(c, "XY4", [P, RING, ROWS, 2, D])
            v1 = sb(c, "v1", [P, ROWS, D])
            v2 = sb(c, "v2", [P, ROWS, D])
            xf = sb(c, "xf", [P, RING, ROWS, D])
            xc = sb(c, "xc4", [P, RING, ROWS, D])
            sq = sb(c, "sq4", [P, RING, ROWS, D])
            HX = sb(c, "HX", [P, RING, ROWS, 2 * D])
            HT = sb(c, "HT4", [D, RING, 2, 512])
            s1 = sb(c, "s14", [P, RING, ROWS])
            vs = sb(c, "vs4", [P, RING, ROWS])
            lnv = sb(c, "lnv4", [P, RING, ROWS])
            rstd = sb(c, "rstd4", [P, RING, ROWS])
            pT, pO = ps[0:2], ps[2:4]

            w_loaded = sem(c, "w_loaded4")
            xy_loaded = sems(c, "xy_loaded")
            rows_stored = sems(c, "rows_stored")
            v1_ready = sem(c, "v1_ready")
            v2_ready = sem(c, "v2_ready")
            xf_ready = sem(c, "xf_ready")
            s1_ready = sem(c, "s1_ready4")
            xc_ready = sem(c, "xc_ready4")
            sq_ready = sem(c, "sq_ready4")
            vs_ready = sem(c, "vs_ready4")
            ln_ready = sem(c, "ln_ready4")
            rstd_ready = sem(c, "rstd_ready4")
            h_ready = sem(c, "h_ready4")
            turned = sem(c, "turned4")
            ht_ready = sem(c, "ht_ready4")
            proj_ready = sem(c, "proj_ready")
            od_ready = sem(c, "od_ready")
            block = c.enter_context(nc.Block())
            DEPTH = 5

            @block.sync
            def _(eng):
                eng.dma_start(wh[:, :], a["L1_gnn_W_kernel"][:, 0:D]).then_inc(w_loaded, 16)
                for j in range(ROWS):
                    eng.dma_start(bh[:, j, :], a["L1_gnn_W_bias"].rearrange("(o d) -> o d", o=1)[:, 0:D]
                                  ).then_inc(w_loaded, 16)

                def step(t):
                    if t.has(0, NT):
                        await_free(eng, v2_ready, t, 0)
                        eng.dma_start(XY[:, t.slot()].rearrange("p j s d -> p (j s d)"),
                                      tiles(xy_rows)[t.unit()]).then_inc(xy_loaded[t.slot()], 16)
                    if t.has(5, NT):
                        await_unit(eng, od_ready, t, 5)
                        eng.dma_start(tiles(hx_rows)[t.unit(5)], HX[:, t.slot(5)].rearrange("p j d -> p (j d)")
                                      ).then_inc(rows_stored[t.slot(5)], 16)
                        eng.dma_start(out.rearrange("(t p j) d -> t p j d", p=P, j=ROWS)[t.unit(5)],
                                      HX[:, t.slot(5), :, D:2 * D]).then_inc(rows_stored[t.slot(5)], 16)

                pipeline(eng, NT, DEPTH, step)
                for s in range(RING):
                    eng.wait_ge(rows_stored[s], 32 * len(range(s, NT, RING)))

            @block.scalar
            def _(eng):
                def step(t):
                    if t.has(3, NT):
                        await_unit(eng, turned, t, 3)
                        await_free(eng, proj_ready, t, 3)
                        for k in range(2):
                            eng.activation(HT[:, t.slot(3), k], pT[k][0:D, :], ACT.Copy).then_inc(ht_ready, 1)
                    if t.has(0, NT):
                        await_unit(eng, xc_ready, t, 0)
                        await_free(eng, vs_ready, t, 0)
                        eng.activation(sq[:, t.slot()], xc[:, t.slot()], ACT.Square).then_inc(sq_ready, 1)
                    if t.has(1, NT):
                        await_unit(eng, vs_ready, t, 1)
                        await_free(eng, rstd_ready, t, 1)
                        eng.activation(lnv[:, t.slot(1)], vs[:, t.slot(1)], ACT.Ln,
                                       bias=epsc[:, :], scale=1.0 / D).then_inc(ln_ready, 1)
                        await_unit(eng, ln_ready, t, 1)
                        await_free(eng, h_ready, t, 1)
                        eng.activation(rstd[:, t.slot(1)], lnv[:, t.slot(1)], ACT.Exp,
                                       scale=-0.5).then_inc(rstd_ready, 1)

                pipeline(eng, NT, DEPTH, step)

            @block.vector
            def _(eng):
                def step(t):
                    if t.has(4, NT):
                        await_unit(eng, proj_ready, t, 4)
                        await_unit(eng, xf_ready, t, 4)
                        eng.tensor_tensor(HX[:, t.slot(4), :, D:2 * D], xf[:, t.slot(4)],
                                          pO[t.slot(4, 2)][:, :].rearrange("p (j d) -> p j d", j=ROWS),
                                          ALU.add).then_inc(od_ready, 1)
                    if t.has(0, NT):
                        await_slot(eng, xy_loaded, t, 0)
                        if not t.first():
                            eng.wait_ge(v2_ready, t.unit())
                        eng.tensor_tensor(v1[:, :, :], XY[:, t.slot(), :, 1, :],
                                          sc2b[:, :].unsqueeze(1).to_broadcast([P, ROWS, D]),
                                          ALU.mult).then_inc(v1_ready, 1)
                        await_unit(eng, v1_ready, t, 0)
                        if not t.first():
                            eng.wait_ge(xf_ready, t.unit())
                        eng.tensor_tensor(v2[:, :, :], v1[:, :, :], XY[:, t.slot(), :, 0, :], ALU.add).then_inc(v2_ready, 1)
                        await_unit(eng, v2_ready, t, 0)
                        await_free(eng, od_ready, t, 0)
                        eng.tensor_tensor(xf[:, t.slot()], v2[:, :, :],
                                          sh2b[:, :].unsqueeze(1).to_broadcast([P, ROWS, D]),
                                          ALU.add).then_inc(xf_ready, 1)
                    if t.has(1, NT):
                        await_unit(eng, sq_ready, t, 1)
                        await_free(eng, ln_ready, t, 1)
                        eng.tensor_reduce(vs[:, t.slot(1)], sq[:, t.slot(1)], AXX, ALU.add).then_inc(vs_ready, 1)
                    if t.has(0, NT):
                        await_unit(eng, xf_ready, t, 0)
                        await_free(eng, xc_ready, t, 0)
                        eng.tensor_reduce(s1[:, t.slot()], xf[:, t.slot()], AXX, ALU.add).then_inc(s1_ready, 1)
                    if t.has(2, NT):
                        await_unit(eng, rstd_ready, t, 2)
                        await_unit(eng, xc_ready, t, 2)
                        await_free(eng, turned, t, 2)
                        await_slot_free(eng, rows_stored, t, 2, 32)
                        eng.scalar_tensor_tensor(
                            out=HX[:, t.slot(2), :, 0:D], in0=xc[:, t.slot(2)], scalar=0.0,
                            in1=rstd[:, t.slot(2)].unsqueeze(2).to_broadcast([P, ROWS, D]),
                            op0=ALU.max, op1=ALU.mult).then_inc(h_ready, 1)
                    if t.has(0, NT):
                        await_unit(eng, s1_ready, t, 0)
                        await_free(eng, h_ready, t, 0)
                        await_free(eng, sq_ready, t, 0)
                        eng.scalar_tensor_tensor(
                            out=xc[:, t.slot()], in0=s1[:, t.slot()].unsqueeze(2).to_broadcast([P, ROWS, D]),
                            scalar=-1.0 / D, in1=xf[:, t.slot()], op0=ALU.mult, op1=ALU.add).then_inc(xc_ready, 1)

                pipeline(eng, NT, DEPTH, step)

            @block.tensor
            def _(eng):
                eng.wait_ge(w_loaded, 16 * (1 + ROWS))

                def step(t):
                    if t.has(4, NT):
                        await_unit(eng, ht_ready, t, 4, 2)
                        await_free(eng, od_ready, t, 4, 2)
                        o = pO[t.slot(4, 2)]
                        eng.matmul(o[:, :], ones[0:1, :], bh[:, :, :].rearrange("o j d -> o (j d)"),
                                   start=True, stop=False, skip_group_check=True)
                        for j in range(ROWS):
                            mm = eng.matmul(o[:, j * D:j * D + D],
                                            HT[:, t.slot(4), j // 4, (j % 4) * P:(j % 4 + 1) * P],
                                            wh[:, :], start=False, stop=True, skip_group_check=True)
                        mm.then_inc(proj_ready, 1)
                    if t.has(3, NT):
                        await_unit(eng, h_ready, t, 3)
                        await_free(eng, ht_ready, t, 3, 1, 2)
                        part_wait(eng, passed_pe)
                        for j in range(ROWS):
                            mm = eng.transpose(pT[j // 4][0:D, (j % 4) * P:(j % 4 + 1) * P],
                                               HX[:, t.slot(3), j, 0:D], ident[:, :])
                        mm.then_inc(turned, 1)

                pipeline(eng, NT, DEPTH, step)

        end_stage()

        with ExitStack() as c:
            wkq = sb(c, "wkq", [D, 2, D])
            wv = sb(c, "wv", [D, D])
            we = sb(c, "we", [D, D])
            bq = sb(c, "bq", [D, 4])
            bt = sb(c, "bt", [D, 2])
            gidx = sb(c, "gidx5", [P, RING, 2 * GROUPS], I32)
            sidx = sb(c, "sidx5", [P, RING, GROUPS], I32)
            sm = sb(c, "sm", [D, RING, UNIT])
            ea = sb(c, "ea", [D, RING, UNIT])
            G = sb(c, "G5", [P, RING, GROUPS, 2, 2 * D])
            HT = sb(c, "HT5", [D, RING, 2, UNIT])
            GT = sb(c, "GT", [D, 2, UNIT])
            MS = sb(c, "MS", [D, 2, UNIT])
            AG = sb(c, "AG", [D, RING, UNIT])
            O = sb(c, "O", [P, RING, GROUPS, D])
            pT, pE, pV, pO = ps[0:2], ps[2:4], ps[4:6], ps[6:8]

            w_loaded = sem(c, "w_loaded5")
            bt_ready = sem(c, "bt_ready")
            gidx_loaded = sems(c, "gidx_loaded5")
            side_loaded = sems(c, "side_loaded")
            sidx_loaded = sems(c, "sidx_loaded5")
            gathered = sems(c, "gathered5")
            scattered = sems(c, "scattered5")
            turned = sem(c, "turned5")
            ht_ready = sem(c, "ht_ready5")
            edge_ready = sem(c, "edge_ready")
            gate_ready = sem(c, "gate_ready")
            ms_ready = sem(c, "ms_ready")
            ag_ready = sem(c, "ag_ready")
            agg_turned = sem(c, "agg_turned")
            o_ready = sem(c, "o_ready")
            block = c.enter_context(nc.Block())
            DEPTH = 5

            @block.sync
            def _(eng):
                W = a["L1_gnn_W_kernel"]
                for dst, src in ((wkq[:, 0], W[:, 2 * D:3 * D]), (wkq[:, 1], W[:, D:2 * D]),
                                 (wv[:, :], W[:, 3 * D:4 * D]), (we[:, :], a["L1_gnn_We_kernel"])):
                    eng.dma_start(dst, src).then_inc(w_loaded, 16)
                wb = a["L1_gnn_W_bias"].rearrange("(k d o) -> k d o", k=4, o=1)
                for i, src in enumerate((wb[1], wb[2], a["L1_gnn_We_bias"].rearrange("(d o) -> d o", o=1), wb[3])):
                    eng.dma_start(bq[:, i:i + 1], src).then_inc(w_loaded, 16)

                def step(t):
                    if t.has(0, EU):
                        await_slot_free(eng, gathered, t, 0, 16 * 2 * GROUPS)
                        eng.dma_start(gidx[:, t.slot()], a["gather_rows"][t.unit()]
                                      ).then_inc(gidx_loaded[t.slot()], 16)
                        await_free(eng, ag_ready, t, 0)
                        await_free(eng, edge_ready, t, 0)
                        eng.dma_start(sm[:, t.slot()],
                                      same_d.rearrange("(u o e) -> u o e", o=1, e=UNIT)[t.unit()]
                                      .to_broadcast([D, UNIT])).then_inc(side_loaded[t.slot()], 16)
                        eng.dma_start(ea[:, t.slot()], a["edge_feats"].rearrange("f (u e) -> u f e", e=UNIT)[t.unit()]
                                      ).then_inc(side_loaded[t.slot()], 16)
                    if t.has(3, EU):
                        await_slot_free(eng, scattered, t, 3, 16 * GROUPS)
                        eng.dma_start(sidx[:, t.slot(3)], sidx_d[:, t.unit(3)]).then_inc(sidx_loaded[t.slot(3)], 16)

                pipeline(eng, EU, DEPTH, step)

            @block.gpsimd
            def _(eng):
                last_row = eng.to_reg(N - 1)

                def step(t):
                    if t.has(5, EU):
                        await_unit(eng, o_ready, t, 5)
                        await_slot(eng, sidx_loaded, t, 5)
                        part_wait(eng, passed_pool)
                        for g in range(GROUPS):
                            eng.indirect_dma_start(
                                out=out, out_offset=bass.IndirectOffsetOnAxis(
                                    ap=sidx[:, t.slot(5), g:g + 1], axis=0),
                                in_=O[:, t.slot(5), g, :], in_offset=None, bounds_check=last_row,
                                oob_is_err=False).then_inc(scattered[t.slot(5)], 16)
                    if t.has(0, EU):
                        await_slot(eng, gidx_loaded, t, 0)
                        await_free(eng, turned, t, 0)
                        await_free(eng, o_ready, t, 0)
                        part_wait(eng, passed_pool)
                        for g in range(GROUPS):
                            for side in range(2):
                                k = side * GROUPS + g
                                eng.indirect_dma_start(
                                    out=G[:, t.slot(), g, side, :], out_offset=None, in_=hx_rows,
                                    in_offset=bass.IndirectOffsetOnAxis(ap=gidx[:, t.slot(), k:k + 1], axis=0),
                                    bounds_check=NP - 1).then_inc(gathered[t.slot()], 16)

                pipeline(eng, EU, DEPTH, step)
                for s in range(RING):
                    eng.wait_ge(scattered[s], 16 * GROUPS * len(range(s, EU, RING)))

            @block.tensor
            def _(eng):
                eng.wait_ge(w_loaded, 16 * 8)

                def step(t):
                    if t.has(3, EU):
                        await_unit(eng, ag_ready, t, 3)
                        await_free(eng, o_ready, t, 3, 2)
                        part_wait(eng, passed_pe)
                        for g in range(GROUPS):
                            mm = eng.transpose(pO[t.slot(3, 2)][:, g * D:g * D + D],
                                               AG[:, t.slot(3), g * P:g * P + P], ident[0:D, 0:D])
                        mm.then_inc(agg_turned, 1)
                    if t.has(1, EU):
                        await_slot(eng, gathered, t, 1, 16 * 2 * GROUPS)
                        await_free(eng, ht_ready, t, 1, 1, 2)
                        part_wait(eng, passed_pe)
                        for side in range(2):
                            for g in range(GROUPS):
                                mm = eng.transpose(pT[side][0:D, g * P:g * P + P],
                                                   G[:, t.slot(1), g, side, 0:D], ident[:, :])
                        mm.then_inc(turned, 1)
                        await_slot(eng, side_loaded, t, 1, 32)
                        await_free(eng, ms_ready, t, 1, 2)
                        await_free(eng, gate_ready, t, 1, 2)
                        part_wait(eng, passed_pe)
                        eng.matmul(pE[t.slot(1, 2)][0:D, :], we[:, :], ea[:, t.slot(1)], start=True, stop=False)
                        await_unit(eng, ht_ready, t, 1, 2)
                        part_wait(eng, passed_pe)
                        for side in range(2):
                            eng.matmul(pE[t.slot(1, 2)][0:D, :], wkq[:, side], HT[:, t.slot(1), side],
                                       start=False, stop=(side == 1))
                        eng.matmul(pV[t.slot(1, 2)][0:D, :], wv[:, :], HT[:, t.slot(1), 0], start=True, stop=True
                                   ).then_inc(edge_ready, 1)

                pipeline(eng, EU, DEPTH, step)

            @block.scalar
            def _(eng):
                eng.preload_act_table_set("sigmoid_and_others")
                eng.wait_ge(bt_ready, 2)

                def step(t):
                    if t.has(1, EU):
                        await_unit(eng, turned, t, 1)
                        await_free(eng, edge_ready, t, 1)
                        for side in range(2):
                            eng.activation(HT[:, t.slot(1), side], pT[side][0:D, :], ACT.Copy).then_inc(ht_ready, 1)
                        await_unit(eng, edge_ready, t, 1)
                        await_free(eng, ms_ready, t, 1, 2)
                        eng.activation(GT[:, t.slot(1, 2)], pE[t.slot(1, 2)][0:D, :], ACT.Sigmoid,
                                       bias=bt[:, 1:2]).then_inc(gate_ready, 1)

                pipeline(eng, EU, DEPTH, step)

            @block.vector
            def _(eng):
                eng.wait_ge(w_loaded, 16 * 8)
                eng.tensor_tensor(bt[:, 0:1], bq[:, 0:1], bq[:, 1:2], ALU.add).then_inc(bt_ready, 1)
                eng.wait_ge(bt_ready, 1)
                eng.tensor_tensor(bt[:, 1:2], bt[:, 0:1], bq[:, 2:3], ALU.add).then_inc(bt_ready, 1)

                def step(t):
                    if t.has(2, EU):
                        s = t.slot(2)
                        await_unit(eng, gate_ready, t, 2)
                        await_free(eng, ag_ready, t, 2, 2)
                        eng.scalar_tensor_tensor(out=MS[:, t.slot(2, 2)], in0=pV[t.slot(2, 2)][0:D, :],
                                                 scalar=bq[:, 3:4], in1=GT[:, t.slot(2, 2)],
                                                 op0=ALU.add, op1=ALU.mult).then_inc(ms_ready, 1)
                        await_unit(eng, ms_ready, t, 2)
                        await_slot(eng, side_loaded, t, 2, 32)
                        await_free(eng, agg_turned, t, 2)
                        eng.tensor_tensor_scan(AG[:, s], sm[:, s], MS[:, t.slot(2, 2)],
                                               0.0 if t.first(2) else AG[:, (s - 1) % RING, UNIT - 1:UNIT],
                                               ALU.mult, ALU.add).then_inc(ag_ready, 1)
                    if t.has(4, EU):
                        await_unit(eng, agg_turned, t, 4)
                        await_slot(eng, gathered, t, 4, 16 * 2 * GROUPS)
                        await_slot_free(eng, scattered, t, 4, 16 * GROUPS)
                        eng.tensor_tensor(O[:, t.slot(4)], G[:, t.slot(4), :, 1, D:2 * D],
                                          pO[t.slot(4, 2)][:, 0:GROUPS * D].rearrange("p (g d) -> p g d", g=GROUPS),
                                          ALU.add).then_inc(o_ready, 1)

                pipeline(eng, EU, DEPTH, step)


WEIGHTS = ["L0_gnn_W_l", "L0_gnn_b_l", "L0_gnn_W_r", "L0_gnn_b_r", "L0_gnn_att", "L0_gnn_bias_gat",
           "L0_gnn_gamma1", "L0_gnn_beta1", "L0_gnn_W1", "L0_gnn_b1", "L0_gnn_W2", "L0_gnn_b2",
           "L0_gnn_gamma2", "L0_gnn_beta2", "L1_gnn_W_kernel", "L1_gnn_W_bias", "L1_gnn_We_kernel",
           "L1_gnn_We_bias"]


def kernel(**inputs):
    import concourse.bacc as bacc
    from concourse.bass_utils import run_bass_kernel_spmd

    N = inputs["x"].shape[0]
    E = inputs["src"].shape[0]
    NP = -(-N // TILE) * TILE
    EU = -(-E // UNIT)
    EU += -EU % 2 + 2 * (EU * UNIT == E)
    EP = EU * UNIT

    x = np.zeros((NP, D), np.float32)
    x[:N] = np.asarray(inputs["x"])
    src = np.zeros(EP, np.int32)
    src[:E] = np.asarray(inputs["src"])
    dst_rows = np.zeros(EP, np.int32)
    dst_rows[:E] = np.asarray(inputs["dst"])
    dst_flat = np.full(EP + 2, N, np.int32)
    dst_flat[0] = -1
    dst_flat[1:E + 1] = np.asarray(inputs["dst"])
    edge_feats = np.zeros((D, EP), np.float32)
    edge_feats[:, :E] = np.asarray(inputs["edge_attr_64"]).T

    def groups(v):
        return np.ascontiguousarray(v.reshape(EU * GROUPS, P).T)

    both = np.stack([src.reshape(EU, GROUPS, P), dst_rows.reshape(EU, GROUPS, P)], 1)
    sel = np.zeros((P, 2, P), np.float32)
    for h in range(HEADS):
        sel[h, h // 2, (h % 2) * D:(h % 2 + 1) * D] = 1.0
    pads = np.zeros((P, 1), np.float32)
    pads[P - (NP - N) // ROWS:] = -1.0
    arrays = {
        "x": x, "edge_feats": edge_feats,
        "gather_rows": np.ascontiguousarray(both.reshape(EU, 2 * GROUPS, P).transpose(0, 2, 1)),
        "dst_flat": dst_flat[1:-1].copy(), "prev_flat": dst_flat[:-2].copy(),
        "dst_groups": groups(dst_flat[1:-1]), "next_groups": groups(dst_flat[2:]),
        "ident": np.eye(P, dtype=np.float32), "ones": np.ones((P, P), np.float32), "sel": sel, "pads": pads,
    }
    for name in WEIGHTS:
        arrays[name] = np.ascontiguousarray(inputs[name])

    nc = bacc.Bacc("TRN2", target_bir_lowering=False, num_devices=1)
    feed, aps = {}, {"nodes": N}
    for name, v in arrays.items():
        feed["in_" + name] = v
        aps[name] = nc.dram_tensor("in_" + name, v.shape, mybir.dt.from_np(v.dtype), kind="ExternalInput").ap()
    out = nc.dram_tensor("out_rows", (NP, D), F32, kind="ExternalOutput").ap()
    build(nc, aps, out)
    r = run_bass_kernel_spmd(nc, [feed], core_ids=[0])
    return r.results[0]["out_rows"][:N]
```

```python
from contextlib import ExitStack

import numpy as np

import concourse.bass as bass
from concourse import mybir

F32 = mybir.dt.float32
I32 = mybir.dt.int32
ALU = mybir.AluOpType
ACT = mybir.ActivationFunctionType
AXX = mybir.AxisListType.X

P = 128
D = 64
HEADS = 4
ROWS = 8
TILE = P * ROWS
GROUPS = 4
UNIT = P * GROUPS
RING = 4
FAR = float(1 << 22)
EPS = 1e-5
NEG_SLOPE = 0.2
RESET = 1e30


class Turn:

    def __init__(self, base, r=None):
        self.base, self.r = base, r

    def unit(self, lag=0):
        return self.base - lag if self.r is None else self.r * RING + (self.base - lag)

    def slot(self, lag=0, ring=RING):
        return (self.base - lag) % ring

    def lap(self, lag=0):
        n = (self.base - lag) // RING
        return n if self.r is None else self.r + n

    def first(self, lag=0):
        return self.r is None and self.base - lag == 0

    def has(self, lag, count):
        return self.r is not None or 0 <= self.base - lag < count


def pipeline(eng, count, depth, step):
    warm = depth + RING
    laps = (count - warm) // RING
    for i in range(warm):
        step(Turn(i))
    if laps > 0:
        with eng.Fori(0, laps) as r:
            for u in range(RING):
                step(Turn(warm + u, r))
    for i in range(warm + RING * max(laps, 0), count + depth):
        step(Turn(i))


def await_unit(eng, sem, turn, lag, per=1):
    eng.wait_ge(sem, (turn.unit(lag) + 1) * per)


def await_free(eng, sem, turn, lag, ring=RING, per=1):
    if turn.r is None and turn.base - lag < ring:
        return
    eng.wait_ge(sem, (turn.unit(lag) + (1 - ring)) * per)


def await_slot(eng, sems, turn, lag, per=16):
    eng.wait_ge(sems[turn.slot(lag)], (turn.lap(lag) + 1) * per)


def await_slot_free(eng, sems, turn, lag, per=16):
    if turn.r is None and turn.base - lag < RING:
        return
    eng.wait_ge(sems[turn.slot(lag)], turn.lap(lag) * per)


def part_wait(eng, passed):
    eng.sem_inc(passed, 1)


def build(nc, a, out):
    NP = a["x"].shape[0]
    N = a["nodes"]
    NT = NP // TILE
    EP = a["dst_flat"].shape[0]
    EU = EP // UNIT
    EC = EP // P
    PADROWS = NP - N

    def dram(name, shape, dt=F32):
        return nc.dram_tensor(name, shape, dt, kind="Internal").ap()

    h_rows = dram("h_rows", (NP, D))
    z_rows = dram("z_rows", (NP, D))
    xy_rows = dram("xy_rows", (NP, 2 * D))
    g_rows = dram("g_rows", (EU, P, GROUPS * 4 * D))
    o_rows = dram("o_rows", (EU, P, GROUPS * D))
    reset_d = dram("reset_d", (EP,))
    same_d = dram("same_d", (EP,))
    ends_d = dram("ends_d", (P, EU, GROUPS))
    sidx_d = dram("sidx_d", (P, EU, GROUPS), I32)

    def tiles(t):
        return t.rearrange("(t p j) d -> t p (j d)", p=P, j=ROWS)

    stage_sems = []
    with ExitStack() as top:
        def sb(ctx, name, shape, dt=F32):
            return ctx.enter_context(nc.sbuf_tensor(name, shape, dt))

        def sem(ctx, name):
            handle = nc.alloc_semaphore(name=name)
            if ctx is not top:
                stage_sems.append(handle)
            return handle

        def sems(ctx, name, n=RING):
            return [sem(ctx, f"{name}{i}") for i in range(n)]

        def end_stage():
            nc.clear_and_free_semaphores(stage_sems)
            stage_sems.clear()
            nc.all_engine_barrier()

        ps = [top.enter_context(nc.psum_tensor(f"ps{i}", [P, 512], F32)) for i in range(8)]
        sum_z, sum_zz = ps[6], ps[7]

        ident = sb(top, "ident", [P, P])
        ones = sb(top, "ones", [P, P])
        sel = sb(top, "sel", [P, 2, P])
        pads = sb(top, "pads", [P, 1])
        epsc = sb(top, "epsc", [P, 1])
        consts_loaded = sem(top, "consts_loaded")
        eps_set = sem(top, "eps_set")
        passed_pe = sem(top, "passed_pe")
        passed_pool = sem(top, "passed_pool")
        passed_sp = sem(top, "passed_sp")

        with ExitStack() as c:
            dst_f = sb(c, "dst_f", [P, EC], I32)
            prev_f = sb(c, "prev_f", [P, EC], I32)
            dst_g = sb(c, "dst_g", [P, EC], I32)
            next_g = sb(c, "next_g", [P, EC], I32)
            same = sb(c, "same", [P, EC])
            reset = sb(c, "reset", [P, EC])
            ends = sb(c, "ends", [P, EC])
            shifted = sb(c, "shifted", [P, EC])
            sidx = sb(c, "sidx", [P, EC], I32)
            X = sb(c, "X", [P, RING, ROWS, D])
            xc = sb(c, "xc", [P, RING, ROWS, D])
            sq = sb(c, "sq", [P, RING, ROWS, D])
            hn = sb(c, "hn", [P, RING, ROWS, D])
            hh = sb(c, "hh", [P, RING, ROWS, D])
            s1 = sb(c, "s1", [P, RING, ROWS])
            vs = sb(c, "vs", [P, RING, ROWS])
            lnv = sb(c, "lnv", [P, RING, ROWS])
            rstd = sb(c, "rstd", [P, RING, ROWS])

            lists_loaded = sem(c, "lists_loaded")
            lists_made = sem(c, "lists_made")
            lists_stored = sem(c, "lists_stored")
            x_loaded = sems(c, "x_loaded")
            h_stored = sems(c, "h_stored")
            s1_ready = sem(c, "s1_ready")
            xc_ready = sem(c, "xc_ready")
            sq_ready = sem(c, "sq_ready")
            vs_ready = sem(c, "vs_ready")
            ln_ready = sem(c, "ln_ready")
            rstd_ready = sem(c, "rstd_ready")
            hn_ready = sem(c, "hn_ready")
            hh_ready = sem(c, "hh_ready")
            h_summed = sem(c, "h_summed")
            block = c.enter_context(nc.Block())
            DEPTH = 3

            @block.sync
            def _(eng):
                for dst, src in ((dst_f, a["dst_flat"]), (prev_f, a["prev_flat"])):
                    eng.dma_start(dst[:, :], src.rearrange("(p c) -> p c", p=P)).then_inc(lists_loaded, 16)
                for dst, src in ((dst_g, a["dst_groups"]), (next_g, a["next_groups"])):
                    eng.dma_start(dst[:, :], src).then_inc(lists_loaded, 16)
                for dst, src in ((ident, a["ident"]), (ones, a["ones"]), (sel, a["sel"]), (pads, a["pads"])):
                    eng.dma_start(dst[:], src).then_inc(consts_loaded, 16)

                def step(t):
                    if t.has(0, NT):
                        await_free(eng, xc_ready, t, 0)
                        eng.dma_start(X[:, t.slot()].rearrange("p j d -> p (j d)"),
                                      tiles(a["x"])[t.unit()]).then_inc(x_loaded[t.slot()], 16)
                    if t.has(3, NT):
                        await_unit(eng, hn_ready, t, 3)
                        rows = hn[:, t.slot(3)].rearrange("p j d -> p (j d)")
                        for dst in (h_rows, z_rows):
                            eng.dma_start(tiles(dst)[t.unit(3)], rows).then_inc(h_stored[t.slot(3)], 16)

                pipeline(eng, NT, DEPTH, step)
                eng.wait_ge(lists_made, 4)
                eng.dma_start(reset_d.rearrange("(p c) -> p c", p=P), reset[:, :]).then_inc(lists_stored, 16)
                eng.dma_start(same_d.rearrange("(p c) -> p c", p=P), same[:, :]).then_inc(lists_stored, 16)
                eng.dma_start(ends_d.rearrange("p u g -> p (u g)"), ends[:, :]).then_inc(lists_stored, 16)
                eng.dma_start(sidx_d.rearrange("p u g -> p (u g)"), sidx[:, :]).then_inc(lists_stored, 16)
                eng.wait_ge(lists_stored, 64)
                for s in range(RING):
                    eng.wait_ge(h_stored[s], 32 * len(range(s, NT, RING)))

            @block.scalar
            def _(eng):
                eng.preload_act_table_set("natural_log_exp_and_others")

                def step(t):
                    if t.has(0, NT):
                        await_unit(eng, xc_ready, t, 0)
                        await_free(eng, vs_ready, t, 0)
                        eng.activation(sq[:, t.slot()], xc[:, t.slot()], ACT.Square).then_inc(sq_ready, 1)
                    if t.has(1, NT):
                        await_unit(eng, vs_ready, t, 1)
                        await_free(eng, rstd_ready, t, 1)
                        eng.activation(lnv[:, t.slot(1)], vs[:, t.slot(1)], ACT.Ln,
                                       bias=epsc[:, :], scale=1.0 / D).then_inc(ln_ready, 1)
                        await_unit(eng, ln_ready, t, 1)
                        await_free(eng, hn_ready, t, 1)
                        eng.activation(rstd[:, t.slot(1)], lnv[:, t.slot(1)], ACT.Exp,
                                       scale=-0.5).then_inc(rstd_ready, 1)
                    if t.has(2, NT):
                        await_unit(eng, hn_ready, t, 2)
                        await_free(eng, h_summed, t, 2)
                        eng.activation(hh[:, t.slot(2)], hn[:, t.slot(2)], ACT.Square).then_inc(hh_ready, 1)

                eng.wait_ge(eps_set, 1)
                pipeline(eng, NT, DEPTH, step)

            @block.vector
            def _(eng):
                eng.memset(epsc[:, :], EPS).then_inc(eps_set, 1)
                eng.wait_ge(lists_loaded, 64)
                eng.tensor_tensor(same[:, :], dst_f[:, :], prev_f[:, :], ALU.is_equal).then_inc(lists_made, 1)
                eng.tensor_tensor(ends[:, :], dst_g[:, :], next_g[:, :], ALU.not_equal).then_inc(lists_made, 1)
                eng.tensor_scalar(shifted[:, :], dst_g[:, :], -FAR, None, ALU.add).then_inc(lists_made, 1)
                eng.wait_ge(lists_made, 3)
                eng.tensor_scalar(reset[:, :], same[:, :], -1.0, RESET, ALU.add, ALU.mult)
                eng.tensor_tensor(shifted[:, :], shifted[:, :], ends[:, :], ALU.mult).then_inc(s1_ready, 1)
                eng.wait_ge(s1_ready, 1)
                eng.tensor_scalar(sidx[:, :], shifted[:, :], FAR, None, ALU.add).then_inc(lists_made, 1)

                def step(t):
                    if t.has(0, NT):
                        await_slot(eng, x_loaded, t, 0)
                        eng.tensor_reduce(s1[:, t.slot()], X[:, t.slot()], AXX, ALU.add).then_inc(s1_ready, 1)
                        eng.wait_ge(s1_ready, t.unit() + 2)
                        await_free(eng, hn_ready, t, 0)
                        await_free(eng, sq_ready, t, 0)
                        eng.scalar_tensor_tensor(
                            out=xc[:, t.slot()], in0=s1[:, t.slot()].unsqueeze(2).to_broadcast([P, ROWS, D]),
                            scalar=-1.0 / D, in1=X[:, t.slot()], op0=ALU.mult, op1=ALU.add).then_inc(xc_ready, 1)
                    if t.has(1, NT):
                        await_unit(eng, sq_ready, t, 1)
                        await_free(eng, ln_ready, t, 1)
                        eng.tensor_reduce(vs[:, t.slot(1)], sq[:, t.slot(1)], AXX, ALU.add).then_inc(vs_ready, 1)
                    if t.has(2, NT):
                        await_unit(eng, rstd_ready, t, 2)
                        await_unit(eng, xc_ready, t, 2)
                        await_free(eng, hh_ready, t, 2)
                        await_free(eng, h_summed, t, 2)
                        await_slot_free(eng, h_stored, t, 2, 32)
                        eng.scalar_tensor_tensor(
                            out=hn[:, t.slot(2)], in0=xc[:, t.slot(2)], scalar=0.0,
                            in1=rstd[:, t.slot(2)].unsqueeze(2).to_broadcast([P, ROWS, D]),
                            op0=ALU.max, op1=ALU.mult).then_inc(hn_ready, 1)

                pipeline(eng, NT, DEPTH, step)

            @block.tensor
            def _(eng):
                eng.wait_ge(consts_loaded, 64)

                def step(t):
                    if t.has(3, NT):
                        await_unit(eng, hn_ready, t, 3)
                        await_unit(eng, hh_ready, t, 3)
                        eng.matmul(sum_z[0:1, :], ones[:, 0:1], hn[:, t.slot(3)].rearrange("p j d -> p (j d)"),
                                   start=t.first(3), stop=False, skip_group_check=True)
                        eng.matmul(sum_zz[0:1, :], ones[:, 0:1], hh[:, t.slot(3)].rearrange("p j d -> p (j d)"),
                                   start=t.first(3), stop=False, skip_group_check=True).then_inc(h_summed, 1)

                pipeline(eng, NT, DEPTH, step)

        end_stage()

        with ExitStack() as c:
            wlr = sb(c, "wlr", [P, 2 * P])
            attc = sb(c, "attc", [P, 2, HEADS])
            bpre = sb(c, "bpre", [P, 2, 2])
            bsum = sb(c, "bsum", [P, 2])
            wfin = sb(c, "wfin", [P, 2, D])
            wfq = sb(c, "wfq", [P, 2, D])
            blh = sb(c, "blh", [HEADS, D])
            quarter = sb(c, "quarter", [HEADS, P])
            cb = sb(c, "cb", [P, D])
            gidx = sb(c, "gidx", [P, RING, 2 * GROUPS], I32)
            G = sb(c, "G", [P, RING, 1 + 2 * GROUPS, D])
            rs = sb(c, "rs", [HEADS, RING, UNIT])
            endf = sb(c, "endf", [P, RING, GROUPS])
            sidx = sb(c, "sidx2", [P, RING, GROUPS], I32)
            HT = sb(c, "HT", [P, RING, UNIT])
            HH = sb(c, "HH", [P, RING, UNIT])
            LK = sb(c, "LK", [P, RING, 2, UNIT])
            att_lin = sb(c, "att_lin", [P, 2, HEADS])
            att_relu = sb(c, "att_relu", [P, 2, HEADS])
            wlrT = sb(c, "wlrT", [P, 2, P])
            wlin = sb(c, "wlin", [P, HEADS])
            blin = sb(c, "blin", [P, HEADS])
            ones_rows = sb(c, "ones_rows", [P, UNIT])
            M = sb(c, "M", [HEADS, 1 + RING * UNIT])
            TT = sb(c, "TT", [HEADS, 2, 2, UNIT])
            TA = sb(c, "TA", [HEADS, 2, UNIT])
            RW = sb(c, "RW", [HEADS, 2, 2, UNIT])
            DEN = sb(c, "DEN", [HEADS, RING, UNIT])
            DG = sb(c, "DG", [HEADS, 2, UNIT])
            RC = sb(c, "RC", [HEADS, 2, UNIT])
            B = sb(c, "B", [P, RING, UNIT])
            KEEP = sb(c, "KEEP", [P, 2, 2, UNIT])
            PR = sb(c, "PR", [P, 2, 2, UNIT])
            GM = sb(c, "GM", [P, RING, 2, UNIT])
            AB = sb(c, "AB", [P, RING, GROUPS, D])
            Z = sb(c, "Z", [P, RING, GROUPS, D])
            ZH = sb(c, "ZH", [P, 2, GROUPS, D])
            QD = sb(c, "QD", [P, RING, GROUPS, D])
            pT, pS, pB, pA = ps[0:2], ps[2], ps[3:5], ps[5]

            w_loaded = sem(c, "w_loaded")
            att_zeroed = sem(c, "att_zeroed")
            w_ready = sem(c, "w_ready")
            cb_ready = sem(c, "cb_ready")
            lin_ready = sem(c, "lin_ready")
            lin_out = sem(c, "lin_out")
            gidx_loaded = sems(c, "gidx_loaded")
            reset_loaded = sems(c, "reset_loaded")
            ends_loaded = sems(c, "ends_loaded")
            gathered = sems(c, "gathered")
            scattered = sems(c, "scattered")
            turned = sem(c, "turned")
            turned_taken = sem(c, "turned_taken")
            pre_ready = sem(c, "pre_ready")
            relu_ready = sem(c, "relu_ready")
            score_ready = sem(c, "score_ready")
            m_carried = sem(c, "m_carried")
            m_ready = sem(c, "m_ready")
            ta_ready = sem(c, "ta_ready")
            tt_ready = sem(c, "tt_ready")
            rw_ready = sem(c, "rw_ready")
            den_ready = sem(c, "den_ready")
            dg_ready = sem(c, "dg_ready")
            rc_ready = sem(c, "rc_ready")
            b_ready = sem(c, "b_ready")
            share_spread = sem(c, "share_spread")
            keep_ready = sem(c, "keep_ready")
            pr_ready = sem(c, "pr_ready")
            gm_ready = sem(c, "gm_ready")
            att_out = sem(c, "att_out")
            ab_ready = sem(c, "ab_ready")
            z_ready = sem(c, "z_ready")
            zh_ready = sem(c, "zh_ready")
            qd_ready = sem(c, "qd_ready")
            z_summed = sem(c, "z_summed")
            block = c.enter_context(nc.Block())
            DEPTH = 5
            NW = 2 + HEADS + 2 + 2 + 1

            @block.sync
            def _(eng):
                eng.wait_ge(att_zeroed, 1)
                eng.dma_start(wlr[0:D, :], a["L0_gnn_W_l"]).then_inc(w_loaded, 16)
                eng.dma_start(wlr[D:P, :], a["L0_gnn_W_r"]).then_inc(w_loaded, 16)
                for h in range(HEADS):
                    eng.dma_start(attc[(h % 2) * D:(h % 2) * D + D, h // 2, h:h + 1],
                                  a["L0_gnn_att"].rearrange("h (c o) -> h c o", o=1)[h]).then_inc(w_loaded, 16)
                for i, b in enumerate(("L0_gnn_b_l", "L0_gnn_b_r")):
                    eng.dma_start(bpre[:, i, :], a[b].rearrange("(k p) -> p k", p=P),
                                  allow_slow_non_contiguous=True).then_inc(w_loaded, 16)
                for h in range(2):
                    eng.dma_start(wfin[h * D:h * D + D, :, :],
                                  a["L0_gnn_W_l"].rearrange("f (k h c) -> h f k c", k=2, h=2)[h]
                                  ).then_inc(w_loaded, 16)
                eng.dma_start(blh[:, :], a["L0_gnn_b_l"].rearrange("(h c) -> h c", h=HEADS)).then_inc(w_loaded, 16)

                def step(t):
                    if t.has(0, EU):
                        await_slot_free(eng, gathered, t, 0, 16 * 2 * GROUPS)
                        eng.dma_start(gidx[:, t.slot()], a["gather_rows"][t.unit()]
                                      ).then_inc(gidx_loaded[t.slot()], 16)
                        await_free(eng, ta_ready, t, 0)
                        await_free(eng, m_ready, t, 0)
                        eng.dma_start(rs[:, t.slot()],
                                      reset_d.rearrange("(u o e) -> u o e", o=1, e=UNIT)[t.unit()]
                                      .to_broadcast([HEADS, UNIT])).then_inc(reset_loaded[t.slot()], 16)
                    if t.has(3, EU):
                        await_slot_free(eng, scattered, t, 3, 16 * GROUPS)
                        part_wait(eng, passed_sp)
                        await_free(eng, z_summed, t, 3)
                        part_wait(eng, passed_sp)
                        eng.dma_start(endf[:, t.slot(3)], ends_d[:, t.unit(3)]).then_inc(ends_loaded[t.slot(3)], 16)
                        eng.dma_start(sidx[:, t.slot(3)], sidx_d[:, t.unit(3)]).then_inc(ends_loaded[t.slot(3)], 16)

                pipeline(eng, EU, DEPTH, step)

            @block.gpsimd
            def _(eng):
                last_row = eng.to_reg(N - 1)

                def step(t):
                    if t.has(5, EU):
                        await_unit(eng, z_ready, t, 5)
                        await_slot(eng, ends_loaded, t, 5, 32)
                        part_wait(eng, passed_pool)
                        for g in range(GROUPS):
                            eng.indirect_dma_start(
                                out=z_rows, out_offset=bass.IndirectOffsetOnAxis(
                                    ap=sidx[:, t.slot(5), g:g + 1], axis=0),
                                in_=Z[:, t.slot(5), g, :], in_offset=None, bounds_check=last_row,
                                oob_is_err=False).then_inc(scattered[t.slot(5)], 16)
                    if t.has(0, EU):
                        await_slot(eng, gidx_loaded, t, 0)
                        await_free(eng, turned, t, 0)
                        await_free(eng, zh_ready, t, 0)
                        part_wait(eng, passed_pool)
                        for g in range(GROUPS):
                            for side in range(2):
                                k = side * GROUPS + g
                                eng.indirect_dma_start(
                                    out=G[:, t.slot(), 1 + 2 * g + side, :], out_offset=None, in_=h_rows,
                                    in_offset=bass.IndirectOffsetOnAxis(ap=gidx[:, t.slot(), k:k + 1], axis=0),
                                    bounds_check=NP - 1).then_inc(gathered[t.slot()], 16)

                pipeline(eng, EU, DEPTH, step)
                for s in range(RING):
                    eng.wait_ge(scattered[s], 16 * GROUPS * len(range(s, EU, RING)))

            @block.tensor
            def _(eng):
                eng.wait_ge(w_ready, 10)
                eng.matmul(pA[:, 0:D], quarter[:, :], blh[:, :], start=True, stop=True)
                for k in range(2):
                    mm = eng.transpose(pT[0][:, k * P:k * P + P], wlr[:, k * P:k * P + P], ident[:, :])
                mm.then_inc(cb_ready, 1)
                eng.wait_ge(lin_ready, 1)
                for k in range(2):
                    eng.matmul(pT[1][:, 0:HEADS], wlrT[:, k], att_lin[:, k], start=(k == 0), stop=(k == 1))
                for k in range(2):
                    mm = eng.matmul(pT[1][0:1, HEADS:2 * HEADS], bsum[:, k:k + 1], att_lin[:, k],
                                    start=(k == 0), stop=(k == 1))
                mm.then_inc(lin_out, 1)

                def step(t):
                    if t.has(4, EU):
                        await_unit(eng, gm_ready, t, 4, 2)
                        await_free(eng, ab_ready, t, 4, 1)
                        for g in range(GROUPS):
                            for k in range(2):
                                mm = eng.matmul(pA[:, g * D:g * D + D], GM[:, t.slot(4), k, g * P:g * P + P],
                                                wfq[:, k, :], start=(k == 0), stop=(k == 1))
                        mm.then_inc(att_out, 1)
                    if t.has(3, EU):
                        await_unit(eng, b_ready, t, 3)
                        await_free(eng, pr_ready, t, 3, 1, 2)
                        await_free(eng, keep_ready, t, 3, 1, 2)
                        for k in range(2):
                            eng.matmul(pB[k][:, :], sel[:, k, :], B[:, t.slot(3)],
                                       start=True, stop=True).then_inc(share_spread, 1)
                    if t.has(1, EU):
                        await_slot(eng, gathered, t, 1, 16 * 2 * GROUPS)
                        await_free(eng, relu_ready, t, 1, 1, 2)
                        for g in range(GROUPS):
                            mm = eng.transpose(pT[0][:, g * P:g * P + P],
                                               G[:, t.slot(1), 1 + 2 * g:3 + 2 * g].rearrange("p s d -> p (s d)"),
                                               ident[:, :])
                        for g in range(GROUPS):
                            mm = eng.transpose(pT[1][:, g * P:g * P + P],
                                               G[:, t.slot(1), 2 * g:2 + 2 * g].rearrange("p s d -> p (s d)"),
                                               ident[:, :])
                        mm.then_inc(turned, 1)
                    if t.has(5, EU):
                        await_unit(eng, qd_ready, t, 5)
                        await_slot(eng, ends_loaded, t, 5, 32)
                        for g in range(GROUPS):
                            for acc, rows in ((sum_z, AB), (sum_zz, QD)):
                                mm = eng.matmul(acc[0:1, 0:D], endf[:, t.slot(5), g:g + 1], rows[:, t.slot(5), g],
                                                start=False, stop=False, skip_group_check=True)
                        mm.then_inc(z_summed, 1)
                    if t.has(1, EU):
                        await_unit(eng, turned_taken, t, 1, 3)
                        for k in range(2):
                            eng.matmul(pT[k][:, :], wlr[:, k * P:k * P + P], HT[:, t.slot(1)],
                                       start=True, stop=True).then_inc(pre_ready, 1)
                        await_free(eng, tt_ready, t, 1, 1)
                        eng.matmul(pS[0:HEADS, :], wlin[:, :], HT[:, t.slot(1)], start=True, stop=False)
                        eng.matmul(pS[0:HEADS, :], blin[:, :], ones_rows[:, :], start=False, stop=False)
                        await_unit(eng, relu_ready, t, 1, 2)
                        for k in range(2):
                            mm = eng.matmul(pS[0:HEADS, :], att_relu[:, k, :], LK[:, t.slot(1), k],
                                            start=False, stop=(k == 1))
                        mm.then_inc(score_ready, 1)

                eng.wait_ge(lin_ready, 2)
                pipeline(eng, EU, DEPTH, step)

            @block.scalar
            def _(eng):
                def step(t):
                    if t.has(1, EU):
                        await_unit(eng, turned, t, 1)
                        await_free(eng, score_ready, t, 1)
                        await_free(eng, pr_ready, t, 1, RING, 2)
                        eng.activation(HT[:, t.slot(1)], pT[0][:, :], ACT.Copy).then_inc(turned_taken, 1)
                        eng.activation(HH[0:D, t.slot(1)], pT[0][0:D, :], ACT.Copy).then_inc(turned_taken, 1)
                        eng.activation(HH[D:P, t.slot(1)], pT[1][D:P, :], ACT.Copy).then_inc(turned_taken, 1)
                    if t.has(3, EU):
                        await_free(eng, gm_ready, t, 3, 2, 2)
                        for k in range(2):
                            eng.wait_ge(pr_ready, t.unit(3) * 2 + (k + 1))
                            eng.activation(KEEP[:, t.slot(3, 2), k], pB[k][:, :], ACT.Copy, bias=1.0,
                                           scale=-1.0).then_inc(keep_ready, 1)
                    if t.has(2, EU):
                        await_unit(eng, tt_ready, t, 2)
                        await_free(eng, b_ready, t, 2, 2)
                        eng.activation(RW[:, t.slot(2, 2)], TT[:, t.slot(2, 2)], ACT.Exp).then_inc(rw_ready, 1)
                    if t.has(1, EU):
                        await_unit(eng, pre_ready, t, 1, 2)
                        for k in range(2):
                            eng.activation(LK[:, t.slot(1), k], pT[k][:, :], ACT.Relu, bias=bsum[:, k:k + 1],
                                           scale=1.0).then_inc(relu_ready, 1)

                pipeline(eng, EU, DEPTH, step)

            @block.vector
            def _(eng):
                eng.memset(attc[:, :, :], 0.0).then_inc(att_zeroed, 1)
                eng.memset(quarter[:, :], 1.0 / HEADS).then_inc(w_ready, 1)
                eng.memset(M[:, 0:1], 0.0).then_inc(w_ready, 1)
                eng.memset(G[:, :, 0], 0.0).then_inc(w_ready, 1)
                eng.memset(ones_rows[:, :], 1.0).then_inc(w_ready, 1)
                eng.memset(blin[:, :], 0.0).then_inc(w_ready, 1)
                eng.memset(B[:, :, :], 0.0).then_inc(w_ready, 1)
                eng.wait_ge(w_loaded, 16 * NW)
                eng.tensor_tensor(bsum[:, :], bpre[:, 0], bpre[:, 1], ALU.add).then_inc(w_ready, 1)
                eng.tensor_scalar(wfq[:, :, :], wfin[:, :, :], 1.0 / HEADS, None, ALU.mult).then_inc(w_ready, 1)
                eng.tensor_scalar(att_lin[:, :, :], attc[:, :, :], NEG_SLOPE, None, ALU.mult).then_inc(w_ready, 1)
                eng.tensor_scalar(att_relu[:, :, :], attc[:, :, :], 1.0 - NEG_SLOPE, None, ALU.mult).then_inc(w_ready, 1)
                eng.wait_ge(cb_ready, 1)
                eng.tensor_copy(cb[:, :], pA[:, 0:D])
                eng.tensor_copy(wlrT[:, :, :], pT[0][:, 0:2 * P].rearrange("p (k f) -> p k f", k=2)
                                ).then_inc(lin_ready, 1)
                eng.wait_ge(lin_out, 1)
                eng.wait_ge(w_ready, 10)
                eng.tensor_copy(wlin[:, :], pT[1][:, 0:HEADS])
                eng.tensor_copy(blin[0:1, :], pT[1][0:1, HEADS:2 * HEADS]).then_inc(lin_ready, 1)

                def step(t):
                    if t.has(2, EU):
                        s, s2 = t.slot(2), t.slot(2, 2)
                        lo, hi = 1 + s * UNIT, 1 + (s + 1) * UNIT
                        if s == 0 and not t.first(2):
                            await_unit(eng, m_ready, t, 3)
                            await_unit(eng, tt_ready, t, 3)
                            eng.tensor_copy(M[:, 0:1], M[:, RING * UNIT:RING * UNIT + 1]).then_inc(m_carried, 1)
                            eng.wait_ge(m_carried, t.lap(2))
                        elif not t.first(2):
                            await_unit(eng, m_ready, t, 3)
                        await_unit(eng, score_ready, t, 2)
                        await_slot(eng, reset_loaded, t, 2)
                        eng.tensor_tensor_scan(M[:, lo:hi], rs[:, s], pS[0:HEADS, :], M[:, lo - 1:lo],
                                               ALU.add, ALU.max).then_inc(m_ready, 1)
                        await_unit(eng, m_ready, t, 2)
                        await_free(eng, tt_ready, t, 2, 2)
                        eng.tensor_tensor(TA[:, s2], M[:, lo - 1:hi - 1], rs[:, s], ALU.add).then_inc(ta_ready, 1)
                        await_free(eng, rw_ready, t, 2, 2)
                        eng.tensor_tensor(TT[:, s2, 1], pS[0:HEADS, :], M[:, lo:hi], ALU.subtract)
                        await_unit(eng, ta_ready, t, 2)
                        eng.tensor_tensor(TT[:, s2, 0], TA[:, s2], M[:, lo:hi], ALU.subtract).then_inc(tt_ready, 1)
                    if t.has(3, EU):
                        await_unit(eng, turned_taken, t, 3, 3)
                        await_unit(eng, share_spread, t, 3, 2)
                        await_free(eng, gm_ready, t, 3, 2, 2)
                        for k in range(2):
                            eng.tensor_tensor(PR[:, t.slot(3, 2), k], pB[k][:, :], HH[:, t.slot(3)],
                                              ALU.mult).then_inc(pr_ready, 1)
                    if t.has(4, EU):
                        s = t.slot(4)
                        await_unit(eng, att_out, t, 4)
                        await_free(eng, z_summed, t, 4)
                        eng.tensor_tensor(AB[:, s], pA[:, 0:GROUPS * D].rearrange("p (g d) -> p g d", g=GROUPS),
                                          cb[:, :].unsqueeze(1).to_broadcast([P, GROUPS, D]),
                                          ALU.add).then_inc(ab_ready, 1)
                        await_unit(eng, ab_ready, t, 4)
                        await_slot(eng, gathered, t, 4, 16 * 2 * GROUPS)
                        await_slot_free(eng, scattered, t, 4, 16 * GROUPS)
                        eng.tensor_tensor(Z[:, s], AB[:, s], G[:, s, 2::2, :], ALU.add).then_inc(z_ready, 1)
                        await_unit(eng, z_ready, t, 4)
                        await_free(eng, qd_ready, t, 4, 2)
                        eng.tensor_tensor(ZH[:, t.slot(4, 2)], Z[:, s], G[:, s, 2:2 * GROUPS + 1:2, :],
                                          ALU.add).then_inc(zh_ready, 1)
                        await_unit(eng, zh_ready, t, 4)
                        eng.tensor_tensor(QD[:, s], ZH[:, t.slot(4, 2)], AB[:, s], ALU.mult).then_inc(qd_ready, 1)
                    if t.has(2, EU):
                        s, s2 = t.slot(2), t.slot(2, 2)
                        await_unit(eng, rw_ready, t, 2)
                        if not t.first(2):
                            await_unit(eng, den_ready, t, 3)
                        await_free(eng, dg_ready, t, 2)
                        eng.tensor_tensor_scan(DEN[:, s], RW[:, s2, 0], RW[:, s2, 1],
                                               0.0 if t.first(2) else DEN[:, (s - 1) % RING, UNIT - 1:UNIT],
                                               ALU.mult, ALU.add).then_inc(den_ready, 1)
                        await_unit(eng, den_ready, t, 2)
                        await_free(eng, rc_ready, t, 2, 2)
                        eng.tensor_scalar(DG[:, s2], DEN[:, s], 1e-16, None, ALU.max).then_inc(dg_ready, 1)
                    if t.has(3, EU):
                        await_unit(eng, pr_ready, t, 3, 2)
                        await_unit(eng, keep_ready, t, 3, 2)
                        await_free(eng, att_out, t, 3)
                        if not t.first(3):
                            await_unit(eng, gm_ready, t, 4, 2)
                        for k in range(2):
                            s = t.slot(3)
                            eng.tensor_tensor_scan(
                                GM[:, s, k], KEEP[:, t.slot(3, 2), k], PR[:, t.slot(3, 2), k],
                                0.0 if t.first(3) else GM[:, (s - 1) % RING, k, UNIT - 1:UNIT],
                                ALU.mult, ALU.add).then_inc(gm_ready, 1)
                    if t.has(2, EU):
                        s, s2 = t.slot(2), t.slot(2, 2)
                        await_unit(eng, dg_ready, t, 2)
                        await_free(eng, b_ready, t, 2, 2)
                        eng.reciprocal(RC[:, s2], DG[:, s2]).then_inc(rc_ready, 1)
                        await_unit(eng, rc_ready, t, 2)
                        await_free(eng, share_spread, t, 2, RING, 2)
                        eng.tensor_tensor(B[0:HEADS, s], RC[:, s2], RW[:, s2, 1], ALU.mult).then_inc(b_ready, 1)

                pipeline(eng, EU, DEPTH, step)

        end_stage()

        sc2b = sb(top, "sc2b", [P, D])
        sh2b = sb(top, "sh2b", [P, D])

        def fold(link, eng, s, sums, squares):
            mean, ms, m2, var = s[:, 0], s[:, 1], s[:, 2], s[:, 3]
            link(eng.tensor_reduce(mean, sums[0:1, :].rearrange("o (j d) -> o d j", j=ROWS), AXX, ALU.add))
            link(eng.tensor_reduce(ms, squares[0:1, :].rearrange("o (j d) -> o d j", j=ROWS), AXX, ALU.add))
            link(eng.tensor_scalar(mean, mean, 1.0 / N, None, ALU.mult))
            link(eng.tensor_scalar(ms, ms, 1.0 / N, None, ALU.mult))
            link(eng.tensor_tensor(m2, mean, mean, ALU.mult))
            link(eng.tensor_tensor(var, ms, m2, ALU.subtract))

        def fold_shift(link, eng, s, rstd, gamma, beta, bias, scale, shift):
            mean, mu, off, prod = s[:, 0], s[:, 4], s[:, 5], s[:, 6]
            link(eng.tensor_tensor(scale, rstd, gamma, ALU.mult))
            link(eng.tensor_tensor(mu, mean, bias, ALU.add))
            link(eng.tensor_tensor(off, bias, mu, ALU.subtract))
            link(eng.tensor_tensor(prod, off, scale, ALU.mult))
            link(eng.tensor_tensor(shift, prod, beta, ALU.add))

        with ExitStack() as c:
            vec1 = sb(c, "vec1", [1, 3, D])
            vec2 = sb(c, "vec2", [1, 3, D])
            st = sb(c, "st", [1, 10, D])
            fold1 = sb(c, "fold1", [1, 2, 2, D])
            fold2 = sb(c, "fold2", [1, 2, D])
            off2 = sb(c, "off2", [1, D])
            col1 = sb(c, "col1", [P, 2])
            sc1b = sb(c, "sc1b", [P, D])
            w1 = sb(c, "w1", [P, 2, 2 * P])
            b1c = sb(c, "b1c", [P, 2])
            w2 = sb(c, "w2", [P, 2, D])
            Zt = sb(c, "Zt", [P, RING, ROWS, D])
            XT = sb(c, "XT", [P, RING, 512])
            R = sb(c, "R", [P, 2, 2, 2, 512])
            ZS = sb(c, "ZS", [P, RING, ROWS, D])
            XY = sb(c, "XY", [P, RING, ROWS, 2, D])
            YY = sb(c, "YY", [P, 2, ROWS, D])
            accy = sb(c, "accy", [P, ROWS, D])
            accyy = sb(c, "accyy", [P, ROWS, D])
            pT, pH, pY = ps[0:2], ps[2:6], ps[6:8]

            w_zeroed = sem(c, "w_zeroed3")
            w_loaded = sem(c, "w_loaded3")
            chain = sem(c, "chain")
            var_ready = sem(c, "var_ready")
            rstd_ready = sem(c, "rstd_ready3")
            folded = sem(c, "folded")
            turned_col = sem(c, "turned_col")
            col_ready = sem(c, "col_ready")
            z_loaded = sems(c, "z_loaded")
            x_loaded = sems(c, "x_loaded3")
            y_stored = sems(c, "y_stored")
            turned = sem(c, "turned3")
            xt_ready = sem(c, "xt_ready")
            hid_ready = sem(c, "hid_ready")
            relu_a = sem(c, "relu_a")
            relu_v = sem(c, "relu_v")
            zs_ready = sem(c, "zs_ready")
            y_out = sem(c, "y_out")
            y_ready = sem(c, "y_ready")
            yy_ready = sem(c, "yy_ready")
            acc_zeroed = sem(c, "acc_zeroed")
            accy_ready = sem(c, "accy_ready")
            accyy_ready = sem(c, "accyy_ready")
            sums_ready = sem(c, "sums_ready")
            block = c.enter_context(nc.Block())
            DEPTH = 4
            links = [0]

            @block.sync
            def _(eng):
                for i, n in enumerate(("gamma1", "beta1", "bias_gat")):
                    eng.dma_start(vec1[:, i, :], a["L0_gnn_" + n].rearrange("(o d) -> o d", o=1)).then_inc(w_loaded, 16)
                for i, n in enumerate(("gamma2", "beta2", "b2")):
                    eng.dma_start(vec2[:, i, :], a["L0_gnn_" + n].rearrange("(o d) -> o d", o=1)).then_inc(w_loaded, 16)
                eng.wait_ge(w_zeroed, 1)
                for q in range(2):
                    eng.dma_start(w1[q * D:q * D + D, q, :], a["L0_gnn_W1"]).then_inc(w_loaded, 16)
                eng.dma_start(b1c[:, :], a["L0_gnn_b1"].rearrange("(k p) -> p k", p=P),
                              allow_slow_non_contiguous=True).then_inc(w_loaded, 16)
                eng.dma_start(w2[:, :, :], a["L0_gnn_W2"].rearrange("(k p) d -> p k d", p=P)).then_inc(w_loaded, 16)

                def step(t):
                    if t.has(0, NT):
                        await_free(eng, turned, t, 0)
                        await_free(eng, zs_ready, t, 0)
                        eng.dma_start(Zt[:, t.slot()].rearrange("p j d -> p (j d)"),
                                      tiles(z_rows)[t.unit()]).then_inc(z_loaded[t.slot()], 16)
                        await_slot_free(eng, y_stored, t, 0)
                        eng.dma_start(XY[:, t.slot(), :, 0, :],
                                      a["x"].rearrange("(t p j) d -> t p j d", p=P, j=ROWS)[t.unit()]
                                      ).then_inc(x_loaded[t.slot()], 16)
                    if t.has(3, NT):
                        await_unit(eng, y_ready, t, 3)
                        await_slot(eng, x_loaded, t, 3)
                        eng.dma_start(tiles(xy_rows)[t.unit(3)], XY[:, t.slot(3)].rearrange("p j s d -> p (j s d)")
                                      ).then_inc(y_stored[t.slot(3)], 16)

                pipeline(eng, NT, DEPTH, step)
                for s in range(RING):
                    eng.wait_ge(y_stored[s], 16 * len(range(s, NT, RING)))

            @block.scalar
            def _(eng):
                def rstd_of(n, k):
                    eng.wait_ge(var_ready, n)
                    eng.activation(st[:, 7], st[:, 3], ACT.Ln, bias=epsc[0:1, :]).then_inc(rstd_ready, 1)
                    eng.wait_ge(rstd_ready, k)
                    eng.activation(st[:, 8], st[:, 7], ACT.Exp, scale=-0.5).then_inc(rstd_ready, 1)

                rstd_of(1, 1)
                eng.wait_ge(col_ready, 1)

                def step(t):
                    if t.has(0, NT):
                        await_unit(eng, turned, t, 0)
                        await_free(eng, hid_ready, t, 0, RING, 4)
                        eng.activation(XT[:, t.slot()], pT[t.slot(0, 2)][:, :], ACT.Identity, bias=col1[:, 1:2],
                                       scale=col1[:, 0:1]).then_inc(xt_ready, 1)
                    if t.has(3, NT):
                        await_unit(eng, y_ready, t, 3)
                        await_free(eng, accyy_ready, t, 3, 2)
                        eng.activation(YY[:, t.slot(3, 2)], XY[:, t.slot(3), :, 1, :],
                                       ACT.Square).then_inc(yy_ready, 1)
                    if t.has(1, NT):
                        await_free(eng, y_out, t, 1, 2)
                        for k in range(2):
                            eng.wait_ge(hid_ready, t.unit(1) * 4 + (k + 1))
                            eng.activation(R[:, t.slot(1, 2), 0, k], pH[k][:, :], ACT.Relu,
                                           bias=b1c[:, k:k + 1]).then_inc(relu_a, 1)

                pipeline(eng, NT, DEPTH, step)
                rstd_of(2, 3)

            @block.vector
            def _(eng):
                def link(ins):
                    links[0] += 1
                    ins.then_inc(chain, 1)
                    eng.wait_ge(chain, links[0])

                eng.memset(w1[:, :, :], 0.0).then_inc(w_zeroed, 1)
                eng.memset(accy[:, :, :], 0.0).then_inc(acc_zeroed, 1)
                eng.memset(accyy[:, :, :], 0.0).then_inc(acc_zeroed, 1)
                eng.wait_ge(w_loaded, 16 * 10)
                fold(link, eng, st, sum_z, sum_zz)
                eng.sem_inc(var_ready, 1)
                eng.wait_ge(rstd_ready, 2)
                fold_shift(link, eng, st, st[:, 8], vec1[:, 0], vec1[:, 1], vec1[:, 2], fold1[:, 0, 0], fold1[:, 1, 0])
                link(eng.tensor_copy(fold1[:, :, 1], fold1[:, :, 0]))
                link(eng.tensor_tensor(off2[:, :], vec2[:, 2], fold1[:, 1, 0], ALU.add))
                eng.sem_inc(folded, 1)
                eng.wait_ge(turned_col, 1)
                eng.tensor_copy(col1[:, :], pH[0][:, 0:2])
                eng.tensor_copy(sc1b[:, :], pH[1][:, 0:D]).then_inc(col_ready, 1)

                def step(t):
                    if t.has(2, NT):
                        await_unit(eng, y_out, t, 2)
                        await_unit(eng, zs_ready, t, 2)
                        await_free(eng, yy_ready, t, 2)
                        await_free(eng, accy_ready, t, 2)
                        await_slot_free(eng, y_stored, t, 2)
                        eng.tensor_tensor(XY[:, t.slot(2), :, 1, :], ZS[:, t.slot(2)],
                                          pY[t.slot(2, 2)][:, :].rearrange("p (j d) -> p j d", j=ROWS),
                                          ALU.add).then_inc(y_ready, 1)
                    if t.has(1, NT):
                        await_free(eng, y_out, t, 1, 2)
                        for k in range(2):
                            eng.wait_ge(hid_ready, t.unit(1) * 4 + (3 + k))
                            eng.tensor_scalar(R[:, t.slot(1, 2), 1, k], pH[2 + k][:, :], b1c[:, k:k + 1], 0.0,
                                              ALU.add, ALU.max).then_inc(relu_v, 1)

                pipeline(eng, NT, DEPTH, step)
                eng.wait_ge(sums_ready, 1)
                fold(link, eng, st, pT[0], pT[1])
                eng.sem_inc(var_ready, 1)
                eng.wait_ge(rstd_ready, 4)
                fold_shift(link, eng, st, st[:, 8], vec2[:, 0], vec2[:, 1], off2[:, :], fold2[:, 0], fold2[:, 1])
                eng.sem_inc(folded, 1)
                eng.wait_ge(turned_col, 2)
                eng.tensor_copy(sc2b[:, :], pH[0][:, 0:D])
                eng.tensor_copy(sh2b[:, :], pH[0][:, D:2 * D])

            @block.gpsimd
            def _(eng):
                eng.wait_ge(col_ready, 1)

                def step(t):
                    if t.has(0, NT):
                        await_slot(eng, z_loaded, t, 0)
                        await_free(eng, y_ready, t, 0)
                        eng.tensor_tensor(ZS[:, t.slot()], Zt[:, t.slot()],
                                          sc1b[:, :].unsqueeze(1).to_broadcast([P, ROWS, D]),
                                          ALU.mult).then_inc(zs_ready, 1)
                    if t.has(4, NT):
                        await_unit(eng, y_ready, t, 4)
                        if t.first(4):
                            eng.wait_ge(acc_zeroed, 2)
                        else:
                            await_unit(eng, accy_ready, t, 5)
                        eng.tensor_tensor(accy[:, :, :], accy[:, :, :], XY[:, t.slot(4), :, 1, :],
                                          ALU.add).then_inc(accy_ready, 1)
                        await_unit(eng, yy_ready, t, 4)
                        if not t.first(4):
                            await_unit(eng, accyy_ready, t, 5)
                        eng.tensor_tensor(accyy[:, :, :], accyy[:, :, :], YY[:, t.slot(4, 2)],
                                          ALU.add).then_inc(accyy_ready, 1)

                pipeline(eng, NT, DEPTH, step)

            @block.tensor
            def _(eng):
                eng.wait_ge(folded, 1)
                for k in range(2):
                    eng.matmul(pH[0][:, k:k + 1], fold1[:, k].rearrange("o t d -> o (t d)"), ones[0:1, 0:1],
                               start=True, stop=True)
                eng.matmul(pH[1][:, 0:D], ones[0:1, :], fold1[:, 0, 0], start=True, stop=True
                           ).then_inc(turned_col, 1)
                eng.wait_ge(col_ready, 1)

                def step(t):
                    if t.has(0, NT):
                        await_slot(eng, z_loaded, t, 0)
                        await_free(eng, xt_ready, t, 0, 2)
                        for g in range(4):
                            mm = eng.transpose(pT[t.slot(0, 2)][:, g * P:g * P + P],
                                               Zt[:, t.slot(), 2 * g:2 * g + 2].rearrange("p j d -> p (j d)"),
                                               ident[:, :])
                        mm.then_inc(turned, 1)
                    if t.has(2, NT):
                        await_unit(eng, relu_a, t, 2, 2)
                        await_unit(eng, relu_v, t, 2, 2)
                        await_free(eng, y_ready, t, 2, 2)
                        o = pY[t.slot(2, 2)]
                        for g in range(4):
                            for q in range(2):
                                for k in range(2):
                                    mm = eng.matmul(o[:, (2 * g + q) * D:(2 * g + q + 1) * D],
                                                    R[:, t.slot(2, 2), q, k, g * P:g * P + P], w2[:, k, :],
                                                    start=(k == 0), stop=(k == 1))
                        mm.then_inc(y_out, 1)
                    if t.has(1, NT):
                        await_unit(eng, xt_ready, t, 1)
                        for q in range(2):
                            if q == 0:
                                await_free(eng, relu_a, t, 1, 1, 2)
                            else:
                                await_free(eng, relu_v, t, 1, 1, 2)
                            for k in range(2):
                                eng.matmul(pH[2 * q + k][:, :], w1[:, q, k * P:k * P + P],
                                           XT[:, t.slot(1)], start=True, stop=True).then_inc(hid_ready, 1)

                pipeline(eng, NT, DEPTH, step)
                eng.wait_ge(accy_ready, NT)
                eng.wait_ge(accyy_ready, NT)
                last = NT - 1
                eng.matmul(pT[0][0:1, :], ones[:, 0:1], accy[:, :, :].rearrange("p j d -> p (j d)"),
                           start=True, stop=False)
                eng.matmul(pT[0][0:1, :].rearrange("o (j d) -> o j d", j=ROWS), pads[:, :],
                           XY[:, last % RING, :, 1, :], start=False, stop=True)
                eng.matmul(pT[1][0:1, :], ones[:, 0:1], accyy[:, :, :].rearrange("p j d -> p (j d)"),
                           start=True, stop=False)
                eng.matmul(pT[1][0:1, :], pads[:, :], YY[:, last % 2].rearrange("p j d -> p (j d)"),
                           start=False, stop=True).then_inc(sums_ready, 1)
                eng.wait_ge(folded, 2)
                eng.matmul(pH[0][:, 0:2 * D], ones[0:1, :], fold2[:, :, :].rearrange("o k d -> o (k d)"),
                           start=True, stop=True).then_inc(turned_col, 1)


        end_stage()

        with ExitStack() as c:
            class Rows:

                def __init__(self, kind):
                    self.XY = sb(c, "XY_" + kind, [P, RING, ROWS, 2, D])
                    self.v1 = sb(c, "v1_" + kind, [P, ROWS, D])
                    self.v2 = sb(c, "v2_" + kind, [P, ROWS, D])
                    self.xf = sb(c, "xf_" + kind, [P, RING, ROWS, D])
                    self.xc = sb(c, "xc_" + kind, [P, RING, ROWS, D])
                    self.sq = sb(c, "sq_" + kind, [P, 2, ROWS, D])
                    self.hn = sb(c, "hn_" + kind, [P, 2, ROWS, D])
                    self.HT = sb(c, "HT_" + kind, [P, RING, 512])
                    self.s1 = sb(c, "s1_" + kind, [P, RING, ROWS])
                    self.vs = sb(c, "vs_" + kind, [P, RING, ROWS])
                    self.lnv = sb(c, "lnv_" + kind, [P, RING, ROWS])
                    self.rstd = sb(c, "rstd_" + kind, [P, RING, ROWS])
                    self.loaded = sems(c, "xy_loaded_" + kind)
                    self.v1_ready = sem(c, "v1_ready_" + kind)
                    self.v2_ready = sem(c, "v2_ready_" + kind)
                    self.xf_ready = sem(c, "xf_ready_" + kind)
                    self.s1_ready = sem(c, "s1_ready_" + kind)
                    self.xc_ready = sem(c, "xc_ready_" + kind)
                    self.sq_ready = sem(c, "sq_ready_" + kind)
                    self.vs_ready = sem(c, "vs_ready_" + kind)
                    self.ln_ready = sem(c, "ln_ready_" + kind)
                    self.rstd_ready = sem(c, "rstd_ready_" + kind)
                    self.h_ready = sem(c, "h_ready_" + kind)
                    self.turned = sem(c, "turned_" + kind)
                    self.ht_ready = sem(c, "ht_ready_" + kind)

            n_, e_ = Rows("nodes"), Rows("edges")
            whh = sb(c, "whh", [P, 2, D])
            bh = sb(c, "bh", [P, ROWS, D])
            On = sb(c, "On", [P, RING, 512])
            wkq = sb(c, "wkq", [P, D])
            wv = sb(c, "wv", [P, D])
            wo = sb(c, "wo", [P, D])
            we = sb(c, "we", [P, D])
            wag = sb(c, "wag", [P, D])
            bq = sb(c, "bq", [D, 4])
            bt = sb(c, "bt", [D, 3])
            gidx = sb(c, "gidx4", [P, RING, 2 * GROUPS], I32)
            Gr = sb(c, "Gr", [P, RING, GROUPS, 2, 2 * D])
            XD = sb(c, "XD", [P, RING, GROUPS, D])
            sm = sb(c, "sm", [D, RING, UNIT])
            ea = sb(c, "ea", [P, RING, UNIT])
            EX = sb(c, "EX", [D, 2, UNIT])
            SP = sb(c, "SP", [D, 2, UNIT])
            GT = sb(c, "GT", [D, 2, UNIT])
            MS = sb(c, "MS", [D, 2, UNIT])
            AG = sb(c, "AG", [P, RING, UNIT])
            Oe = sb(c, "Oe", [P, RING, GROUPS, D])
            Os = sb(c, "Os", [P, RING, GROUPS, D])
            sidx = sb(c, "sidx4", [P, RING, GROUPS], I32)
            pT, pE, pV, pO = ps[0:2], ps[2:4], ps[4:6], ps[6:8]

            w_zeroed = sem(c, "w_zeroed4")
            w_loaded = sem(c, "w_loaded4")
            bt_ready = sem(c, "bt_ready")
            proj_ready = sem(c, "proj_ready")
            on_ready = sem(c, "on_ready")
            rows_stored = sems(c, "rows_stored")
            gidx_loaded = sems(c, "gidx_loaded4")
            gathered = sems(c, "gathered4")
            spilled = sems(c, "spilled")
            side_loaded = sems(c, "side_loaded")
            xd_ready = sem(c, "xd_ready")
            edge_ready = sem(c, "edge_ready")
            ex_ready = sem(c, "ex_ready")
            softplus_ready = sem(c, "softplus_ready")
            gate_ready = sem(c, "gate_ready")
            ms_ready = sem(c, "ms_ready")
            ag_ready = sem(c, "ag_ready")
            out_ready = sem(c, "out_ready")
            oe_ready = sem(c, "oe_ready")
            o_stored = sems(c, "o_stored")
            os_loaded = sems(c, "os_loaded")
            scattered = sems(c, "scattered4")
            block = c.enter_context(nc.Block())
            DEPTH = 7
            ZEROED = 9

            def center(eng, t, b):
                s = t.slot(2)
                await_slot(eng, b.loaded, t, 2)
                if not t.first(2):
                    await_unit(eng, b.v2_ready, t, 3)
                eng.tensor_tensor(b.v1[:, :, :], b.XY[:, s, :, 1, :],
                                  sc2b[:, :].unsqueeze(1).to_broadcast([P, ROWS, D]),
                                  ALU.mult).then_inc(b.v1_ready, 1)
                await_unit(eng, b.v1_ready, t, 2)
                if not t.first(2):
                    await_unit(eng, b.xf_ready, t, 3)
                eng.tensor_tensor(b.v2[:, :, :], b.v1[:, :, :], b.XY[:, s, :, 0, :], ALU.add
                                  ).then_inc(b.v2_ready, 1)
                await_unit(eng, b.v2_ready, t, 2)
                await_free(eng, on_ready if b is n_ else xd_ready, t, 2)
                eng.tensor_tensor(b.xf[:, s], b.v2[:, :, :], sh2b[:, :].unsqueeze(1).to_broadcast([P, ROWS, D]),
                                  ALU.add).then_inc(b.xf_ready, 1)
                await_unit(eng, b.xf_ready, t, 2)
                await_free(eng, b.xc_ready, t, 2)
                eng.tensor_reduce(b.s1[:, s], b.xf[:, s], AXX, ALU.add).then_inc(b.s1_ready, 1)
                await_unit(eng, b.s1_ready, t, 2)
                await_free(eng, b.h_ready, t, 2)
                await_free(eng, b.sq_ready, t, 2)
                eng.scalar_tensor_tensor(
                    out=b.xc[:, s], in0=b.s1[:, s].unsqueeze(2).to_broadcast([P, ROWS, D]),
                    scalar=-1.0 / D, in1=b.xf[:, s], op0=ALU.mult, op1=ALU.add).then_inc(b.xc_ready, 1)

            def sum_squares(eng, t, b):
                await_unit(eng, b.sq_ready, t, 3)
                await_free(eng, b.ln_ready, t, 3)
                eng.tensor_reduce(b.vs[:, t.slot(3)], b.sq[:, t.slot(3, 2)], AXX, ALU.add).then_inc(b.vs_ready, 1)

            def scale(eng, t, b):
                await_unit(eng, b.rstd_ready, t, 4)
                await_unit(eng, b.xc_ready, t, 4)
                await_free(eng, b.turned, t, 4, 2)
                eng.scalar_tensor_tensor(
                    out=b.hn[:, t.slot(4, 2)], in0=b.xc[:, t.slot(4)], scalar=0.0,
                    in1=b.rstd[:, t.slot(4)].unsqueeze(2).to_broadcast([P, ROWS, D]),
                    op0=ALU.max, op1=ALU.mult).then_inc(b.h_ready, 1)

            def square(eng, t, b):
                await_unit(eng, b.xc_ready, t, 2)
                await_free(eng, b.vs_ready, t, 2, 2)
                eng.activation(b.sq[:, t.slot(2, 2)], b.xc[:, t.slot(2)], ACT.Square).then_inc(b.sq_ready, 1)

            def deviation(eng, t, b):
                await_unit(eng, b.vs_ready, t, 3)
                await_free(eng, b.rstd_ready, t, 3)
                eng.activation(b.lnv[:, t.slot(3)], b.vs[:, t.slot(3)], ACT.Ln,
                               bias=epsc[:, :], scale=1.0 / D).then_inc(b.ln_ready, 1)
                await_unit(eng, b.ln_ready, t, 3)
                await_free(eng, b.h_ready, t, 3)
                eng.activation(b.rstd[:, t.slot(3)], b.lnv[:, t.slot(3)], ACT.Exp,
                               scale=-0.5).then_inc(b.rstd_ready, 1)

            def turn_rows(eng, t, b):
                await_unit(eng, b.h_ready, t, 4)
                await_free(eng, b.ht_ready, t, 4, 2)
                for g in range(4):
                    mm = eng.transpose(pT[t.slot(4, 2)][:, g * P:g * P + P],
                                       b.hn[:, t.slot(4, 2), 2 * g:2 * g + 2].rearrange("p j d -> p (j d)"),
                                       ident[:, :])
                mm.then_inc(b.turned, 1)

            def take_turned(eng, t, b):
                await_unit(eng, b.turned, t, 4)
                await_free(eng, proj_ready if b is n_ else out_ready, t, 4)
                eng.activation(b.HT[:, t.slot(4)], pT[t.slot(4, 2)][:, :], ACT.Copy).then_inc(b.ht_ready, 1)

            @block.sync
            def _(eng):
                W = a["L1_gnn_W_kernel"]
                wb = a["L1_gnn_W_bias"].rearrange("(o d) -> o d", o=1)
                wc = a["L1_gnn_W_bias"].rearrange("(k d o) -> k d o", k=4, o=1)
                eng.wait_ge(w_zeroed, ZEROED)
                for dst, src in ((whh[0:D, 0], W[:, 0:D]), (whh[D:P, 1], W[:, 0:D]),
                                 (wkq[0:D, :], W[:, 2 * D:3 * D]), (wkq[D:P, :], W[:, D:2 * D]),
                                 (wv[0:D, :], W[:, 3 * D:4 * D]), (wo[D:P, :], W[:, 0:D]),
                                 (we[0:D, :], a["L1_gnn_We_kernel"]), (wag[0:D, :], a["ident"][0:D, 0:D]),
                                 (wag[D:D + 1, :], wb[:, 0:D])):
                    eng.dma_start(dst, src).then_inc(w_loaded, 16)
                for j in range(ROWS):
                    eng.dma_start(bh[0:1, j, :], wb[:, 0:D]).then_inc(w_loaded, 16)
                for i, src in enumerate((wc[1], wc[2], a["L1_gnn_We_bias"].rearrange("(d o) -> d o", o=1), wc[3])):
                    eng.dma_start(bq[:, i:i + 1], src).then_inc(w_loaded, 16)

                def gathers(t):
                    if t.has(0, EU):
                        await_slot_free(eng, gathered, t, 0, 16 * 2 * GROUPS)
                        eng.dma_start(gidx[:, t.slot()], a["gather_rows"][t.unit()]
                                      ).then_inc(gidx_loaded[t.slot()], 16)
                    if t.has(1, EU):
                        await_slot(eng, gathered, t, 1, 16 * 2 * GROUPS)
                        eng.dma_start(g_rows[t.unit(1)], Gr[:, t.slot(1)].rearrange("p g e s -> p (g e s)")
                                      ).then_inc(spilled[t.slot(1)], 16)

                def scatters(t):
                    if t.has(0, EU):
                        await_slot(eng, o_stored, t, 0)
                        await_slot_free(eng, scattered, t, 0, 16 * GROUPS)
                        eng.dma_start(Os[:, t.slot()].rearrange("p g d -> p (g d)"),
                                      o_rows[t.unit()]).then_inc(os_loaded[t.slot()], 16)
                        eng.dma_start(sidx[:, t.slot()], sidx_d[:, t.unit()]).then_inc(os_loaded[t.slot()], 16)

                pipeline(eng, EU, 1, gathers)
                pipeline(eng, EU, 0, scatters)

            @block.gpsimd
            def _(eng):
                last_row = eng.to_reg(N - 1)
                last_any = eng.to_reg(NP - 1)

                def gather(t):
                    if t.has(0, EU):
                        await_slot(eng, gidx_loaded, t, 0)
                        await_slot_free(eng, spilled, t, 0)
                        part_wait(eng, passed_pool)
                        for g in range(GROUPS):
                            for side in range(2):
                                k = side * GROUPS + g
                                eng.indirect_dma_start(
                                    out=Gr[:, t.slot(), g, side], out_offset=None, in_=xy_rows,
                                    in_offset=bass.IndirectOffsetOnAxis(ap=gidx[:, t.slot(), k:k + 1], axis=0),
                                    bounds_check=last_any).then_inc(gathered[t.slot()], 16)

                def scatter(t):
                    if t.has(0, EU):
                        await_slot(eng, os_loaded, t, 0, 32)
                        part_wait(eng, passed_pool)
                        for g in range(GROUPS):
                            eng.indirect_dma_start(
                                out=out, out_offset=bass.IndirectOffsetOnAxis(
                                    ap=sidx[:, t.slot(), g:g + 1], axis=0),
                                in_=Os[:, t.slot(), g, :], in_offset=None, bounds_check=last_row,
                                oob_is_err=False).then_inc(scattered[t.slot()], 16)

                pipeline(eng, EU, 0, gather)
                for s in range(RING):
                    eng.wait_ge(rows_stored[s], 16 * len(range(s, NT, RING)))
                pipeline(eng, EU, 0, scatter)
                for s in range(RING):
                    eng.wait_ge(scattered[s], 16 * GROUPS * len(range(s, EU, RING)))

            @block.scalar
            def _(eng):
                def nodes(t):
                    if t.has(0, NT):
                        await_free(eng, n_.v2_ready, t, 0)
                        eng.dma_start(n_.XY[:, t.slot()].rearrange("p j s d -> p (j s d)"),
                                      tiles(xy_rows)[t.unit()]).then_inc(n_.loaded[t.slot()], 16)
                    if t.has(4, NT):
                        take_turned(eng, t, n_)
                    if t.has(3, NT):
                        deviation(eng, t, n_)
                    if t.has(2, NT):
                        square(eng, t, n_)
                    if t.has(7, NT):
                        await_unit(eng, on_ready, t, 7)
                        eng.dma_start(tiles(out)[t.unit(7)], On[:, t.slot(7)]).then_inc(rows_stored[t.slot(7)], 16)

                def edges(t):
                    if t.has(0, EU):
                        await_slot(eng, spilled, t, 0)
                        await_free(eng, e_.v2_ready, t, 0)
                        eng.dma_start(e_.XY[:, t.slot()].rearrange("p j s d -> p (j s d)"),
                                      g_rows[t.unit()]).then_inc(e_.loaded[t.slot()], 16)
                    if t.has(3, EU):
                        await_free(eng, ag_ready, t, 3)
                        await_free(eng, edge_ready, t, 3)
                        eng.dma_start(sm[:, t.slot(3)],
                                      same_d.rearrange("(u o e) -> u o e", o=1, e=UNIT)[t.unit(3)]
                                      .to_broadcast([D, UNIT])).then_inc(side_loaded[t.slot(3)], 16)
                        eng.dma_start(ea[0:D, t.slot(3)],
                                      a["edge_feats"].rearrange("f (u e) -> u f e", e=UNIT)[t.unit(3)]
                                      ).then_inc(side_loaded[t.slot(3)], 16)
                    if t.has(5, EU):
                        await_unit(eng, edge_ready, t, 5)
                        await_free(eng, softplus_ready, t, 5, 2)
                        eng.activation(EX[:, t.slot(5, 2)], pE[t.slot(5, 2)][0:D, :], ACT.Exp,
                                       bias=bt[:, 2:3], scale=-1.0).then_inc(ex_ready, 1)
                        await_unit(eng, ex_ready, t, 5)
                        await_free(eng, gate_ready, t, 5, 2)
                        eng.activation(SP[:, t.slot(5, 2)], EX[:, t.slot(5, 2)], ACT.Ln, bias=ones[0:D, 0:1]
                                       ).then_inc(softplus_ready, 1)
                        await_unit(eng, softplus_ready, t, 5)
                        await_free(eng, ms_ready, t, 5, 2)
                        eng.activation(GT[:, t.slot(5, 2)], SP[:, t.slot(5, 2)], ACT.Exp, scale=-1.0
                                       ).then_inc(gate_ready, 1)
                    if t.has(4, EU):
                        take_turned(eng, t, e_)
                    if t.has(3, EU):
                        deviation(eng, t, e_)
                    if t.has(4, EU):
                        await_unit(eng, e_.xf_ready, t, 4)
                        await_free(eng, oe_ready, t, 4)
                        eng.activation(XD[:, t.slot(4)],
                                       e_.xf[:, t.slot(4)].rearrange("p (g e) d -> p g e d", e=2)[:, :, 1],
                                       ACT.Copy).then_inc(xd_ready, 1)
                    if t.has(2, EU):
                        square(eng, t, e_)
                    if t.has(8, EU):
                        await_unit(eng, oe_ready, t, 8)
                        eng.dma_start(o_rows[t.unit(8)], Oe[:, t.slot(8)].rearrange("p g d -> p (g d)")
                                      ).then_inc(o_stored[t.slot(8)], 16)

                eng.wait_ge(bt_ready, 3)
                eng.wait_ge(w_zeroed, ZEROED)
                pipeline(eng, NT, DEPTH, nodes)
                pipeline(eng, EU, DEPTH + 1, edges)

            @block.vector
            def _(eng):
                for t_ in (whh, bh, wv, wo, we, wag, ea, AG):
                    eng.memset(t_[:], 0.0).then_inc(w_zeroed, 1)
                eng.wait_ge(w_zeroed, ZEROED - 1)
                eng.memset(AG[D:D + 1, :, :], 1.0).then_inc(w_zeroed, 1)
                eng.wait_ge(w_loaded, 16 * (9 + ROWS + 4))
                eng.tensor_tensor(bt[:, 0:1], bq[:, 0:1], bq[:, 1:2], ALU.add).then_inc(bt_ready, 1)
                eng.wait_ge(bt_ready, 1)
                eng.tensor_tensor(bt[:, 1:2], bt[:, 0:1], bq[:, 2:3], ALU.add).then_inc(bt_ready, 1)
                eng.wait_ge(bt_ready, 2)
                eng.tensor_scalar(bt[:, 2:3], bt[:, 1:2], -1.0, None, ALU.mult).then_inc(bt_ready, 1)

                def nodes(t):
                    if t.has(6, NT):
                        await_unit(eng, proj_ready, t, 6)
                        await_slot_free(eng, rows_stored, t, 6)
                        eng.tensor_tensor(On[:, t.slot(6)], n_.xf[:, t.slot(6)].rearrange("p j d -> p (j d)"),
                                          pO[t.slot(6, 2)][:, :], ALU.add).then_inc(on_ready, 1)
                    if t.has(4, NT):
                        scale(eng, t, n_)
                    if t.has(2, NT):
                        center(eng, t, n_)
                    if t.has(3, NT):
                        sum_squares(eng, t, n_)

                def edges(t):
                    if t.has(7, EU):
                        await_unit(eng, out_ready, t, 7)
                        await_unit(eng, xd_ready, t, 7)
                        await_slot_free(eng, o_stored, t, 7)
                        eng.tensor_tensor(Oe[:, t.slot(7)], XD[:, t.slot(7)],
                                          pO[t.slot(7, 2)][:, 0:GROUPS * D].rearrange("p (g d) -> p g d", g=GROUPS),
                                          ALU.add).then_inc(oe_ready, 1)
                    if t.has(4, EU):
                        scale(eng, t, e_)
                    if t.has(6, EU):
                        s, s2 = t.slot(6), t.slot(6, 2)
                        await_unit(eng, gate_ready, t, 6)
                        await_free(eng, ag_ready, t, 6, 2)
                        eng.scalar_tensor_tensor(out=MS[:, s2], in0=pV[s2][0:D, :], scalar=bq[:, 3:4],
                                                 in1=GT[:, s2], op0=ALU.add, op1=ALU.mult).then_inc(ms_ready, 1)
                        await_unit(eng, ms_ready, t, 6)
                        await_slot(eng, side_loaded, t, 6, 32)
                        await_free(eng, out_ready, t, 6)
                        eng.tensor_tensor_scan(AG[0:D, s], sm[:, s], MS[:, s2],
                                               0.0 if t.first(6) else AG[0:D, (s - 1) % RING, UNIT - 1:UNIT],
                                               ALU.mult, ALU.add).then_inc(ag_ready, 1)
                    if t.has(2, EU):
                        center(eng, t, e_)
                    if t.has(3, EU):
                        sum_squares(eng, t, e_)

                pipeline(eng, NT, DEPTH, nodes)
                pipeline(eng, EU, DEPTH + 1, edges)

            @block.tensor
            def _(eng):
                eng.wait_ge(w_zeroed, ZEROED)
                eng.wait_ge(w_loaded, 16 * (9 + ROWS + 4))

                def nodes(t):
                    if t.has(5, NT):
                        await_unit(eng, n_.ht_ready, t, 5)
                        await_free(eng, on_ready, t, 5, 2)
                        o = pO[t.slot(5, 2)]
                        eng.matmul(o[:, :], ones[:, :], bh[:, :, :].rearrange("o j d -> o (j d)"),
                                   start=True, stop=False, skip_group_check=True)
                        for g in range(4):
                            mm = eng.matmul(o[:, g * P:g * P + P], n_.HT[:, t.slot(5), g * P:g * P + P],
                                            whh[:, :, :].rearrange("p q d -> p (q d)"),
                                            start=False, stop=True, skip_group_check=True)
                        mm.then_inc(proj_ready, 1)
                    if t.has(4, NT):
                        turn_rows(eng, t, n_)

                def edges(t):
                    if t.has(5, EU):
                        s, s2 = t.slot(5), t.slot(5, 2)
                        await_unit(eng, e_.ht_ready, t, 5)
                        await_slot(eng, side_loaded, t, 5, 32)
                        await_free(eng, ex_ready, t, 5, 2)
                        await_free(eng, ms_ready, t, 5, 2)
                        eng.matmul(pE[s2][0:D, :], we[:, :], ea[:, s], start=True, stop=False)
                        eng.matmul(pE[s2][0:D, :], wkq[:, :], e_.HT[:, s], start=False, stop=True)
                        eng.matmul(pV[s2][0:D, :], wv[:, :], e_.HT[:, s], start=True, stop=True
                                   ).then_inc(edge_ready, 1)
                    if t.has(4, EU):
                        turn_rows(eng, t, e_)
                    if t.has(6, EU):
                        await_unit(eng, ag_ready, t, 6)
                        await_free(eng, oe_ready, t, 6, 2)
                        o = pO[t.slot(6, 2)]
                        for g in range(GROUPS):
                            eng.matmul(o[:, g * D:g * D + D], e_.HT[:, t.slot(6), g * P:g * P + P], wo[:, :],
                                       start=True, stop=False)
                            mm = eng.matmul(o[:, g * D:g * D + D], AG[:, t.slot(6), g * P:g * P + P], wag[:, :],
                                            start=False, stop=True)
                        mm.then_inc(out_ready, 1)

                pipeline(eng, NT, DEPTH, nodes)
                eng.wait_ge(on_ready, NT)
                eng.wait_ge(n_.ht_ready, NT)
                pipeline(eng, EU, DEPTH + 1, edges)


WEIGHTS = ["L0_gnn_W_l", "L0_gnn_b_l", "L0_gnn_W_r", "L0_gnn_b_r", "L0_gnn_att", "L0_gnn_bias_gat",
           "L0_gnn_gamma1", "L0_gnn_beta1", "L0_gnn_W1", "L0_gnn_b1", "L0_gnn_W2", "L0_gnn_b2",
           "L0_gnn_gamma2", "L0_gnn_beta2", "L1_gnn_W_kernel", "L1_gnn_W_bias", "L1_gnn_We_kernel",
           "L1_gnn_We_bias"]


def kernel(**inputs):
    import concourse.bacc as bacc
    from concourse.bass_utils import run_bass_kernel_spmd

    N = inputs["x"].shape[0]
    E = inputs["src"].shape[0]
    NP = -(-N // TILE) * TILE
    EU = -(-E // UNIT)
    EU += -EU % 2 + 2 * (EU * UNIT == E)
    EP = EU * UNIT

    x = np.zeros((NP, D), np.float32)
    x[:N] = np.asarray(inputs["x"])
    src = np.zeros(EP, np.int32)
    src[:E] = np.asarray(inputs["src"])
    dst_rows = np.zeros(EP, np.int32)
    dst_rows[:E] = np.asarray(inputs["dst"])
    dst_flat = np.full(EP + 2, N, np.int32)
    dst_flat[0] = -1
    dst_flat[1:E + 1] = np.asarray(inputs["dst"])
    edge_feats = np.zeros((D, EP), np.float32)
    edge_feats[:, :E] = np.asarray(inputs["edge_attr_64"]).T

    def groups(v):
        return np.ascontiguousarray(v.reshape(EU * GROUPS, P).T)

    both = np.stack([src.reshape(EU, GROUPS, P), dst_rows.reshape(EU, GROUPS, P)], 1)
    sel = np.zeros((P, 2, P), np.float32)
    for h in range(HEADS):
        sel[h, h // 2, (h % 2) * D:(h % 2 + 1) * D] = 1.0
    pads = np.zeros((P, 1), np.float32)
    pads[P - (NP - N) // ROWS:] = -1.0
    arrays = {
        "x": x, "edge_feats": edge_feats,
        "gather_rows": np.ascontiguousarray(both.reshape(EU, 2 * GROUPS, P).transpose(0, 2, 1)),
        "dst_flat": dst_flat[1:-1].copy(), "prev_flat": dst_flat[:-2].copy(),
        "dst_groups": groups(dst_flat[1:-1]), "next_groups": groups(dst_flat[2:]),
        "ident": np.eye(P, dtype=np.float32), "ones": np.ones((P, P), np.float32), "sel": sel, "pads": pads,
    }
    for name in WEIGHTS:
        arrays[name] = np.ascontiguousarray(inputs[name])

    nc = bacc.Bacc("TRN2", target_bir_lowering=False, num_devices=1)
    feed, aps = {}, {"nodes": N}
    for name, v in arrays.items():
        feed["in_" + name] = v
        aps[name] = nc.dram_tensor("in_" + name, v.shape, mybir.dt.from_np(v.dtype), kind="ExternalInput").ap()
    out = nc.dram_tensor("out_rows", (NP, D), F32, kind="ExternalOutput").ap()
    build(nc, aps, out)
    r = run_bass_kernel_spmd(nc, [feed], core_ids=[0])
    return r.results[0]["out_rows"][:N]
```

```python
from contextlib import ExitStack

import numpy as np

import concourse.bass as bass
from concourse import mybir

F32 = mybir.dt.float32
I32 = mybir.dt.int32
ALU = mybir.AluOpType
ACT = mybir.ActivationFunctionType
AXX = mybir.AxisListType.X

P = 128
D = 64
HEADS = 4
ROWS = 8
TILE = P * ROWS
GROUPS = 4
UNIT = P * GROUPS
RING = 4
FAR = float(1 << 22)
EPS = 1e-5
NEG_SLOPE = 0.2
RESET = 1e30


class Turn:

    def __init__(self, base, r=None):
        self.base, self.r = base, r

    def unit(self, lag=0):
        return self.base - lag if self.r is None else self.r * RING + (self.base - lag)

    def slot(self, lag=0, ring=RING):
        return (self.base - lag) % ring

    def lap(self, lag=0):
        n = (self.base - lag) // RING
        return n if self.r is None else self.r + n

    def first(self, lag=0):
        return self.r is None and self.base - lag == 0

    def has(self, lag, count):
        return self.r is not None or 0 <= self.base - lag < count


def pipeline(eng, count, depth, step):
    warm = depth + RING
    laps = (count - warm) // RING
    for i in range(warm):
        step(Turn(i))
    if laps > 0:
        with eng.Fori(0, laps) as r:
            for u in range(RING):
                step(Turn(warm + u, r))
    for i in range(warm + RING * max(laps, 0), count + depth):
        step(Turn(i))


def await_unit(eng, sem, turn, lag, per=1):
    eng.wait_ge(sem, (turn.unit(lag) + 1) * per)


def await_free(eng, sem, turn, lag, ring=RING, per=1):
    if turn.r is None and turn.base - lag < ring:
        return
    eng.wait_ge(sem, (turn.unit(lag) + (1 - ring)) * per)


def await_slot(eng, sems, turn, lag, per=16):
    eng.wait_ge(sems[turn.slot(lag)], (turn.lap(lag) + 1) * per)


def await_slot_free(eng, sems, turn, lag, per=16):
    if turn.r is None and turn.base - lag < RING:
        return
    eng.wait_ge(sems[turn.slot(lag)], turn.lap(lag) * per)


def part_wait(eng, passed):
    eng.sem_inc(passed, 1)


def build(nc, a, out):
    NP = a["x"].shape[0]
    N = a["nodes"]
    NT = NP // TILE
    EP = a["dst_flat"].shape[0]
    EU = EP // UNIT
    EC = EP // P
    PADROWS = NP - N

    def dram(name, shape, dt=F32):
        return nc.dram_tensor(name, shape, dt, kind="Internal").ap()

    z_rows = dram("z_rows", (NP, D))
    x_ends = dram("x_ends", (EU, P, 2 * GROUPS * D))
    y_rows = dram("y_rows", (NP, D))
    y_ends = dram("y_ends", (EU, P, 2 * GROUPS * D))
    o_rows = dram("o_rows", (EU, P, GROUPS * D))
    reset_d = dram("reset_d", (EP,))
    same_d = dram("same_d", (EP,))
    ends_d = dram("ends_d", (P, EU, GROUPS))
    sidx_d = dram("sidx_d", (P, EU, GROUPS), I32)

    def tiles(t):
        return t.rearrange("(t p j) d -> t p (j d)", p=P, j=ROWS)

    stage_sems = []
    with ExitStack() as top:
        def sb(ctx, name, shape, dt=F32):
            return ctx.enter_context(nc.sbuf_tensor(name, shape, dt))

        def sem(ctx, name):
            handle = nc.alloc_semaphore(name=name)
            if ctx is not top:
                stage_sems.append(handle)
            return handle

        def sems(ctx, name, n=RING):
            return [sem(ctx, f"{name}{i}") for i in range(n)]

        def end_stage():
            nc.clear_and_free_semaphores(stage_sems)
            stage_sems.clear()
            nc.all_engine_barrier()

        ps = [top.enter_context(nc.psum_tensor(f"ps{i}", [P, 512], F32)) for i in range(8)]
        sum_z, sum_zz = ps[6], ps[7]

        ident = sb(top, "ident", [P, P])
        ones = sb(top, "ones", [P, P])
        sel = sb(top, "sel", [P, 2, P])
        pads = sb(top, "pads", [P, 1])
        epsc = sb(top, "epsc", [P, 1])
        consts_loaded = sem(top, "consts_loaded")
        eps_set = sem(top, "eps_set")
        passed_pool = sem(top, "passed_pool")

        with ExitStack() as c:
            class Rows:

                def __init__(self, kind):
                    self.X = sb(c, "X1_" + kind, [P, RING, ROWS, D])
                    self.xc = sb(c, "xc1_" + kind, [P, 2, ROWS, D])
                    self.sq = sb(c, "sq1_" + kind, [P, 2, ROWS, D])
                    self.s1 = sb(c, "s11_" + kind, [P, RING, ROWS])
                    self.vs = sb(c, "vs1_" + kind, [P, RING, ROWS])
                    self.lnv = sb(c, "lnv1_" + kind, [P, RING, ROWS])
                    self.rstd = sb(c, "rstd1_" + kind, [P, RING, ROWS])
                    self.loaded = sems(c, "x_loaded1_" + kind)
                    self.s1_ready = sem(c, "s1_ready1_" + kind)
                    self.xc_ready = sem(c, "xc_ready1_" + kind)
                    self.sq_ready = sem(c, "sq_ready1_" + kind)
                    self.vs_ready = sem(c, "vs_ready1_" + kind)
                    self.ln_ready = sem(c, "ln_ready1_" + kind)
                    self.rstd_ready = sem(c, "rstd_ready1_" + kind)
                    self.h_ready = sem(c, "h_ready1_" + kind)

            n_, e_ = Rows("nodes"), Rows("edges")
            dst_f = sb(c, "dst_f", [P, EC], I32)
            prev_f = sb(c, "prev_f", [P, EC], I32)
            dst_g = sb(c, "dst_g", [P, EC], I32)
            next_g = sb(c, "next_g", [P, EC], I32)
            same = sb(c, "same", [P, EC])
            reset = sb(c, "reset", [P, EC])
            ends = sb(c, "ends", [P, EC])
            shifted = sb(c, "shifted", [P, EC])
            sidx = sb(c, "sidx", [P, EC], I32)
            hn = sb(c, "hn", [P, RING, ROWS, D])
            hh = sb(c, "hh", [P, 2, ROWS, D])
            wlr = sb(c, "wlr", [P, 2 * P])
            attc = sb(c, "attc", [P, 2, HEADS])
            bpre = sb(c, "bpre", [P, 2, 2])
            bsum = sb(c, "bsum", [P, 2])
            wfin = sb(c, "wfin", [P, 2, D])
            wfq = sb(c, "wfq", [P, 2, D])
            blh = sb(c, "blh", [HEADS, D])
            quarter = sb(c, "quarter", [HEADS, P])
            cb = sb(c, "cb", [P, D])
            gidx = sb(c, "gidx", [P, RING, 2 * GROUPS], I32)
            G = sb(c, "G", [P, RING, 1 + 2 * GROUPS, D])
            rs = sb(c, "rs", [HEADS, RING, UNIT])
            endf = sb(c, "endf", [P, RING, GROUPS])
            Gr = sb(c, "Gr1", [P, RING, 2 * GROUPS, D])
            Os = sb(c, "Os1", [P, RING, GROUPS, D])
            oidx = sb(c, "oidx", [P, RING, GROUPS], I32)
            HT = sb(c, "HT", [P, 2, UNIT])
            HH = sb(c, "HH", [P, RING, UNIT])
            LK = sb(c, "LK", [P, 2, 2, UNIT])
            att_lin = sb(c, "att_lin", [P, 2, HEADS])
            att_relu = sb(c, "att_relu", [P, 2, HEADS])
            wlrT = sb(c, "wlrT", [P, 2, P])
            wlin = sb(c, "wlin", [P, HEADS])
            blin = sb(c, "blin", [P, HEADS])
            ones_rows = sb(c, "ones_rows", [P, UNIT])
            M = sb(c, "M", [HEADS, 1 + RING * UNIT])
            TT = sb(c, "TT", [HEADS, 2, 2, UNIT])
            TA = sb(c, "TA", [HEADS, 2, UNIT])
            RW = sb(c, "RW", [HEADS, 2, 2, UNIT])
            DEN = sb(c, "DEN", [HEADS, 2, UNIT])
            LD = sb(c, "LD", [HEADS, 2, UNIT])
            RC = sb(c, "RC", [HEADS, 2, UNIT])
            B = sb(c, "B", [P, 2, UNIT])
            KEEP = sb(c, "KEEP", [P, 2, 2, UNIT])
            PR = sb(c, "PR", [P, 2, 2, UNIT])
            GM = sb(c, "GM", [P, RING, 2, UNIT])
            AB = sb(c, "AB", [P, RING, GROUPS, D])
            Z = sb(c, "Z", [P, RING, GROUPS, D])
            ZH = sb(c, "ZH", [P, 2, GROUPS, D])
            QD = sb(c, "QD", [P, RING, GROUPS, D])
            pT, pS, pB, pA = ps[0:2], ps[2], ps[3:5], ps[5]

            w_loaded = sem(c, "w_loaded")
            att_zeroed = sem(c, "att_zeroed")
            w_ready = sem(c, "w_ready")
            cb_ready = sem(c, "cb_ready")
            lin_ready = sem(c, "lin_ready")
            lin_out = sem(c, "lin_out")
            gidx_loaded = sems(c, "gidx_loaded")
            reset_loaded = sems(c, "reset_loaded")
            ends_loaded = sems(c, "ends_loaded")
            gathered = sems(c, "gathered")
            spilled = sems(c, "spilled1")
            z_stored = sems(c, "z_stored")
            os_loaded = sems(c, "os_loaded1")
            scattered = sems(c, "scattered")
            turned = sem(c, "turned")
            turned_taken = sem(c, "turned_taken")
            pre_ready = sem(c, "pre_ready")
            relu_ready = sem(c, "relu_ready")
            score_ready = sem(c, "score_ready")
            m_carried = sem(c, "m_carried")
            m_ready = sem(c, "m_ready")
            ta_ready = sem(c, "ta_ready")
            tt_ready = sem(c, "tt_ready")
            rw_ready = sem(c, "rw_ready")
            den_ready = sem(c, "den_ready")
            ld_ready = sem(c, "ld_ready")
            rc_ready = sem(c, "rc_ready")
            b_ready = sem(c, "b_ready")
            share_spread = sem(c, "share_spread")
            keep_ready = sem(c, "keep_ready")
            pr_ready = sem(c, "pr_ready")
            gm_ready = sem(c, "gm_ready")
            att_out = sem(c, "att_out")
            ab_ready = sem(c, "ab_ready")
            z_ready = sem(c, "z_ready")
            zh_ready = sem(c, "zh_ready")
            qd_ready = sem(c, "qd_ready")
            z_summed = sem(c, "z_summed")
            lists_loaded = sem(c, "lists_loaded")
            lists_made = sem(c, "lists_made")
            shifted_ready = sem(c, "shifted_ready")
            lists_stored = sem(c, "lists_stored")
            h_stored = sems(c, "h_stored")
            hh_ready = sem(c, "hh_ready")
            h_summed = sem(c, "h_summed")
            block = c.enter_context(nc.Block())
            DEPTH = 8
            NW = 2 + HEADS + 2 + 2 + 1

            def row_sums(eng, t, b):
                await_slot(eng, b.loaded, t, 2)
                eng.tensor_reduce(b.s1[:, t.slot(2)], b.X[:, t.slot(2)], AXX, ALU.add).then_inc(b.s1_ready, 1)

            def center(eng, t, b):
                await_unit(eng, b.s1_ready, t, 2)
                await_free(eng, b.h_ready, t, 2, 2)
                await_free(eng, b.sq_ready, t, 2, 2)
                eng.scalar_tensor_tensor(
                    out=b.xc[:, t.slot(2, 2)], in0=b.s1[:, t.slot(2)].unsqueeze(2).to_broadcast([P, ROWS, D]),
                    scalar=-1.0 / D, in1=b.X[:, t.slot(2)], op0=ALU.mult, op1=ALU.add).then_inc(b.xc_ready, 1)

            def sum_squares(eng, t, b):
                await_unit(eng, b.sq_ready, t, 3)
                await_free(eng, b.ln_ready, t, 3)
                eng.tensor_reduce(b.vs[:, t.slot(3)], b.sq[:, t.slot(3, 2)], AXX, ALU.add).then_inc(b.vs_ready, 1)

            def scale(eng, t, b, rows):
                await_unit(eng, b.rstd_ready, t, 3)
                await_unit(eng, b.xc_ready, t, 3)
                eng.scalar_tensor_tensor(
                    out=rows, in0=b.xc[:, t.slot(3, 2)], scalar=0.0,
                    in1=b.rstd[:, t.slot(3)].unsqueeze(2).to_broadcast([P, ROWS, D]),
                    op0=ALU.max, op1=ALU.mult).then_inc(b.h_ready, 1)

            def square(eng, t, b):
                await_unit(eng, b.xc_ready, t, 2)
                await_free(eng, b.vs_ready, t, 2, 2)
                eng.activation(b.sq[:, t.slot(2, 2)], b.xc[:, t.slot(2, 2)], ACT.Square).then_inc(b.sq_ready, 1)

            def deviation(eng, t, b):
                await_unit(eng, b.vs_ready, t, 3)
                await_free(eng, b.rstd_ready, t, 3)
                eng.activation(b.lnv[:, t.slot(3)], b.vs[:, t.slot(3)], ACT.Ln,
                               bias=epsc[:, :], scale=1.0 / D).then_inc(b.ln_ready, 1)
                await_unit(eng, b.ln_ready, t, 3)
                await_free(eng, b.h_ready, t, 3)
                eng.activation(b.rstd[:, t.slot(3)], b.lnv[:, t.slot(3)], ACT.Exp,
                               scale=-0.5).then_inc(b.rstd_ready, 1)

            @block.sync
            def _(eng):
                for dst, src in ((dst_f, a["dst_flat"]), (prev_f, a["prev_flat"])):
                    eng.dma_start(dst[:, :], src.rearrange("(p c) -> p c", p=P)).then_inc(lists_loaded, 16)
                for dst, src in ((dst_g, a["dst_groups"]), (next_g, a["next_groups"])):
                    eng.dma_start(dst[:, :], src).then_inc(lists_loaded, 16)
                for dst, src in ((ident, a["ident"]), (ones, a["ones"]), (sel, a["sel"]), (pads, a["pads"])):
                    eng.dma_start(dst[:], src).then_inc(consts_loaded, 16)
                eng.wait_ge(att_zeroed, 1)
                eng.dma_start(wlr[0:D, :], a["L0_gnn_W_l"]).then_inc(w_loaded, 16)
                eng.dma_start(wlr[D:P, :], a["L0_gnn_W_r"]).then_inc(w_loaded, 16)
                for h in range(HEADS):
                    eng.dma_start(attc[(h % 2) * D:(h % 2) * D + D, h // 2, h:h + 1],
                                  a["L0_gnn_att"].rearrange("h (c o) -> h c o", o=1)[h]).then_inc(w_loaded, 16)
                for i, b in enumerate(("L0_gnn_b_l", "L0_gnn_b_r")):
                    eng.dma_start(bpre[:, i, :], a[b].rearrange("(k p) -> p k", p=P),
                                  allow_slow_non_contiguous=True).then_inc(w_loaded, 16)
                for h in range(2):
                    eng.dma_start(wfin[h * D:h * D + D, :, :],
                                  a["L0_gnn_W_l"].rearrange("f (k h c) -> h f k c", k=2, h=2)[h]
                                  ).then_inc(w_loaded, 16)
                eng.dma_start(blh[:, :], a["L0_gnn_b_l"].rearrange("(h c) -> h c", h=HEADS)).then_inc(w_loaded, 16)

                eng.wait_ge(lists_made, 4)
                eng.dma_start(reset_d.rearrange("(p c) -> p c", p=P), reset[:, :]).then_inc(lists_stored, 16)
                eng.dma_start(same_d.rearrange("(p c) -> p c", p=P), same[:, :]).then_inc(lists_stored, 16)
                eng.dma_start(ends_d.rearrange("p u g -> p (u g)"), ends[:, :]).then_inc(lists_stored, 16)
                eng.dma_start(sidx_d.rearrange("p u g -> p (u g)"), sidx[:, :]).then_inc(lists_stored, 16)

                def gathers(t):
                    if t.has(0, EU):
                        await_slot_free(eng, gathered, t, 0, 16 * 2 * GROUPS)
                        eng.dma_start(gidx[:, t.slot()], a["gather_rows"][t.unit()]
                                      ).then_inc(gidx_loaded[t.slot()], 16)
                    if t.has(1, EU):
                        await_slot(eng, gathered, t, 1, 16 * 2 * GROUPS)
                        eng.dma_start(x_ends[t.unit(1)], Gr[:, t.slot(1)].rearrange("p k d -> p (k d)")
                                      ).then_inc(spilled[t.slot(1)], 16)

                def scatters(t):
                    if t.has(0, EU):
                        await_slot(eng, z_stored, t, 0)
                        await_slot_free(eng, scattered, t, 0, 16 * GROUPS)
                        eng.dma_start(Os[:, t.slot()].rearrange("p g d -> p (g d)"),
                                      o_rows[t.unit()]).then_inc(os_loaded[t.slot()], 16)
                        eng.dma_start(oidx[:, t.slot()], sidx_d[:, t.unit()]).then_inc(os_loaded[t.slot()], 16)

                pipeline(eng, EU, 1, gathers)
                eng.wait_ge(lists_stored, 64)
                pipeline(eng, EU, 0, scatters)

            @block.gpsimd
            def _(eng):
                last_row = eng.to_reg(N - 1)
                last_any = eng.to_reg(NP - 1)

                def gather(t):
                    if t.has(0, EU):
                        await_slot(eng, gidx_loaded, t, 0)
                        await_slot_free(eng, spilled, t, 0)
                        part_wait(eng, passed_pool)
                        for g in range(GROUPS):
                            for side in range(2):
                                k = side * GROUPS + g
                                eng.indirect_dma_start(
                                    out=Gr[:, t.slot(), 2 * g + side, :], out_offset=None, in_=a["x"],
                                    in_offset=bass.IndirectOffsetOnAxis(ap=gidx[:, t.slot(), k:k + 1], axis=0),
                                    bounds_check=last_any).then_inc(gathered[t.slot()], 16)

                def scatter(t):
                    if t.has(0, EU):
                        await_slot(eng, os_loaded, t, 0, 32)
                        part_wait(eng, passed_pool)
                        for g in range(GROUPS):
                            eng.indirect_dma_start(
                                out=z_rows, out_offset=bass.IndirectOffsetOnAxis(
                                    ap=oidx[:, t.slot(), g:g + 1], axis=0),
                                in_=Os[:, t.slot(), g, :], in_offset=None, bounds_check=last_row,
                                oob_is_err=False).then_inc(scattered[t.slot()], 16)

                pipeline(eng, EU, 0, gather)
                for s in range(RING):
                    eng.wait_ge(h_stored[s], 16 * len(range(s, NT, RING)))
                pipeline(eng, EU, 0, scatter)
                for s in range(RING):
                    eng.wait_ge(scattered[s], 16 * GROUPS * len(range(s, EU, RING)))

            @block.tensor
            def _(eng):
                eng.wait_ge(consts_loaded, 64)

                def nodes(t):
                    if t.has(5, NT):
                        await_unit(eng, hh_ready, t, 5)
                        eng.matmul(sum_z[0:1, :], ones[:, 0:1], hn[:, t.slot(5)].rearrange("p j d -> p (j d)"),
                                   start=t.first(5), stop=False, skip_group_check=True)
                        eng.matmul(sum_zz[0:1, :], ones[:, 0:1], hh[:, t.slot(5, 2)].rearrange("p j d -> p (j d)"),
                                   start=t.first(5), stop=False, skip_group_check=True).then_inc(h_summed, 1)

                pipeline(eng, NT, 5, nodes)
                eng.wait_ge(w_ready, 10)
                eng.matmul(pA[:, 0:D], quarter[:, :], blh[:, :], start=True, stop=True)
                for k in range(2):
                    mm = eng.transpose(pT[0][:, k * P:k * P + P], wlr[:, k * P:k * P + P], ident[:, :])
                mm.then_inc(cb_ready, 1)
                eng.wait_ge(lin_ready, 1)
                for k in range(2):
                    eng.matmul(pT[1][:, 0:HEADS], wlrT[:, k], att_lin[:, k], start=(k == 0), stop=(k == 1))
                for k in range(2):
                    mm = eng.matmul(pT[1][0:1, HEADS:2 * HEADS], bsum[:, k:k + 1], att_lin[:, k],
                                    start=(k == 0), stop=(k == 1))
                mm.then_inc(lin_out, 1)

                def edges(t):
                    if t.has(6, EU):
                        await_unit(eng, b_ready, t, 6)
                        await_free(eng, pr_ready, t, 6, 1, 2)
                        await_free(eng, keep_ready, t, 6, 1, 2)
                        for k in range(2):
                            eng.matmul(pB[k][:, :], sel[:, k, :], B[:, t.slot(6, 2)],
                                       start=True, stop=True).then_inc(share_spread, 1)
                    if t.has(4, EU):
                        await_unit(eng, e_.h_ready, t, 4)
                        await_free(eng, relu_ready, t, 4, 1, 2)
                        for g in range(GROUPS):
                            mm = eng.transpose(pT[0][:, g * P:g * P + P],
                                               G[:, t.slot(4), 1 + 2 * g:3 + 2 * g].rearrange("p s d -> p (s d)"),
                                               ident[:, :])
                        for g in range(GROUPS):
                            mm = eng.transpose(pT[1][:, g * P:g * P + P],
                                               G[:, t.slot(4), 2 * g:2 + 2 * g].rearrange("p s d -> p (s d)"),
                                               ident[:, :])
                        mm.then_inc(turned, 1)
                    if t.has(7, EU):
                        await_unit(eng, gm_ready, t, 7, 2)
                        await_free(eng, ab_ready, t, 7, 1)
                        for g in range(GROUPS):
                            for k in range(2):
                                mm = eng.matmul(pA[:, g * D:g * D + D], GM[:, t.slot(7), k, g * P:g * P + P],
                                                wfq[:, k, :], start=(k == 0), stop=(k == 1))
                        mm.then_inc(att_out, 1)
                    if t.has(8, EU):
                        await_unit(eng, qd_ready, t, 8)
                        await_slot(eng, ends_loaded, t, 8)
                        for g in range(GROUPS):
                            for acc, rows in ((sum_z, AB), (sum_zz, QD)):
                                mm = eng.matmul(acc[0:1, 0:D], endf[:, t.slot(8), g:g + 1], rows[:, t.slot(8), g],
                                                start=False, stop=False, skip_group_check=True)
                        mm.then_inc(z_summed, 1)
                    if t.has(4, EU):
                        await_unit(eng, turned_taken, t, 4, 3)
                        for k in range(2):
                            eng.matmul(pT[k][:, :], wlr[:, k * P:k * P + P], HT[:, t.slot(4, 2)],
                                       start=True, stop=True).then_inc(pre_ready, 1)
                        await_free(eng, tt_ready, t, 4, 1)
                        eng.matmul(pS[0:HEADS, :], wlin[:, :], HT[:, t.slot(4, 2)], start=True, stop=False)
                        eng.matmul(pS[0:HEADS, :], blin[:, :], ones_rows[:, :], start=False, stop=False)
                        await_unit(eng, relu_ready, t, 4, 2)
                        for k in range(2):
                            mm = eng.matmul(pS[0:HEADS, :], att_relu[:, k, :], LK[:, t.slot(4, 2), k],
                                            start=False, stop=(k == 1))
                        mm.then_inc(score_ready, 1)

                eng.wait_ge(lin_ready, 2)
                pipeline(eng, EU, DEPTH, edges)

            @block.scalar
            def _(eng):
                eng.preload_act_table_set("natural_log_exp_and_others")

                def nodes(t):
                    if t.has(0, NT):
                        await_free(eng, n_.xc_ready, t, 0)
                        eng.dma_start(n_.X[:, t.slot()].rearrange("p j d -> p (j d)"),
                                      tiles(a["x"])[t.unit()]).then_inc(n_.loaded[t.slot()], 16)
                    if t.has(3, NT):
                        deviation(eng, t, n_)
                    if t.has(2, NT):
                        square(eng, t, n_)
                    if t.has(4, NT):
                        await_unit(eng, n_.h_ready, t, 4)
                        await_free(eng, h_summed, t, 4, 2)
                        eng.activation(hh[:, t.slot(4, 2)], hn[:, t.slot(4)], ACT.Square).then_inc(hh_ready, 1)
                        eng.dma_start(tiles(z_rows)[t.unit(4)], hn[:, t.slot(4)].rearrange("p j d -> p (j d)")
                                      ).then_inc(h_stored[t.slot(4)], 16)

                eng.wait_ge(eps_set, 1)
                pipeline(eng, NT, 5, nodes)
                eng.wait_ge(lists_stored, 64)

                def edges(t):
                    if t.has(0, EU):
                        await_slot(eng, spilled, t, 0)
                        await_free(eng, e_.xc_ready, t, 0)
                        eng.dma_start(e_.X[:, t.slot()].rearrange("p j d -> p (j d)"),
                                      x_ends[t.unit()]).then_inc(e_.loaded[t.slot()], 16)
                    if t.has(3, EU):
                        await_free(eng, ta_ready, t, 3)
                        eng.dma_start(rs[:, t.slot(3)],
                                      reset_d.rearrange("(u o e) -> u o e", o=1, e=UNIT)[t.unit(3)]
                                      .to_broadcast([HEADS, UNIT])).then_inc(reset_loaded[t.slot(3)], 16)
                    if t.has(6, EU):
                        await_free(eng, z_summed, t, 6)
                        eng.dma_start(endf[:, t.slot(6)], ends_d[:, t.unit(6)]).then_inc(ends_loaded[t.slot(6)], 16)

                    if t.has(4, EU):
                        await_unit(eng, turned, t, 4)
                        await_free(eng, score_ready, t, 4, 2)
                        await_free(eng, pr_ready, t, 4, RING, 2)
                        eng.activation(HT[:, t.slot(4, 2)], pT[0][:, :], ACT.Copy).then_inc(turned_taken, 1)
                        eng.activation(HH[0:D, t.slot(4)], pT[0][0:D, :], ACT.Copy).then_inc(turned_taken, 1)
                        eng.activation(HH[D:P, t.slot(4)], pT[1][D:P, :], ACT.Copy).then_inc(turned_taken, 1)
                    if t.has(3, EU):
                        deviation(eng, t, e_)
                    if t.has(5, EU):
                        await_unit(eng, tt_ready, t, 5)
                        await_free(eng, b_ready, t, 5, 2)
                        eng.activation(RW[:, t.slot(5, 2)], TT[:, t.slot(5, 2)], ACT.Exp).then_inc(rw_ready, 1)
                    if t.has(6, EU):
                        await_free(eng, gm_ready, t, 6, 2, 2)
                        for k in range(2):
                            eng.wait_ge(pr_ready, t.unit(6) * 2 + (k + 1))
                            eng.activation(KEEP[:, t.slot(6, 2), k], pB[k][:, :], ACT.Copy, bias=1.0,
                                           scale=-1.0).then_inc(keep_ready, 1)
                    if t.has(4, EU):
                        await_unit(eng, pre_ready, t, 4, 2)
                        for k in range(2):
                            eng.activation(LK[:, t.slot(4, 2), k], pT[k][:, :], ACT.Relu, bias=bsum[:, k:k + 1],
                                           scale=1.0).then_inc(relu_ready, 1)
                    if t.has(5, EU):
                        await_unit(eng, den_ready, t, 5)
                        await_free(eng, rc_ready, t, 5, 2)
                        eng.activation(LD[:, t.slot(5, 2)], DEN[:, t.slot(5, 2)], ACT.Ln).then_inc(ld_ready, 1)
                        await_unit(eng, ld_ready, t, 5)
                        await_free(eng, b_ready, t, 5, 2)
                        eng.activation(RC[:, t.slot(5, 2)], LD[:, t.slot(5, 2)], ACT.Exp, scale=-1.0
                                       ).then_inc(rc_ready, 1)
                    if t.has(2, EU):
                        square(eng, t, e_)
                    if t.has(8, EU):
                        await_unit(eng, z_ready, t, 8)
                        eng.dma_start(o_rows[t.unit(8)], Z[:, t.slot(8)].rearrange("p g d -> p (g d)")
                                      ).then_inc(z_stored[t.slot(8)], 16)

                pipeline(eng, EU, DEPTH, edges)
                for s in range(RING):
                    eng.wait_ge(z_stored[s], 16 * len(range(s, EU, RING)))

            @block.vector
            def _(eng):
                eng.memset(attc[:, :, :], 0.0).then_inc(att_zeroed, 1)
                eng.memset(epsc[:, :], EPS).then_inc(eps_set, 1)
                eng.wait_ge(lists_loaded, 64)
                eng.tensor_tensor(same[:, :], dst_f[:, :], prev_f[:, :], ALU.is_equal).then_inc(lists_made, 1)
                eng.tensor_tensor(ends[:, :], dst_g[:, :], next_g[:, :], ALU.not_equal).then_inc(lists_made, 1)
                eng.tensor_scalar(shifted[:, :], dst_g[:, :], -FAR, None, ALU.add).then_inc(lists_made, 1)
                eng.wait_ge(lists_made, 3)
                eng.tensor_scalar(reset[:, :], same[:, :], -1.0, RESET, ALU.add, ALU.mult)
                eng.tensor_tensor(shifted[:, :], shifted[:, :], ends[:, :], ALU.mult).then_inc(shifted_ready, 1)
                eng.wait_ge(shifted_ready, 1)
                eng.tensor_scalar(sidx[:, :], shifted[:, :], FAR, None, ALU.add).then_inc(lists_made, 1)
                eng.memset(quarter[:, :], 1.0 / HEADS).then_inc(w_ready, 1)
                eng.memset(M[:, 0:1], 0.0).then_inc(w_ready, 1)
                eng.memset(G[:, :, 0], 0.0).then_inc(w_ready, 1)
                eng.memset(ones_rows[:, :], 1.0).then_inc(w_ready, 1)
                eng.memset(blin[:, :], 0.0).then_inc(w_ready, 1)
                eng.memset(B[:, :, :], 0.0).then_inc(w_ready, 1)

                def nodes(t):
                    if t.has(2, NT):
                        row_sums(eng, t, n_)
                    if t.has(3, NT):
                        sum_squares(eng, t, n_)
                    if t.has(2, NT):
                        center(eng, t, n_)
                    if t.has(3, NT):
                        await_free(eng, h_summed, t, 3)
                        await_slot_free(eng, h_stored, t, 3)
                        scale(eng, t, n_, hn[:, t.slot(3)])

                pipeline(eng, NT, 5, nodes)
                eng.wait_ge(w_loaded, 16 * NW)
                eng.tensor_tensor(bsum[:, :], bpre[:, 0], bpre[:, 1], ALU.add).then_inc(w_ready, 1)
                eng.tensor_scalar(wfq[:, :, :], wfin[:, :, :], 1.0 / HEADS, None, ALU.mult).then_inc(w_ready, 1)
                eng.tensor_scalar(att_lin[:, :, :], attc[:, :, :], NEG_SLOPE, None, ALU.mult).then_inc(w_ready, 1)
                eng.tensor_scalar(att_relu[:, :, :], attc[:, :, :], 1.0 - NEG_SLOPE, None, ALU.mult).then_inc(w_ready, 1)
                eng.wait_ge(cb_ready, 1)
                eng.tensor_copy(cb[:, :], pA[:, 0:D])
                eng.tensor_copy(wlrT[:, :, :], pT[0][:, 0:2 * P].rearrange("p (k f) -> p k f", k=2)
                                ).then_inc(lin_ready, 1)
                eng.wait_ge(lin_out, 1)
                eng.wait_ge(w_ready, 10)
                eng.tensor_copy(wlin[:, :], pT[1][:, 0:HEADS])
                eng.tensor_copy(blin[0:1, :], pT[1][0:1, HEADS:2 * HEADS]).then_inc(lin_ready, 1)

                def running_mean(t, k):
                    s = t.slot(6)
                    await_unit(eng, pr_ready, t, 6, 2)
                    await_unit(eng, keep_ready, t, 6, 2)
                    await_free(eng, att_out, t, 6)
                    if not t.first(6):
                        await_unit(eng, gm_ready, t, 7, 2)
                    eng.tensor_tensor_scan(
                        GM[:, s, k], KEEP[:, t.slot(6, 2), k], PR[:, t.slot(6, 2), k],
                        0.0 if t.first(6) else GM[:, (s - 1) % RING, k, UNIT - 1:UNIT],
                        ALU.mult, ALU.add).then_inc(gm_ready, 1)

                def edges(t):
                    if t.has(5, EU):
                        s = t.slot(5)
                        lo, hi = 1 + s * UNIT, 1 + (s + 1) * UNIT
                        if s == 0 and not t.first(5):
                            await_unit(eng, m_ready, t, 6)
                            await_unit(eng, tt_ready, t, 6)
                            eng.tensor_copy(M[:, 0:1], M[:, RING * UNIT:RING * UNIT + 1]).then_inc(m_carried, 1)
                            eng.wait_ge(m_carried, t.lap(5))
                        elif not t.first(5):
                            await_unit(eng, m_ready, t, 6)
                        await_unit(eng, score_ready, t, 5)
                        await_slot(eng, reset_loaded, t, 5)
                        eng.tensor_tensor_scan(M[:, lo:hi], rs[:, s], pS[0:HEADS, :], M[:, lo - 1:lo],
                                               ALU.add, ALU.max).then_inc(m_ready, 1)
                    if t.has(3, EU):
                        sum_squares(eng, t, e_)
                    if t.has(5, EU):
                        s, s2 = t.slot(5), t.slot(5, 2)
                        lo, hi = 1 + s * UNIT, 1 + (s + 1) * UNIT
                        await_unit(eng, m_ready, t, 5)
                        await_free(eng, tt_ready, t, 5, 2)
                        eng.tensor_tensor(TA[:, s2], M[:, lo - 1:hi - 1], rs[:, s], ALU.add).then_inc(ta_ready, 1)
                    if t.has(5, EU):
                        s2 = t.slot(5, 2)
                        lo, hi = 1 + t.slot(5) * UNIT, 1 + (t.slot(5) + 1) * UNIT
                        await_free(eng, rw_ready, t, 5, 2)
                        eng.tensor_tensor(TT[:, s2, 1], pS[0:HEADS, :], M[:, lo:hi], ALU.subtract)
                        await_unit(eng, ta_ready, t, 5)
                        eng.tensor_tensor(TT[:, s2, 0], TA[:, s2], M[:, lo:hi], ALU.subtract).then_inc(tt_ready, 1)
                    if t.has(2, EU):
                        row_sums(eng, t, e_)
                    if t.has(6, EU):
                        await_unit(eng, turned_taken, t, 6, 3)
                        await_unit(eng, share_spread, t, 6, 2)
                        await_free(eng, gm_ready, t, 6, 2, 2)
                        for k in range(2):
                            eng.tensor_tensor(PR[:, t.slot(6, 2), k], pB[k][:, :], HH[:, t.slot(6)],
                                              ALU.mult).then_inc(pr_ready, 1)
                    if t.has(7, EU):
                        s = t.slot(7)
                        await_unit(eng, att_out, t, 7)
                        await_free(eng, z_summed, t, 7)
                        eng.tensor_tensor(AB[:, s], pA[:, 0:GROUPS * D].rearrange("p (g d) -> p g d", g=GROUPS),
                                          cb[:, :].unsqueeze(1).to_broadcast([P, GROUPS, D]),
                                          ALU.add).then_inc(ab_ready, 1)
                    if t.has(2, EU):
                        center(eng, t, e_)
                    if t.has(7, EU):
                        s = t.slot(7)
                        await_unit(eng, ab_ready, t, 7)
                        await_slot_free(eng, z_stored, t, 7)
                        eng.tensor_tensor(Z[:, s], AB[:, s], G[:, s, 2::2, :], ALU.add).then_inc(z_ready, 1)
                    if t.has(5, EU):
                        s, s2 = t.slot(5), t.slot(5, 2)
                        await_unit(eng, rw_ready, t, 5)
                        if not t.first(5):
                            await_unit(eng, den_ready, t, 6)
                        await_free(eng, ld_ready, t, 5, 2)
                        eng.tensor_tensor_scan(DEN[:, s2], RW[:, s2, 0], RW[:, s2, 1],
                                               0.0 if t.first(5) else DEN[:, (s2 - 1) % 2, UNIT - 1:UNIT],
                                               ALU.mult, ALU.add).then_inc(den_ready, 1)
                    if t.has(7, EU):
                        s = t.slot(7)
                        await_unit(eng, z_ready, t, 7)
                        await_free(eng, qd_ready, t, 7, 2)
                        eng.tensor_tensor(ZH[:, t.slot(7, 2)], Z[:, s], G[:, s, 2:2 * GROUPS + 1:2, :],
                                          ALU.add).then_inc(zh_ready, 1)
                    if t.has(6, EU):
                        running_mean(t, 0)
                    if t.has(7, EU):
                        s = t.slot(7)
                        await_unit(eng, zh_ready, t, 7)
                        eng.tensor_tensor(QD[:, s], ZH[:, t.slot(7, 2)], AB[:, s], ALU.mult).then_inc(qd_ready, 1)
                    if t.has(6, EU):
                        running_mean(t, 1)
                    if t.has(5, EU):
                        s2 = t.slot(5, 2)
                        await_unit(eng, rc_ready, t, 5)
                        await_free(eng, share_spread, t, 5, 2, 2)
                        eng.scalar_tensor_tensor(out=B[0:HEADS, s2], in0=RC[:, s2], scalar=1e16,
                                                 in1=RW[:, s2, 1], op0=ALU.min, op1=ALU.mult).then_inc(b_ready, 1)
                    if t.has(3, EU):
                        await_free(eng, turned, t, 3)
                        await_free(eng, zh_ready, t, 3)
                        scale(eng, t, e_, G[:, t.slot(3), 1:, :])

                pipeline(eng, EU, DEPTH, edges)

        end_stage()

        sc2b = sb(top, "sc2b", [P, D])
        sh2b = sb(top, "sh2b", [P, D])
        st = sb(top, "st", [1, 10, D])
        vec2 = sb(top, "vec2", [1, 3, D])
        off2 = sb(top, "off2", [1, D])
        sum_y, sum_yy = ps[0], ps[1]

        def fold(link, eng, s, sums, squares):
            mean, ms, m2, var = s[:, 0], s[:, 1], s[:, 2], s[:, 3]
            link(eng.tensor_reduce(mean, sums[0:1, :].rearrange("o (j d) -> o d j", j=ROWS), AXX, ALU.add))
            link(eng.tensor_reduce(ms, squares[0:1, :].rearrange("o (j d) -> o d j", j=ROWS), AXX, ALU.add))
            link(eng.tensor_scalar(mean, mean, 1.0 / N, None, ALU.mult))
            link(eng.tensor_scalar(ms, ms, 1.0 / N, None, ALU.mult))
            link(eng.tensor_tensor(m2, mean, mean, ALU.mult))
            link(eng.tensor_tensor(var, ms, m2, ALU.subtract))

        def fold_shift(link, eng, s, rstd, gamma, beta, bias, scale, shift):
            mean, mu, off, prod = s[:, 0], s[:, 4], s[:, 5], s[:, 6]
            link(eng.tensor_tensor(scale, rstd, gamma, ALU.mult))
            link(eng.tensor_tensor(mu, mean, bias, ALU.add))
            link(eng.tensor_tensor(off, bias, mu, ALU.subtract))
            link(eng.tensor_tensor(prod, off, scale, ALU.mult))
            link(eng.tensor_tensor(shift, prod, beta, ALU.add))

        with ExitStack() as c:
            vec1 = sb(c, "vec1", [1, 3, D])
            fold1 = sb(c, "fold1", [1, 2, 2, D])
            col1 = sb(c, "col1", [P, 2])
            sc1b = sb(c, "sc1b", [P, D])
            w1 = sb(c, "w1", [P, 2, 2 * P])
            b1c = sb(c, "b1c", [P, 2])
            w2 = sb(c, "w2", [P, 2, D])
            Zt = sb(c, "Zt", [P, RING, ROWS, D])
            XT = sb(c, "XT", [P, RING, 512])
            R = sb(c, "R", [P, 2, 2, 2, 512])
            ZS = sb(c, "ZS", [P, RING, ROWS, D])
            Y = sb(c, "Y", [P, RING, ROWS, D])
            YY = sb(c, "YY", [P, 2, ROWS, D])
            accy = sb(c, "accy", [P, ROWS, D])
            accyy = sb(c, "accyy", [P, ROWS, D])
            pT, pH, pY = ps[0:2], ps[2:6], ps[6:8]

            w_zeroed = sem(c, "w_zeroed3")
            w_loaded = sem(c, "w_loaded3")
            chain = sem(c, "chain")
            var_ready = sem(c, "var_ready")
            rstd_ready = sem(c, "rstd_ready3")
            folded = sem(c, "folded")
            turned_col = sem(c, "turned_col")
            col_ready = sem(c, "col_ready")
            z_loaded = sems(c, "z_loaded")
            y_stored = sems(c, "y_stored")
            turned = sem(c, "turned3")
            xt_ready = sem(c, "xt_ready")
            hid_ready = sem(c, "hid_ready")
            relu_a = sem(c, "relu_a")
            relu_v = sem(c, "relu_v")
            zs_ready = sem(c, "zs_ready")
            y_out = sem(c, "y_out")
            y_ready = sem(c, "y_ready")
            yy_ready = sem(c, "yy_ready")
            acc_zeroed = sem(c, "acc_zeroed")
            accy_ready = sem(c, "accy_ready")
            accyy_ready = sem(c, "accyy_ready")
            block = c.enter_context(nc.Block())
            DEPTH = 4
            links = [0]

            @block.sync
            def _(eng):
                for i, n in enumerate(("gamma1", "beta1", "bias_gat")):
                    eng.dma_start(vec1[:, i, :], a["L0_gnn_" + n].rearrange("(o d) -> o d", o=1)).then_inc(w_loaded, 16)
                for i, n in enumerate(("gamma2", "beta2", "b2")):
                    eng.dma_start(vec2[:, i, :], a["L0_gnn_" + n].rearrange("(o d) -> o d", o=1)).then_inc(w_loaded, 16)
                eng.wait_ge(w_zeroed, 1)
                for q in range(2):
                    eng.dma_start(w1[q * D:q * D + D, q, :], a["L0_gnn_W1"]).then_inc(w_loaded, 16)
                eng.dma_start(b1c[:, :], a["L0_gnn_b1"].rearrange("(k p) -> p k", p=P),
                              allow_slow_non_contiguous=True).then_inc(w_loaded, 16)
                eng.dma_start(w2[:, :, :], a["L0_gnn_W2"].rearrange("(k p) d -> p k d", p=P)).then_inc(w_loaded, 16)

                def step(t):
                    if t.has(0, NT):
                        await_free(eng, turned, t, 0)
                        await_free(eng, zs_ready, t, 0)
                        eng.dma_start(Zt[:, t.slot()].rearrange("p j d -> p (j d)"),
                                      tiles(z_rows)[t.unit()]).then_inc(z_loaded[t.slot()], 16)
                    if t.has(3, NT):
                        await_unit(eng, y_ready, t, 3)
                        eng.dma_start(tiles(y_rows)[t.unit(3)], Y[:, t.slot(3)].rearrange("p j d -> p (j d)")
                                      ).then_inc(y_stored[t.slot(3)], 16)

                pipeline(eng, NT, DEPTH, step)
                for s in range(RING):
                    eng.wait_ge(y_stored[s], 16 * len(range(s, NT, RING)))

            @block.scalar
            def _(eng):
                eng.wait_ge(var_ready, 1)
                eng.activation(st[:, 7], st[:, 3], ACT.Ln, bias=epsc[0:1, :]).then_inc(rstd_ready, 1)
                eng.wait_ge(rstd_ready, 1)
                eng.activation(st[:, 8], st[:, 7], ACT.Exp, scale=-0.5).then_inc(rstd_ready, 1)
                eng.wait_ge(col_ready, 1)

                def step(t):
                    if t.has(0, NT):
                        await_unit(eng, turned, t, 0)
                        await_free(eng, hid_ready, t, 0, RING, 4)
                        eng.activation(XT[:, t.slot()], pT[t.slot(0, 2)][:, :], ACT.Identity, bias=col1[:, 1:2],
                                       scale=col1[:, 0:1]).then_inc(xt_ready, 1)
                    if t.has(3, NT):
                        await_unit(eng, y_ready, t, 3)
                        await_free(eng, accyy_ready, t, 3, 2)
                        eng.activation(YY[:, t.slot(3, 2)], Y[:, t.slot(3)],
                                       ACT.Square).then_inc(yy_ready, 1)
                    if t.has(1, NT):
                        await_free(eng, y_out, t, 1, 2)
                        for k in range(2):
                            eng.wait_ge(hid_ready, t.unit(1) * 4 + (k + 1))
                            eng.activation(R[:, t.slot(1, 2), 0, k], pH[k][:, :], ACT.Relu,
                                           bias=b1c[:, k:k + 1]).then_inc(relu_a, 1)

                pipeline(eng, NT, DEPTH, step)

            @block.vector
            def _(eng):
                def link(ins):
                    links[0] += 1
                    ins.then_inc(chain, 1)
                    eng.wait_ge(chain, links[0])

                eng.memset(w1[:, :, :], 0.0).then_inc(w_zeroed, 1)
                eng.memset(accy[:, :, :], 0.0).then_inc(acc_zeroed, 1)
                eng.memset(accyy[:, :, :], 0.0).then_inc(acc_zeroed, 1)
                fold(link, eng, st, sum_z, sum_zz)
                eng.sem_inc(var_ready, 1)
                eng.wait_ge(rstd_ready, 2)
                eng.wait_ge(w_loaded, 16 * 10)
                fold_shift(link, eng, st, st[:, 8], vec1[:, 0], vec1[:, 1], vec1[:, 2], fold1[:, 0, 0], fold1[:, 1, 0])
                link(eng.tensor_copy(fold1[:, :, 1], fold1[:, :, 0]))
                link(eng.tensor_tensor(off2[:, :], vec2[:, 2], fold1[:, 1, 0], ALU.add))
                eng.sem_inc(folded, 1)
                eng.wait_ge(turned_col, 1)
                eng.tensor_copy(col1[:, :], pH[0][:, 0:2])
                eng.tensor_copy(sc1b[:, :], pH[1][:, 0:D]).then_inc(col_ready, 1)

                def step(t):
                    if t.has(2, NT):
                        await_unit(eng, y_out, t, 2)
                        await_unit(eng, zs_ready, t, 2)
                        await_free(eng, yy_ready, t, 2)
                        await_free(eng, accy_ready, t, 2)
                        await_slot_free(eng, y_stored, t, 2)
                        eng.tensor_tensor(Y[:, t.slot(2)], ZS[:, t.slot(2)],
                                          pY[t.slot(2, 2)][:, :].rearrange("p (j d) -> p j d", j=ROWS),
                                          ALU.add).then_inc(y_ready, 1)
                    if t.has(1, NT):
                        await_free(eng, y_out, t, 1, 2)
                        for k in range(2):
                            eng.wait_ge(hid_ready, t.unit(1) * 4 + (3 + k))
                            eng.tensor_scalar(R[:, t.slot(1, 2), 1, k], pH[2 + k][:, :], b1c[:, k:k + 1], 0.0,
                                              ALU.add, ALU.max).then_inc(relu_v, 1)

                pipeline(eng, NT, DEPTH, step)

            @block.gpsimd
            def _(eng):
                eng.wait_ge(col_ready, 1)

                def step(t):
                    if t.has(0, NT):
                        await_slot(eng, z_loaded, t, 0)
                        await_free(eng, y_ready, t, 0)
                        eng.tensor_tensor(ZS[:, t.slot()], Zt[:, t.slot()],
                                          sc1b[:, :].unsqueeze(1).to_broadcast([P, ROWS, D]),
                                          ALU.mult).then_inc(zs_ready, 1)
                    if t.has(4, NT):
                        await_unit(eng, y_ready, t, 4)
                        if t.first(4):
                            eng.wait_ge(acc_zeroed, 2)
                        else:
                            await_unit(eng, accy_ready, t, 5)
                        eng.tensor_tensor(accy[:, :, :], accy[:, :, :], Y[:, t.slot(4)],
                                          ALU.add).then_inc(accy_ready, 1)
                        await_unit(eng, yy_ready, t, 4)
                        if not t.first(4):
                            await_unit(eng, accyy_ready, t, 5)
                        eng.tensor_tensor(accyy[:, :, :], accyy[:, :, :], YY[:, t.slot(4, 2)],
                                          ALU.add).then_inc(accyy_ready, 1)

                pipeline(eng, NT, DEPTH, step)

            @block.tensor
            def _(eng):
                eng.wait_ge(folded, 1)
                for k in range(2):
                    eng.matmul(pH[0][:, k:k + 1], fold1[:, k].rearrange("o t d -> o (t d)"), ones[0:1, 0:1],
                               start=True, stop=True)
                eng.matmul(pH[1][:, 0:D], ones[0:1, :], fold1[:, 0, 0], start=True, stop=True
                           ).then_inc(turned_col, 1)
                eng.wait_ge(col_ready, 1)

                def step(t):
                    if t.has(0, NT):
                        await_slot(eng, z_loaded, t, 0)
                        await_free(eng, xt_ready, t, 0, 2)
                        for g in range(4):
                            mm = eng.transpose(pT[t.slot(0, 2)][:, g * P:g * P + P],
                                               Zt[:, t.slot(), 2 * g:2 * g + 2].rearrange("p j d -> p (j d)"),
                                               ident[:, :])
                        mm.then_inc(turned, 1)
                    if t.has(2, NT):
                        await_unit(eng, relu_a, t, 2, 2)
                        await_unit(eng, relu_v, t, 2, 2)
                        await_free(eng, y_ready, t, 2, 2)
                        o = pY[t.slot(2, 2)]
                        for g in range(4):
                            for q in range(2):
                                for k in range(2):
                                    mm = eng.matmul(o[:, (2 * g + q) * D:(2 * g + q + 1) * D],
                                                    R[:, t.slot(2, 2), q, k, g * P:g * P + P], w2[:, k, :],
                                                    start=(k == 0), stop=(k == 1))
                        mm.then_inc(y_out, 1)
                    if t.has(1, NT):
                        await_unit(eng, xt_ready, t, 1)
                        for q in range(2):
                            if q == 0:
                                await_free(eng, relu_a, t, 1, 1, 2)
                            else:
                                await_free(eng, relu_v, t, 1, 1, 2)
                            for k in range(2):
                                eng.matmul(pH[2 * q + k][:, :], w1[:, q, k * P:k * P + P],
                                           XT[:, t.slot(1)], start=True, stop=True).then_inc(hid_ready, 1)

                pipeline(eng, NT, DEPTH, step)
                eng.wait_ge(accy_ready, NT)
                eng.wait_ge(accyy_ready, NT)
                last = NT - 1
                eng.matmul(sum_y[0:1, :], ones[:, 0:1], accy[:, :, :].rearrange("p j d -> p (j d)"),
                           start=True, stop=False)
                eng.matmul(sum_y[0:1, :].rearrange("o (j d) -> o j d", j=ROWS), pads[:, :],
                           Y[:, last % RING], start=False, stop=True)
                eng.matmul(sum_yy[0:1, :], ones[:, 0:1], accyy[:, :, :].rearrange("p j d -> p (j d)"),
                           start=True, stop=False)
                eng.matmul(sum_yy[0:1, :], pads[:, :], YY[:, last % 2].rearrange("p j d -> p (j d)"),
                           start=False, stop=True)

        end_stage()

        with ExitStack() as c:
            class Rows:

                def __init__(self, kind):
                    self.X = sb(c, "X_" + kind, [P, RING, ROWS, D])
                    self.Y = sb(c, "Y_" + kind, [P, RING, ROWS, D])
                    self.v1 = sb(c, "v1_" + kind, [P, ROWS, D])
                    self.v2 = sb(c, "v2_" + kind, [P, ROWS, D])
                    self.xf = sb(c, "xf_" + kind, [P, RING, ROWS, D])
                    self.xc = sb(c, "xc_" + kind, [P, RING, ROWS, D])
                    self.sq = sb(c, "sq_" + kind, [P, 2, ROWS, D])
                    self.hn = sb(c, "hn_" + kind, [P, 2, ROWS, D])
                    self.HT = sb(c, "HT_" + kind, [P, RING, 512])
                    self.s1 = sb(c, "s1_" + kind, [P, RING, ROWS])
                    self.vs = sb(c, "vs_" + kind, [P, RING, ROWS])
                    self.lnv = sb(c, "lnv_" + kind, [P, RING, ROWS])
                    self.rstd = sb(c, "rstd_" + kind, [P, RING, ROWS])
                    self.loaded = sems(c, "xy_loaded_" + kind)
                    self.v1_ready = sem(c, "v1_ready_" + kind)
                    self.v2_ready = sem(c, "v2_ready_" + kind)
                    self.xf_ready = sem(c, "xf_ready_" + kind)
                    self.s1_ready = sem(c, "s1_ready_" + kind)
                    self.xc_ready = sem(c, "xc_ready_" + kind)
                    self.sq_ready = sem(c, "sq_ready_" + kind)
                    self.vs_ready = sem(c, "vs_ready_" + kind)
                    self.ln_ready = sem(c, "ln_ready_" + kind)
                    self.rstd_ready = sem(c, "rstd_ready_" + kind)
                    self.h_ready = sem(c, "h_ready_" + kind)
                    self.turned = sem(c, "turned_" + kind)
                    self.ht_ready = sem(c, "ht_ready_" + kind)

            n_, e_ = Rows("nodes"), Rows("edges")
            whh = sb(c, "whh", [P, 2, D])
            bh = sb(c, "bh", [P, ROWS, D])
            On = sb(c, "On", [P, RING, 512])
            wkq = sb(c, "wkq", [P, D])
            wv = sb(c, "wv", [P, D])
            wo = sb(c, "wo", [P, D])
            we = sb(c, "we", [P, D])
            wag = sb(c, "wag", [P, D])
            bq = sb(c, "bq", [D, 4])
            bt = sb(c, "bt", [D, 3])
            gidx = sb(c, "gidx4", [P, RING, 2 * GROUPS], I32)
            Gr = sb(c, "Gr", [P, RING, 2 * GROUPS, D])
            XD = sb(c, "XD", [P, RING, GROUPS, D])
            sm = sb(c, "sm", [D, RING, UNIT])
            ea = sb(c, "ea", [P, RING, UNIT])
            EX = sb(c, "EX", [D, 2, UNIT])
            SP = sb(c, "SP", [D, 2, UNIT])
            GT = sb(c, "GT", [D, 2, UNIT])
            MS = sb(c, "MS", [D, 2, UNIT])
            AG = sb(c, "AG", [P, RING, UNIT])
            Oe = sb(c, "Oe", [P, RING, GROUPS, D])
            Os = sb(c, "Os", [P, RING, GROUPS, D])
            sidx = sb(c, "sidx4", [P, RING, GROUPS], I32)
            fold2 = sb(c, "fold2", [1, 2, D])
            pT, pE, pV, pO = ps[0:2], ps[2:4], ps[4:6], ps[6:8]

            chain = sem(c, "chain4")
            var_ready = sem(c, "var_ready4")
            fold_rstd_ready = sem(c, "fold_rstd_ready")
            folded = sem(c, "folded4")
            spread = sem(c, "spread")
            w_zeroed = sem(c, "w_zeroed4")
            w_loaded = sem(c, "w_loaded4")
            bt_ready = sem(c, "bt_ready")
            proj_ready = sem(c, "proj_ready")
            on_ready = sem(c, "on_ready")
            rows_stored = sems(c, "rows_stored")
            gidx_loaded = sems(c, "gidx_loaded4")
            gathered = sems(c, "gathered4")
            spilled = sems(c, "spilled")
            side_loaded = sems(c, "side_loaded")
            xd_ready = sem(c, "xd_ready")
            edge_ready = sem(c, "edge_ready")
            ex_ready = sem(c, "ex_ready")
            softplus_ready = sem(c, "softplus_ready")
            gate_ready = sem(c, "gate_ready")
            ms_ready = sem(c, "ms_ready")
            ag_ready = sem(c, "ag_ready")
            out_ready = sem(c, "out_ready")
            oe_ready = sem(c, "oe_ready")
            o_stored = sems(c, "o_stored")
            os_loaded = sems(c, "os_loaded")
            scattered = sems(c, "scattered4")
            block = c.enter_context(nc.Block())
            DEPTH = 7
            ZEROED = 9
            links4 = [0]

            def times_scale(eng, t, b):
                await_slot(eng, b.loaded, t, 2, 32)
                if not t.first(2):
                    await_unit(eng, b.v2_ready, t, 3)
                eng.tensor_tensor(b.v1[:, :, :], b.Y[:, t.slot(2)],
                                  sc2b[:, :].unsqueeze(1).to_broadcast([P, ROWS, D]),
                                  ALU.mult).then_inc(b.v1_ready, 1)

            def plus_x(eng, t, b):
                await_unit(eng, b.v1_ready, t, 2)
                if not t.first(2):
                    await_unit(eng, b.xf_ready, t, 3)
                eng.tensor_tensor(b.v2[:, :, :], b.v1[:, :, :], b.X[:, t.slot(2)], ALU.add
                                  ).then_inc(b.v2_ready, 1)

            def plus_shift(eng, t, b):
                await_unit(eng, b.v2_ready, t, 2)
                await_free(eng, on_ready if b is n_ else xd_ready, t, 2)
                eng.tensor_tensor(b.xf[:, t.slot(2)], b.v2[:, :, :],
                                  sh2b[:, :].unsqueeze(1).to_broadcast([P, ROWS, D]),
                                  ALU.add).then_inc(b.xf_ready, 1)

            def row_sums(eng, t, b):
                await_unit(eng, b.xf_ready, t, 2)
                await_free(eng, b.xc_ready, t, 2)
                eng.tensor_reduce(b.s1[:, t.slot(2)], b.xf[:, t.slot(2)], AXX, ALU.add).then_inc(b.s1_ready, 1)

            def center(eng, t, b):
                s = t.slot(2)
                await_unit(eng, b.s1_ready, t, 2)
                await_free(eng, b.h_ready, t, 2)
                await_free(eng, b.sq_ready, t, 2)
                eng.scalar_tensor_tensor(
                    out=b.xc[:, s], in0=b.s1[:, s].unsqueeze(2).to_broadcast([P, ROWS, D]),
                    scalar=-1.0 / D, in1=b.xf[:, s], op0=ALU.mult, op1=ALU.add).then_inc(b.xc_ready, 1)

            def sum_squares(eng, t, b):
                await_unit(eng, b.sq_ready, t, 3)
                await_free(eng, b.ln_ready, t, 3)
                eng.tensor_reduce(b.vs[:, t.slot(3)], b.sq[:, t.slot(3, 2)], AXX, ALU.add).then_inc(b.vs_ready, 1)

            def scale(eng, t, b):
                await_unit(eng, b.rstd_ready, t, 4)
                await_unit(eng, b.xc_ready, t, 4)
                await_free(eng, b.turned, t, 4, 2)
                eng.scalar_tensor_tensor(
                    out=b.hn[:, t.slot(4, 2)], in0=b.xc[:, t.slot(4)], scalar=0.0,
                    in1=b.rstd[:, t.slot(4)].unsqueeze(2).to_broadcast([P, ROWS, D]),
                    op0=ALU.max, op1=ALU.mult).then_inc(b.h_ready, 1)

            def square(eng, t, b):
                await_unit(eng, b.xc_ready, t, 2)
                await_free(eng, b.vs_ready, t, 2, 2)
                eng.activation(b.sq[:, t.slot(2, 2)], b.xc[:, t.slot(2)], ACT.Square).then_inc(b.sq_ready, 1)

            def deviation(eng, t, b):
                await_unit(eng, b.vs_ready, t, 3)
                await_free(eng, b.rstd_ready, t, 3)
                eng.activation(b.lnv[:, t.slot(3)], b.vs[:, t.slot(3)], ACT.Ln,
                               bias=epsc[:, :], scale=1.0 / D).then_inc(b.ln_ready, 1)
                await_unit(eng, b.ln_ready, t, 3)
                await_free(eng, b.h_ready, t, 3)
                eng.activation(b.rstd[:, t.slot(3)], b.lnv[:, t.slot(3)], ACT.Exp,
                               scale=-0.5).then_inc(b.rstd_ready, 1)

            def turn_rows(eng, t, b):
                await_unit(eng, b.h_ready, t, 4)
                await_free(eng, b.ht_ready, t, 4, 2)
                for g in range(4):
                    mm = eng.transpose(pT[t.slot(4, 2)][:, g * P:g * P + P],
                                       b.hn[:, t.slot(4, 2), 2 * g:2 * g + 2].rearrange("p j d -> p (j d)"),
                                       ident[:, :])
                mm.then_inc(b.turned, 1)

            def take_turned(eng, t, b):
                await_unit(eng, b.turned, t, 4)
                await_free(eng, proj_ready if b is n_ else out_ready, t, 4)
                eng.activation(b.HT[:, t.slot(4)], pT[t.slot(4, 2)][:, :], ACT.Copy).then_inc(b.ht_ready, 1)

            @block.sync
            def _(eng):
                def gathers(t):
                    if t.has(0, EU):
                        await_slot_free(eng, gathered, t, 0, 16 * 2 * GROUPS)
                        eng.dma_start(gidx[:, t.slot()], a["gather_rows"][t.unit()]
                                      ).then_inc(gidx_loaded[t.slot()], 16)
                    if t.has(1, EU):
                        await_slot(eng, gathered, t, 1, 16 * 2 * GROUPS)
                        eng.dma_start(y_ends[t.unit(1)], Gr[:, t.slot(1)].rearrange("p k d -> p (k d)")
                                      ).then_inc(spilled[t.slot(1)], 16)

                def scatters(t):
                    if t.has(0, EU):
                        await_slot(eng, o_stored, t, 0)
                        await_slot_free(eng, scattered, t, 0, 16 * GROUPS)
                        eng.dma_start(Os[:, t.slot()].rearrange("p g d -> p (g d)"),
                                      o_rows[t.unit()]).then_inc(os_loaded[t.slot()], 16)
                        eng.dma_start(sidx[:, t.slot()], sidx_d[:, t.unit()]).then_inc(os_loaded[t.slot()], 16)

                pipeline(eng, EU, 1, gathers)
                pipeline(eng, EU, 0, scatters)

            @block.gpsimd
            def _(eng):
                last_row = eng.to_reg(N - 1)
                last_any = eng.to_reg(NP - 1)

                def gather(t):
                    if t.has(0, EU):
                        await_slot(eng, gidx_loaded, t, 0)
                        await_slot_free(eng, spilled, t, 0)
                        part_wait(eng, passed_pool)
                        for g in range(GROUPS):
                            for side in range(2):
                                k = side * GROUPS + g
                                eng.indirect_dma_start(
                                    out=Gr[:, t.slot(), 2 * g + side, :], out_offset=None, in_=y_rows,
                                    in_offset=bass.IndirectOffsetOnAxis(ap=gidx[:, t.slot(), k:k + 1], axis=0),
                                    bounds_check=last_any).then_inc(gathered[t.slot()], 16)

                def scatter(t):
                    if t.has(0, EU):
                        await_slot(eng, os_loaded, t, 0, 32)
                        part_wait(eng, passed_pool)
                        for g in range(GROUPS):
                            eng.indirect_dma_start(
                                out=out, out_offset=bass.IndirectOffsetOnAxis(
                                    ap=sidx[:, t.slot(), g:g + 1], axis=0),
                                in_=Os[:, t.slot(), g, :], in_offset=None, bounds_check=last_row,
                                oob_is_err=False).then_inc(scattered[t.slot()], 16)

                pipeline(eng, EU, 0, gather)
                for s in range(RING):
                    eng.wait_ge(rows_stored[s], 16 * len(range(s, NT, RING)))
                pipeline(eng, EU, 0, scatter)
                for s in range(RING):
                    eng.wait_ge(scattered[s], 16 * GROUPS * len(range(s, EU, RING)))

            @block.scalar
            def _(eng):
                W = a["L1_gnn_W_kernel"]
                wb = a["L1_gnn_W_bias"].rearrange("(o d) -> o d", o=1)
                wc = a["L1_gnn_W_bias"].rearrange("(k d o) -> k d o", k=4, o=1)
                eng.wait_ge(w_zeroed, 6)
                for dst, src in ((whh[0:D, 0], W[:, 0:D]), (whh[D:P, 1], W[:, 0:D]),
                                 (wkq[0:D, :], W[:, 2 * D:3 * D]), (wkq[D:P, :], W[:, D:2 * D]),
                                 (wv[0:D, :], W[:, 3 * D:4 * D]), (wo[D:P, :], W[:, 0:D]),
                                 (we[0:D, :], a["L1_gnn_We_kernel"]), (wag[0:D, :], a["ident"][0:D, 0:D]),
                                 (wag[D:D + 1, :], wb[:, 0:D])):
                    eng.dma_start(dst, src).then_inc(w_loaded, 16)
                for j in range(ROWS):
                    eng.dma_start(bh[0:1, j, :], wb[:, 0:D]).then_inc(w_loaded, 16)
                for i, src in enumerate((wc[1], wc[2], a["L1_gnn_We_bias"].rearrange("(d o) -> d o", o=1), wc[3])):
                    eng.dma_start(bq[:, i:i + 1], src).then_inc(w_loaded, 16)

                eng.wait_ge(var_ready, 1)
                eng.activation(st[:, 7], st[:, 3], ACT.Ln, bias=epsc[0:1, :]).then_inc(fold_rstd_ready, 1)
                eng.wait_ge(fold_rstd_ready, 1)
                eng.activation(st[:, 8], st[:, 7], ACT.Exp, scale=-0.5).then_inc(fold_rstd_ready, 1)

                def nodes(t):
                    if t.has(0, NT):
                        await_free(eng, n_.v2_ready, t, 0)
                        for dst, src in ((n_.X, a["x"]), (n_.Y, y_rows)):
                            eng.dma_start(dst[:, t.slot()].rearrange("p j d -> p (j d)"),
                                          tiles(src)[t.unit()]).then_inc(n_.loaded[t.slot()], 16)
                    if t.has(4, NT):
                        take_turned(eng, t, n_)
                    if t.has(3, NT):
                        deviation(eng, t, n_)
                    if t.has(2, NT):
                        square(eng, t, n_)
                    if t.has(7, NT):
                        await_unit(eng, on_ready, t, 7)
                        eng.dma_start(tiles(out)[t.unit(7)], On[:, t.slot(7)]).then_inc(rows_stored[t.slot(7)], 16)

                def edges(t):
                    if t.has(0, EU):
                        await_slot(eng, spilled, t, 0)
                        await_free(eng, e_.v2_ready, t, 0)
                        for dst, src in ((e_.X, x_ends), (e_.Y, y_ends)):
                            eng.dma_start(dst[:, t.slot()].rearrange("p j d -> p (j d)"),
                                          src[t.unit()]).then_inc(e_.loaded[t.slot()], 16)
                    if t.has(3, EU):
                        await_free(eng, ag_ready, t, 3)
                        await_free(eng, edge_ready, t, 3)
                        eng.dma_start(sm[:, t.slot(3)],
                                      same_d.rearrange("(u o e) -> u o e", o=1, e=UNIT)[t.unit(3)]
                                      .to_broadcast([D, UNIT])).then_inc(side_loaded[t.slot(3)], 16)
                        eng.dma_start(ea[0:D, t.slot(3)],
                                      a["edge_feats"].rearrange("f (u e) -> u f e", e=UNIT)[t.unit(3)]
                                      ).then_inc(side_loaded[t.slot(3)], 16)
                    if t.has(5, EU):
                        await_unit(eng, edge_ready, t, 5)
                        await_free(eng, softplus_ready, t, 5, 2)
                        eng.activation(EX[:, t.slot(5, 2)], pE[t.slot(5, 2)][0:D, :], ACT.Exp,
                                       bias=bt[:, 2:3], scale=-1.0).then_inc(ex_ready, 1)
                        await_unit(eng, ex_ready, t, 5)
                        await_free(eng, gate_ready, t, 5, 2)
                        eng.activation(SP[:, t.slot(5, 2)], EX[:, t.slot(5, 2)], ACT.Ln, bias=ones[0:D, 0:1]
                                       ).then_inc(softplus_ready, 1)
                        await_unit(eng, softplus_ready, t, 5)
                        await_free(eng, ms_ready, t, 5, 2)
                        eng.activation(GT[:, t.slot(5, 2)], SP[:, t.slot(5, 2)], ACT.Exp, scale=-1.0
                                       ).then_inc(gate_ready, 1)
                    if t.has(4, EU):
                        take_turned(eng, t, e_)
                    if t.has(3, EU):
                        deviation(eng, t, e_)
                    if t.has(4, EU):
                        await_unit(eng, e_.xf_ready, t, 4)
                        await_free(eng, oe_ready, t, 4)
                        eng.activation(XD[:, t.slot(4)],
                                       e_.xf[:, t.slot(4)].rearrange("p (g e) d -> p g e d", e=2)[:, :, 1],
                                       ACT.Copy).then_inc(xd_ready, 1)
                    if t.has(2, EU):
                        square(eng, t, e_)
                    if t.has(8, EU):
                        await_unit(eng, oe_ready, t, 8)
                        eng.dma_start(o_rows[t.unit(8)], Oe[:, t.slot(8)].rearrange("p g d -> p (g d)")
                                      ).then_inc(o_stored[t.slot(8)], 16)

                eng.wait_ge(bt_ready, 3)
                eng.wait_ge(w_zeroed, ZEROED)
                pipeline(eng, NT, DEPTH, nodes)
                pipeline(eng, EU, DEPTH + 1, edges)

            @block.vector
            def _(eng):
                for t_ in (whh, bh, wv, wo, we, wag):
                    eng.memset(t_[:], 0.0).then_inc(w_zeroed, 1)

                def link(ins):
                    links4[0] += 1
                    ins.then_inc(chain, 1)
                    eng.wait_ge(chain, links4[0])

                fold(link, eng, st, sum_y, sum_yy)
                eng.sem_inc(var_ready, 1)
                for t_ in (ea, AG):
                    eng.memset(t_[:], 0.0).then_inc(w_zeroed, 1)
                eng.wait_ge(fold_rstd_ready, 2)
                fold_shift(link, eng, st, st[:, 8], vec2[:, 0], vec2[:, 1], off2[:, :], fold2[:, 0], fold2[:, 1])
                eng.sem_inc(folded, 1)
                eng.wait_ge(spread, 1)
                link(eng.tensor_copy(sc2b[:, :], pO[0][:, 0:D]))
                link(eng.tensor_copy(sh2b[:, :], pO[0][:, D:2 * D]))
                eng.wait_ge(w_zeroed, ZEROED - 1)
                eng.memset(AG[D:D + 1, :, :], 1.0).then_inc(w_zeroed, 1)
                eng.wait_ge(w_loaded, 16 * (9 + ROWS + 4))
                eng.tensor_tensor(bt[:, 0:1], bq[:, 0:1], bq[:, 1:2], ALU.add).then_inc(bt_ready, 1)
                eng.wait_ge(bt_ready, 1)
                eng.tensor_tensor(bt[:, 1:2], bt[:, 0:1], bq[:, 2:3], ALU.add).then_inc(bt_ready, 1)
                eng.wait_ge(bt_ready, 2)
                eng.tensor_scalar(bt[:, 2:3], bt[:, 1:2], -1.0, None, ALU.mult).then_inc(bt_ready, 1)

                def nodes(t):
                    if t.has(2, NT):
                        times_scale(eng, t, n_)
                    if t.has(6, NT):
                        await_unit(eng, proj_ready, t, 6)
                        await_slot_free(eng, rows_stored, t, 6)
                        eng.tensor_tensor(On[:, t.slot(6)], n_.xf[:, t.slot(6)].rearrange("p j d -> p (j d)"),
                                          pO[t.slot(6, 2)][:, :], ALU.add).then_inc(on_ready, 1)
                    if t.has(2, NT):
                        plus_x(eng, t, n_)
                    if t.has(4, NT):
                        scale(eng, t, n_)
                    if t.has(2, NT):
                        plus_shift(eng, t, n_)
                    if t.has(3, NT):
                        sum_squares(eng, t, n_)
                    if t.has(2, NT):
                        row_sums(eng, t, n_)
                    if t.has(2, NT):
                        center(eng, t, n_)

                def edges(t):
                    if t.has(2, EU):
                        times_scale(eng, t, e_)
                    if t.has(7, EU):
                        await_unit(eng, out_ready, t, 7)
                        await_unit(eng, xd_ready, t, 7)
                        await_slot_free(eng, o_stored, t, 7)
                        eng.tensor_tensor(Oe[:, t.slot(7)], XD[:, t.slot(7)],
                                          pO[t.slot(7, 2)][:, 0:GROUPS * D].rearrange("p (g d) -> p g d", g=GROUPS),
                                          ALU.add).then_inc(oe_ready, 1)
                    if t.has(2, EU):
                        plus_x(eng, t, e_)
                    if t.has(4, EU):
                        scale(eng, t, e_)
                    if t.has(2, EU):
                        plus_shift(eng, t, e_)
                    if t.has(6, EU):
                        s2 = t.slot(6, 2)
                        await_unit(eng, gate_ready, t, 6)
                        await_free(eng, ag_ready, t, 6, 2)
                        eng.scalar_tensor_tensor(out=MS[:, s2], in0=pV[s2][0:D, :], scalar=bq[:, 3:4],
                                                 in1=GT[:, s2], op0=ALU.add, op1=ALU.mult).then_inc(ms_ready, 1)
                    if t.has(2, EU):
                        row_sums(eng, t, e_)
                    if t.has(6, EU):
                        s, s2 = t.slot(6), t.slot(6, 2)
                        await_unit(eng, ms_ready, t, 6)
                        await_slot(eng, side_loaded, t, 6, 32)
                        await_free(eng, out_ready, t, 6)
                        eng.tensor_tensor_scan(AG[0:D, s], sm[:, s], MS[:, s2],
                                               0.0 if t.first(6) else AG[0:D, (s - 1) % RING, UNIT - 1:UNIT],
                                               ALU.mult, ALU.add).then_inc(ag_ready, 1)
                    if t.has(2, EU):
                        center(eng, t, e_)
                    if t.has(3, EU):
                        sum_squares(eng, t, e_)

                pipeline(eng, NT, DEPTH, nodes)
                pipeline(eng, EU, DEPTH + 1, edges)

            @block.tensor
            def _(eng):
                eng.wait_ge(folded, 1)
                eng.matmul(pO[0][:, 0:2 * D], ones[0:1, :], fold2[:, :, :].rearrange("o k d -> o (k d)"),
                           start=True, stop=True).then_inc(spread, 1)
                eng.wait_ge(w_zeroed, ZEROED)
                eng.wait_ge(w_loaded, 16 * (9 + ROWS + 4))

                def nodes(t):
                    if t.has(5, NT):
                        await_unit(eng, n_.ht_ready, t, 5)
                        await_free(eng, on_ready, t, 5, 2)
                        o = pO[t.slot(5, 2)]
                        eng.matmul(o[:, :], ones[:, :], bh[:, :, :].rearrange("o j d -> o (j d)"),
                                   start=True, stop=False, skip_group_check=True)
                        for g in range(4):
                            mm = eng.matmul(o[:, g * P:g * P + P], n_.HT[:, t.slot(5), g * P:g * P + P],
                                            whh[:, :, :].rearrange("p q d -> p (q d)"),
                                            start=False, stop=True, skip_group_check=True)
                        mm.then_inc(proj_ready, 1)
                    if t.has(4, NT):
                        turn_rows(eng, t, n_)

                def edges(t):
                    if t.has(5, EU):
                        s, s2 = t.slot(5), t.slot(5, 2)
                        await_unit(eng, e_.ht_ready, t, 5)
                        await_slot(eng, side_loaded, t, 5, 32)
                        await_free(eng, ex_ready, t, 5, 2)
                        await_free(eng, ms_ready, t, 5, 2)
                        eng.matmul(pE[s2][0:D, :], we[:, :], ea[:, s], start=True, stop=False)
                        eng.matmul(pE[s2][0:D, :], wkq[:, :], e_.HT[:, s], start=False, stop=True)
                        eng.matmul(pV[s2][0:D, :], wv[:, :], e_.HT[:, s], start=True, stop=True
                                   ).then_inc(edge_ready, 1)
                    if t.has(4, EU):
                        turn_rows(eng, t, e_)
                    if t.has(6, EU):
                        await_unit(eng, ag_ready, t, 6)
                        await_free(eng, oe_ready, t, 6, 2)
                        o = pO[t.slot(6, 2)]
                        for g in range(GROUPS):
                            eng.matmul(o[:, g * D:g * D + D], e_.HT[:, t.slot(6), g * P:g * P + P], wo[:, :],
                                       start=True, stop=False)
                            mm = eng.matmul(o[:, g * D:g * D + D], AG[:, t.slot(6), g * P:g * P + P], wag[:, :],
                                            start=False, stop=True)
                        mm.then_inc(out_ready, 1)

                pipeline(eng, NT, DEPTH, nodes)
                eng.wait_ge(on_ready, NT)
                eng.wait_ge(n_.ht_ready, NT)
                pipeline(eng, EU, DEPTH + 1, edges)


WEIGHTS = ["L0_gnn_W_l", "L0_gnn_b_l", "L0_gnn_W_r", "L0_gnn_b_r", "L0_gnn_att", "L0_gnn_bias_gat",
           "L0_gnn_gamma1", "L0_gnn_beta1", "L0_gnn_W1", "L0_gnn_b1", "L0_gnn_W2", "L0_gnn_b2",
           "L0_gnn_gamma2", "L0_gnn_beta2", "L1_gnn_W_kernel", "L1_gnn_W_bias", "L1_gnn_We_kernel",
           "L1_gnn_We_bias"]


def kernel(**inputs):
    import concourse.bacc as bacc
    from concourse.bass_utils import run_bass_kernel_spmd

    N = inputs["x"].shape[0]
    E = inputs["src"].shape[0]
    NP = -(-N // TILE) * TILE
    EU = -(-E // UNIT)
    EU += -EU % 2 + 2 * (EU * UNIT == E)
    EP = EU * UNIT

    x = np.zeros((NP, D), np.float32)
    x[:N] = np.asarray(inputs["x"])
    src = np.zeros(EP, np.int32)
    src[:E] = np.asarray(inputs["src"])
    dst_rows = np.zeros(EP, np.int32)
    dst_rows[:E] = np.asarray(inputs["dst"])
    dst_flat = np.full(EP + 2, N, np.int32)
    dst_flat[0] = -1
    dst_flat[1:E + 1] = np.asarray(inputs["dst"])
    edge_feats = np.zeros((D, EP), np.float32)
    edge_feats[:, :E] = np.asarray(inputs["edge_attr_64"]).T

    def groups(v):
        return np.ascontiguousarray(v.reshape(EU * GROUPS, P).T)

    both = np.stack([src.reshape(EU, GROUPS, P), dst_rows.reshape(EU, GROUPS, P)], 1)
    sel = np.zeros((P, 2, P), np.float32)
    for h in range(HEADS):
        sel[h, h // 2, (h % 2) * D:(h % 2 + 1) * D] = 1.0
    pads = np.zeros((P, 1), np.float32)
    pads[P - (NP - N) // ROWS:] = -1.0
    arrays = {
        "x": x, "edge_feats": edge_feats,
        "gather_rows": np.ascontiguousarray(both.reshape(EU, 2 * GROUPS, P).transpose(0, 2, 1)),
        "dst_flat": dst_flat[1:-1].copy(), "prev_flat": dst_flat[:-2].copy(),
        "dst_groups": groups(dst_flat[1:-1]), "next_groups": groups(dst_flat[2:]),
        "ident": np.eye(P, dtype=np.float32), "ones": np.ones((P, P), np.float32), "sel": sel, "pads": pads,
    }
    for name in WEIGHTS:
        arrays[name] = np.ascontiguousarray(inputs[name])

    nc = bacc.Bacc("TRN2", target_bir_lowering=False, num_devices=1)
    feed, aps = {}, {"nodes": N}
    for name, v in arrays.items():
        feed["in_" + name] = v
        aps[name] = nc.dram_tensor("in_" + name, v.shape, mybir.dt.from_np(v.dtype), kind="ExternalInput").ap()
    out = nc.dram_tensor("out_rows", (NP, D), F32, kind="ExternalOutput").ap()
    build(nc, aps, out)
    r = run_bass_kernel_spmd(nc, [feed], core_ids=[0])
    return r.results[0]["out_rows"][:N]
```
